# Optimizing a Trainium2 kernel written in Bass

```python
import numpy as np
import jax
import jax.numpy as jnp

def _softmax(x, axis=-1):
    return jax.nn.softmax(x, axis=axis)

def _gelu(x):
    return jax.nn.gelu(x, approximate=True)

def _silu(x):
    return jax.nn.silu(x)

def _sigmoid(x):
    return jax.nn.sigmoid(x)

def _layernorm(x, axis=-1, eps=1e-05):
    m = jnp.mean(x, axis=axis, keepdims=True)
    v = jnp.var(x, axis=axis, keepdims=True)
    return (x - m) / jnp.sqrt(v + eps)

def _scatter_add(tgt, idx, src, axis=0):
    return tgt.at[idx].add(src)

def _segment_sum(src, seg, n):
    return jax.ops.segment_sum(src, seg, n)
kernel_name = 'mk_prb_d1_jaxref_r8_df732b'

def setup_inputs(seed: int=0):
    np.random.seed(seed)
    _w = jnp.asarray

    def _L0_attn_setup():
        import jax, jax.numpy as jnp
        import numpy as np
        NUM_HEADS = 16

        def _rope_tables(seq_len, head_dim, dtype):
            pos = jnp.arange(seq_len, dtype=jnp.float32)
            inv = jnp.power(10000.0, -2.0 * jnp.arange(head_dim // 2, dtype=jnp.float32) / head_dim)
            ang = pos[:, None] * inv[None, :]
            cos = jnp.repeat(jnp.cos(ang), 2, axis=-1).astype(dtype)
            sin = jnp.repeat(jnp.sin(ang), 2, axis=-1).astype(dtype)
            return (cos[None, None], sin[None, None])

        def _rotate_half_interleaved(x):
            x2 = jnp.stack([-x[..., 1::2], x[..., ::2]], axis=-1)
            return x2.reshape(x.shape)
        key = jax.random.key(seed)
        k0, k1, k2, k3 = jax.random.split(key, 4)
        B, N, C = (2, 256, 128)
        s = 1.0 / np.sqrt(C)
        return {'x': jax.random.normal(k0, (B, N, C), dtype=jnp.float32), 'Wq': jax.random.normal(k1, (C, C), dtype=jnp.float32) * s, 'Wk': jax.random.normal(k2, (C, C), dtype=jnp.float32) * s, 'Wv': jax.random.normal(k3, (C, C), dtype=jnp.float32) * s}
    _L0_attn_in = _L0_attn_setup()

    def _L0_ffn_setup():
        import jax, jax.numpy as jnp
        import numpy as np
        DIM = 128
        DEPTH = 6
        HEADS = 16
        DIM_HEAD = 64
        WINDOW = 32
        INNER = HEADS * DIM_HEAD
        DIM_INNER = int(DIM * 4 * 2 / 3)
        QK_SCALE = 8.0

        def shift_tokens(t):
            a, s = jnp.split(t, 2, -1)
            s = jnp.pad(s, ((0, 0), (1, 0), (0, 0)))[:, :-1]
            return jnp.concatenate([a, s], -1)

        def l2norm(t):
            return t / jnp.maximum(jnp.linalg.norm(t, axis=-1, keepdims=True), 1e-12)

        def rotate_half(x):
            x1, x2 = jnp.split(x, 2, -1)
            return jnp.concatenate([-x2, x1], -1)

        def rotary_tables(n):
            half = jnp.arange(0, DIM_HEAD, 2, dtype=jnp.float32)
            inv_freq = 1.0 / 10000.0 ** (half / DIM_HEAD)
            t = jnp.arange(n, dtype=jnp.float32)
            freqs = t[:, None] * inv_freq[None, :]
            freqs = jnp.concatenate([freqs, freqs], -1)
            base_scale = (half + 0.4 * DIM_HEAD) / (1.4 * DIM_HEAD)
            power = (t - n // 2) / (WINDOW // 2)
            scale = base_scale[None, :] ** power[:, None]
            scale = jnp.concatenate([scale, scale], -1)
            return (freqs, scale)

        def local_attention(q, k, v):
            b, h, n, d = q.shape
            w = WINDOW
            nw = n // w
            bq = q.reshape(b, h, nw, w, d)
            bk = k.reshape(b, h, nw, w, d)
            bv = v.reshape(b, h, nw, w, d)

            def look(t):
                p = jnp.pad(t, ((0, 0), (0, 0), (1, 0), (0, 0), (0, 0)))
                return jnp.concatenate([p[:, :, :nw], p[:, :, 1:]], axis=3)
            bk2, bv2 = (look(bk), look(bv))
            seq = jnp.arange(n).reshape(nw, w)
            seq_p = jnp.pad(seq, ((1, 0), (0, 0)), constant_values=-1)
            jt = jnp.concatenate([seq_p[:nw], seq_p[1:]], axis=1)
            it = seq[:, :, None]
            jb = jt[:, None, :]
            mask = (it < jb) | (it > jb + w) | (jb == -1)
            sim = jnp.einsum('bhwie,bhwje->bhwij', bq, bk2) * QK_SCALE
            sim = jnp.where(mask, -jnp.finfo(sim.dtype).max, sim)
            attn = jax.nn.softmax(sim, -1)
            out = jnp.einsum('bhwij,bhwje->bhwie', attn, bv2)
            return out.reshape(b, h, n, d)

        def attn_layer(x, Wqkv, qs, ksc, Wo):
            b, n, _ = x.shape
            qkv = x @ Wqkv
            q, k, v = jnp.split(qkv, 3, -1)
            sh = lambda t: t.reshape(b, n, HEADS, DIM_HEAD).transpose(0, 2, 1, 3)
            q, k, v = (sh(q), sh(k), sh(v))
            q = l2norm(q) * qs
            k = l2norm(k) * ksc
            freqs, scale = rotary_tables(n)
            cos, sin = (jnp.cos(freqs), jnp.sin(freqs))
            q = q * cos * scale + rotate_half(q) * sin * scale
            inv = 1.0 / scale
            k = k * cos * inv + rotate_half(k) * sin * inv
            out = local_attention(q, k, v)
            out = out.transpose(0, 2, 1, 3).reshape(b, n, INNER)
            return out @ Wo

        def ffn_layer(x, g, bln, W1, b1, W2, b2):
            mu = x.mean(-1, keepdims=True)
            var = ((x - mu) ** 2).mean(-1, keepdims=True)
            xn = (x - mu) / jnp.sqrt(var + 1e-05) * g + bln
            hg = xn @ W1 + b1
            a, gate = jnp.split(hg, 2, -1)
            return a * jax.nn.gelu(gate, approximate=False) @ W2 + b2
        key = jax.random.key(seed)
        ks = jax.random.split(key, 8)
        B, N = (2, 256)
        init = lambda k, shape: jax.random.normal(k, shape, jnp.float32) * 0.02
        return {'x': jax.random.normal(ks[0], (B, N, DIM), jnp.float32), 'Wqkv': init(ks[1], (DEPTH, DIM, 3 * INNER)), 'q_scale': jnp.ones((DEPTH, DIM_HEAD), jnp.float32), 'k_scale': jnp.ones((DEPTH, DIM_HEAD), jnp.float32), 'Wo': init(ks[2], (DEPTH, INNER, DIM)), 'ln_g': jnp.ones((DEPTH, DIM), jnp.float32), 'ln_b': jnp.zeros((DEPTH, DIM), jnp.float32), 'W1': init(ks[3], (DEPTH, DIM, 2 * DIM_INNER)), 'b1': jnp.zeros((DEPTH, 2 * DIM_INNER), jnp.float32), 'W2': init(ks[4], (DEPTH, DIM_INNER, DIM)), 'b2': jnp.zeros((DEPTH, DIM), jnp.float32)}
    _L0_ffn_in = _L0_ffn_setup()
    _d = {'L0_attn_x': _L0_attn_in['x'], 'L0_attn_Wq': _L0_attn_in['Wq'], 'L0_attn_Wk': _L0_attn_in['Wk'], 'L0_attn_Wv': _L0_attn_in['Wv'], 'L0_ffn_Wqkv': _L0_ffn_in['Wqkv'], 'L0_ffn_q_scale': _L0_ffn_in['q_scale'], 'L0_ffn_k_scale': _L0_ffn_in['k_scale'], 'L0_ffn_Wo': _L0_ffn_in['Wo'], 'L0_ffn_ln_g': _L0_ffn_in['ln_g'], 'L0_ffn_ln_b': _L0_ffn_in['ln_b'], 'L0_ffn_W1': _L0_ffn_in['W1'], 'L0_ffn_b1': _L0_ffn_in['b1'], 'L0_ffn_W2': _L0_ffn_in['W2'], 'L0_ffn_b2': _L0_ffn_in['b2']}
    _x0 = _d['L0_attn_x']
    _d['L0_attn_x'] = jax.random.normal(jax.random.fold_in(jax.random.key(seed), 1), (8, 512, 128), dtype=_x0.dtype)
    del _x0
    return _d

def reference(L0_attn_x, L0_attn_Wq, L0_attn_Wk, L0_attn_Wv, L0_ffn_Wqkv, L0_ffn_q_scale, L0_ffn_k_scale, L0_ffn_Wo, L0_ffn_ln_g, L0_ffn_ln_b, L0_ffn_W1, L0_ffn_b1, L0_ffn_W2, L0_ffn_b2):

    def _L0_attn_ref(x, Wq, Wk, Wv):
        import jax, jax.numpy as jnp
        import numpy as np
        NUM_HEADS = 16

        def _rope_tables(seq_len, head_dim, dtype):
            pos = jnp.arange(seq_len, dtype=jnp.float32)
            inv = jnp.power(10000.0, -2.0 * jnp.arange(head_dim // 2, dtype=jnp.float32) / head_dim)
            ang = pos[:, None] * inv[None, :]
            cos = jnp.repeat(jnp.cos(ang), 2, axis=-1).astype(dtype)
            sin = jnp.repeat(jnp.sin(ang), 2, axis=-1).astype(dtype)
            return (cos[None, None], sin[None, None])

        def _rotate_half_interleaved(x):
            x2 = jnp.stack([-x[..., 1::2], x[..., ::2]], axis=-1)
            return x2.reshape(x.shape)
        B, N, C = x.shape
        H = NUM_HEADS
        D = C // H
        scale = D ** (-0.5)

        def heads(y):
            return y.reshape(B, N, H, D).transpose(0, 2, 1, 3)
        q = heads(x @ Wq.T)
        k = heads(x @ Wk.T)
        v = heads(x @ Wv.T)
        cos, sin = _rope_tables(N, D, x.dtype)
        q = q * cos + _rotate_half_interleaved(q) * sin
        k = k * cos + _rotate_half_interleaved(k) * sin
        attn = jnp.einsum('bhnd,bhmd->bhnm', q, k) * scale
        attn = jax.nn.softmax(attn, axis=-1)
        out = jnp.einsum('bhnm,bhmd->bhnd', attn, v)
        return out.transpose(0, 2, 1, 3).reshape(B, N, C)

    def _L0_ffn_ref(x, Wqkv, q_scale, k_scale, Wo, ln_g, ln_b, W1, b1, W2, b2):
        import jax, jax.numpy as jnp
        import numpy as np
        DIM = 128
        DEPTH = 6
        HEADS = 16
        DIM_HEAD = 64
        WINDOW = 32
        INNER = HEADS * DIM_HEAD
        DIM_INNER = int(DIM * 4 * 2 / 3)
        QK_SCALE = 8.0

        def shift_tokens(t):
            a, s = jnp.split(t, 2, -1)
            s = jnp.pad(s, ((0, 0), (1, 0), (0, 0)))[:, :-1]
            return jnp.concatenate([a, s], -1)

        def l2norm(t):
            return t / jnp.maximum(jnp.linalg.norm(t, axis=-1, keepdims=True), 1e-12)

        def rotate_half(x):
            x1, x2 = jnp.split(x, 2, -1)
            return jnp.concatenate([-x2, x1], -1)

        def rotary_tables(n):
            half = jnp.arange(0, DIM_HEAD, 2, dtype=jnp.float32)
            inv_freq = 1.0 / 10000.0 ** (half / DIM_HEAD)
            t = jnp.arange(n, dtype=jnp.float32)
            freqs = t[:, None] * inv_freq[None, :]
            freqs = jnp.concatenate([freqs, freqs], -1)
            base_scale = (half + 0.4 * DIM_HEAD) / (1.4 * DIM_HEAD)
            power = (t - n // 2) / (WINDOW // 2)
            scale = base_scale[None, :] ** power[:, None]
            scale = jnp.concatenate([scale, scale], -1)
            return (freqs, scale)

        def local_attention(q, k, v):
            b, h, n, d = q.shape
            w = WINDOW
            nw = n // w
            bq = q.reshape(b, h, nw, w, d)
            bk = k.reshape(b, h, nw, w, d)
            bv = v.reshape(b, h, nw, w, d)

            def look(t):
                p = jnp.pad(t, ((0, 0), (0, 0), (1, 0), (0, 0), (0, 0)))
                return jnp.concatenate([p[:, :, :nw], p[:, :, 1:]], axis=3)
            bk2, bv2 = (look(bk), look(bv))
            seq = jnp.arange(n).reshape(nw, w)
            seq_p = jnp.pad(seq, ((1, 0), (0, 0)), constant_values=-1)
            jt = jnp.concatenate([seq_p[:nw], seq_p[1:]], axis=1)
            it = seq[:, :, None]
            jb = jt[:, None, :]
            mask = (it < jb) | (it > jb + w) | (jb == -1)
            sim = jnp.einsum('bhwie,bhwje->bhwij', bq, bk2) * QK_SCALE
            sim = jnp.where(mask, -jnp.finfo(sim.dtype).max, sim)
            attn = jax.nn.softmax(sim, -1)
            out = jnp.einsum('bhwij,bhwje->bhwie', attn, bv2)
            return out.reshape(b, h, n, d)

        def attn_layer(x, Wqkv, qs, ksc, Wo):
            b, n, _ = x.shape
            qkv = x @ Wqkv
            q, k, v = jnp.split(qkv, 3, -1)
            sh = lambda t: t.reshape(b, n, HEADS, DIM_HEAD).transpose(0, 2, 1, 3)
            q, k, v = (sh(q), sh(k), sh(v))
            q = l2norm(q) * qs
            k = l2norm(k) * ksc
            freqs, scale = rotary_tables(n)
            cos, sin = (jnp.cos(freqs), jnp.sin(freqs))
            q = q * cos * scale + rotate_half(q) * sin * scale
            inv = 1.0 / scale
            k = k * cos * inv + rotate_half(k) * sin * inv
            out = local_attention(q, k, v)
            out = out.transpose(0, 2, 1, 3).reshape(b, n, INNER)
            return out @ Wo

        def ffn_layer(x, g, bln, W1, b1, W2, b2):
            mu = x.mean(-1, keepdims=True)
            var = ((x - mu) ** 2).mean(-1, keepdims=True)
            xn = (x - mu) / jnp.sqrt(var + 1e-05) * g + bln
            hg = xn @ W1 + b1
            a, gate = jnp.split(hg, 2, -1)
            return a * jax.nn.gelu(gate, approximate=False) @ W2 + b2
        for i in range(DEPTH):
            x = attn_layer(shift_tokens(x), Wqkv[i], q_scale[i], k_scale[i], Wo[i]) + x
            x = ffn_layer(shift_tokens(x), ln_g[i], ln_b[i], W1[i], b1[i], W2[i], b2[i]) + x
        return x
    x = L0_attn_x
    xn = _layernorm(x, axis=-1)
    x = x + _L0_attn_ref(xn, L0_attn_Wq, L0_attn_Wk, L0_attn_Wv) + _L0_ffn_ref(xn, L0_ffn_Wqkv, L0_ffn_q_scale, L0_ffn_k_scale, L0_ffn_Wo, L0_ffn_ln_g, L0_ffn_ln_b, L0_ffn_W1, L0_ffn_b1, L0_ffn_W2, L0_ffn_b2)
    return x

_drawn_inputs = setup_inputs


def setup_inputs(seed=0):
    import zlib

    import numpy as np

    out = dict(_drawn_inputs(seed))
    spreads = {'L0_ffn_q_scale': (1.0, 0.6),
     'L0_ffn_k_scale': (1.0, 0.6),
     'L0_ffn_ln_g': (1.0, 0.6),
     'L0_ffn_ln_b': (0.0, 0.8),
     'L0_ffn_b1': (0.0, 0.8),
     'L0_ffn_b2': (0.0, 0.1)}
    factors = {'L0_ffn_W1': 3.643,
     'L0_ffn_W2': 3.578,
     'L0_attn_Wq': 4.352,
     'L0_attn_Wk': 4.252,
     'L0_attn_Wv': 3.698}
    for name, (base, spread) in spreads.items():
        noise = np.random.default_rng([zlib.crc32(name.encode()), seed]).standard_normal(out[name].shape)
        drawn = base * np.exp(spread * noise) if base else spread * noise
        out[name] = jnp.asarray(drawn.astype(out[name].dtype))
    for name, factor in factors.items():
        out[name] = (out[name] * factor).astype(out[name].dtype)
    return out
```

```python
from contextlib import ExitStack

import numpy as np
import concourse.bass as bass
from concourse import mybir

F32 = mybir.dt.float32
BF16 = mybir.dt.bfloat16
I32 = mybir.dt.int32
ALU = mybir.AluOpType
ACT = mybir.ActivationFunctionType
AX = mybir.AxisListType

P = 128
B, N, C = 8, 512, 128
T = N // P
EPS = 1e-5

GH, GD = 16, 8
GROUPS = 4
TERMS = ((0, 0), (0, 1), (1, 0), (1, 1), (0, 2), (2, 0))
KROWS = len(TERMS) * GD
AROWS = KROWS + 3

RSQRT_MAGIC = float(0x5F3759DF)


class Signal:

    def __init__(self, sem, per):
        self.sem, self.per = sem, per

    def at(self, batch, n):
        assert 1 <= n <= self.per
        return batch * self.per + self.per + n

    def before(self, batch):
        return batch * self.per + self.per


def rsqrt(eng, y, x, t, steps, batch, n):
    eng.tensor_scalar(y.bitcast(I32), x.bitcast(I32), -0.5, RSQRT_MAGIC, ALU.mult, ALU.add).then_inc(steps.sem, 1)
    for i in range(3):
        eng.wait_ge(steps.sem, steps.at(batch, n + 3 * i + 1))
        eng.tensor_tensor(t, y, y, ALU.mult).then_inc(steps.sem, 1)
        eng.wait_ge(steps.sem, steps.at(batch, n + 3 * i + 2))
        eng.scalar_tensor_tensor(t, t, -0.5, x, ALU.mult, ALU.mult).then_inc(steps.sem, 1)
        eng.wait_ge(steps.sem, steps.at(batch, n + 3 * i + 3))
        eng.scalar_tensor_tensor(y, t, 1.5, y, ALU.add, ALU.mult).then_inc(steps.sem, 1)
    eng.wait_ge(steps.sem, steps.at(batch, n + RSQRT_LINKS))


RSQRT_LINKS = 10
NORM_LINKS = RSQRT_LINKS + 2


def layernorm_part(nc, x_dram, ident_dram, X):
    with ExitStack() as ctx:
        sb = lambda n, s, d=F32: ctx.enter_context(nc.sbuf_tensor(n, s, d))
        sem = lambda n: ctx.enter_context(nc.semaphore(n))
        xt = sb("ln_xt", [P, B * T, C])
        xn = sb("ln_xn", [P, B * T, C])
        ident = sb("ln_ident", [P, P])
        stats = sb("ln_stats", [P, B * T, 6])
        mv = sb("ln_mv", [P, B * T, 2])
        var = sb("ln_var", [P, B * T])
        rstd = sb("ln_rstd", [P, B * T])
        tmp = sb("ln_tmp", [P, B * T])
        tr = ctx.enter_context(nc.psum_tensor("ln_tr", [P, 2, 512], F32))
        loaded, ident_loaded, normed, transposed, copied = (
            sem(n) for n in ("ln_loaded", "ln_ident_loaded", "ln_normed", "ln_transposed", "ln_copied"))
        chain = Signal(sem("ln_chain"), 3 + RSQRT_LINKS)
        block = ctx.enter_context(nc.Block())

        @block.sync
        def _(sp):
            sp.dma_start(xt[:], x_dram.rearrange("b (t p) c -> p (b t) c", p=P)).then_inc(loaded, 16)
            sp.dma_start(ident[:], ident_dram).then_inc(ident_loaded, 16)

        @block.vector
        def _(dve):
            dve.sem_inc(chain.sem, chain.per)
            dve.wait_ge(loaded, 16)
            for i in range(B * T):
                last = dve.bn_stats(stats[:, i, :], xt[:, i, :])
            last.then_inc(chain.sem, 1)
            dve.wait_ge(chain.sem, chain.at(0, 1))
            for i in range(B * T):
                last = dve.bn_aggr(mv[:, i, :], stats[:, i, :])
            last.then_inc(chain.sem, 1)
            dve.wait_ge(chain.sem, chain.at(0, 2))
            dve.tensor_scalar(var[:], mv[:, :, 1], EPS, None, ALU.add).then_inc(chain.sem, 1)
            dve.wait_ge(chain.sem, chain.at(0, 3))
            rsqrt(dve, rstd[:], var[:], tmp[:], chain, 0, 3)
            for i in range(B * T):
                dve.tensor_scalar(xn[:, i, :], xt[:, i, :], mv[:, i, 0:1], rstd[:, i:i + 1],
                                  ALU.subtract, ALU.mult).then_inc(normed, 1)

        @block.tensor
        def _(pe):
            pe.wait_ge(ident_loaded, 16)
            for b in range(B):
                pe.wait_ge(normed, T * (b + 1))
                if b >= 2:
                    pe.wait_ge(copied, b - 1)
                for t in range(T):
                    last = pe.transpose(tr[:, b % 2, t * P:(t + 1) * P], xn[:, b * T + t, :], ident[:])
                last.then_inc(transposed, 1)

        @block.scalar
        def _(act):
            for b in range(B):
                act.wait_ge(transposed, b + 1)
                act.copy(X[:, b, 1:1 + N], tr[:, b % 2, :]).then_inc(copied, 1)

        @block.gpsimd
        def _(pool):
            pool.memset(X[:, :, 0:1], 0.0)


def global_attention_part(nc, x_dram, w_dram, rope_dram, ident_dram, X, sum_dram, parts_dram, maxes_dram):
    with ExitStack() as ctx:
        sb = lambda n, s, d=F32: ctx.enter_context(nc.sbuf_tensor(n, s, d))
        ps = lambda n, s, d=F32: ctx.enter_context(nc.psum_tensor(n, s, d))
        sem = lambda n: ctx.enter_context(nc.semaphore(n))
        signal = lambda n, per: Signal(sem(n), per)
        w = sb("ga_w", [P, 5, P])
        rope = sb("ga_rope", [P, 2, N])
        ident = sb("ga_ident", [P, P])
        xa = sb("ga_xa", [P, N])
        prod = sb("ga_prod", [P, 4, N])
        full = sb("ga_full", [P, 2, 3, N])
        parts = sb("ga_parts", [P, 2, 3, N], BF16)
        qs = sb("ga_qs", [P, GH // 2, N], BF16)
        ks = sb("ga_ks", [P, GH // 2, N], BF16)
        va = sb("ga_va", [P, T, GH, 32])
        mx = sb("ga_mx", [P, GH * T])
        mfull = sb("ga_mfull", [GH * T, 3, P])
        mparts = sb("ga_mparts", [GH * T, 3, P], BF16)
        pt = sb("ga_pt", [P, 8, 2, N])
        os = sb("ga_os", [P, 2, N])
        rec = sb("ga_rec", [P, T, 4])
        xraw = sb("ga_xraw", [P, T, C])
        y = sb("ga_y", [P, T, C])
        s_ps = ps("ga_s_ps", [P, 4, N])
        pv_ps = ps("ga_pv_ps", [P, 2, N])
        aux_ps = ps("ga_aux_ps", [P, 2, N])
        consts, init = sem("ga_consts"), sem("ga_init")
        xa_ready = signal("ga_xa_ready", 1)
        proj_ready = signal("ga_proj_ready", 5)
        prod_done = signal("ga_prod_done", 4)
        v_ready = signal("ga_v_ready", 1)
        full_ready = signal("ga_full_ready", 6)
        parts_ready = signal("ga_parts_ready", 6)
        parts_out = [signal(f"ga_{n}_parts_out", 16) for n in "qk"]
        stacked = signal("ga_stacked", 16 * 4 * len(TERMS))
        s_ready = signal("ga_s_ready", 64)
        max_done = signal("ga_max_done", 64)
        mt_ready = signal("ga_mt_ready", 1)
        m_steps = signal("ga_m_steps", 6)
        m_out = signal("ga_m_out", 16)
        m_rows = signal("ga_m_rows", 16 * GH)
        st_ready = signal("ga_st_ready", 32)
        exp_done = signal("ga_exp_done", 32)
        pv_done = signal("ga_pv_done", 16)
        os_ready = signal("ga_os_ready", 4)
        ot_ready = signal("ga_ot_ready", 4)
        out_steps = signal("ga_out_steps", 8)
        x_loaded = signal("ga_x_loaded", 16)
        y_ready = signal("ga_y_ready", 1)
        stored = signal("ga_stored", 16)
        block = ctx.enter_context(nc.Block())

        def place(h):
            return 64 * (h % 2), h // 2

        @block.sync
        def _(sp):
            for s in (*parts_out, stacked, m_out, m_rows, x_loaded, stored):
                sp.sem_inc(s.sem, s.per)
            sp.dma_start(w[:], w_dram).then_inc(consts, 16)
            sp.dma_start(rope[:], rope_dram).then_inc(consts, 16)
            sp.dma_start(ident[:], ident_dram).then_inc(consts, 16)
            sp.wait_ge(init, 3)
            with sp.Fori(0, B) as b:
                sp.wait_ge(y_ready.sem, y_ready.before(b))
                sp.dma_start(xraw[:], x_dram[bass.ds(b, 1)].rearrange("o (t p) c -> p (o t) c", p=P)).then_inc(x_loaded.sem, 16)
                for a in range(2):
                    sp.wait_ge(parts_ready.sem, parts_ready.at(b, 3 * a + 3))
                    sp.dma_start(parts_dram[bass.ds(b, 1), :, a].rearrange("o p c n -> (o p) c n"), parts[:, a]).then_inc(parts_out[a].sem, 16)
                sp.wait_ge(st_ready.sem, st_ready.before(b))
                for a, dst in ((0, qs), (1, ks)):
                    sp.wait_ge(parts_out[a].sem, parts_out[a].at(b, 16))
                    for z in range(2):
                        for j, term in enumerate(TERMS):
                            at = 64 * z + GD * j
                            src = parts_dram[bass.ds(b, 1), :, a, term[a]].rearrange("o (hp z d) n -> z d (o hp) n", z=2, d=GD)
                            sp.dma_start(dst[at:at + GD], src[z]).then_inc(stacked.sem, 16)
                sp.wait_ge(m_steps.sem, m_steps.at(b, 6))
                sp.dma_start(maxes_dram[bass.ds(b, 1)].rearrange("o r c n -> (o r) c n"), mparts[:]).then_inc(m_out.sem, 16)
                sp.wait_ge(m_out.sem, m_out.at(b, 16))
                for z in range(2):
                    src = maxes_dram[bass.ds(b, 1)].rearrange("o (hp z t) c n -> z c (o hp) t n", z=2, t=T)[z]
                    for hp in range(GH // 2):
                        sp.dma_start(qs[64 * z + KROWS:64 * z + AROWS, hp].rearrange("c (t n) -> c t n", t=T), src[:, hp]).then_inc(m_rows.sem, 16)
                sp.wait_ge(y_ready.sem, y_ready.at(b, 1))
                sp.dma_start(sum_dram[bass.ds(b, 1)].rearrange("o (t p) c -> p (o t) c", p=P), y[:]).then_inc(stored.sem, 16)
            sp.wait_ge(stored.sem, stored.before(B))

        @block.tensor
        def _(pe):
            for s in (proj_ready, s_ready, mt_ready, st_ready, pv_done, ot_ready):
                pe.sem_inc(s.sem, s.per)
            pe.wait_ge(consts, 48)
            with pe.Fori(0, B) as b:
                pe.wait_ge(xa_ready.sem, xa_ready.at(b, 1))
                pe.wait_ge(out_steps.sem, out_steps.before(b))
                for i in range(4):
                    if i >= 2:
                        pe.wait_ge(prod_done.sem, prod_done.at(b, i - 1))
                    pe.matmul(aux_ps[:, i % 2, :], w[:, i, :], xa[:], start=True, stop=True).then_inc(proj_ready.sem, 1)
                pe.wait_ge(prod_done.sem, prod_done.at(b, 3))
                for t in range(T):
                    last = pe.matmul(aux_ps[:, 0, t * P:(t + 1) * P], xa[:, t * P:(t + 1) * P], w[:, 4, :], start=True, stop=True)
                last.then_inc(proj_ready.sem, 1)
                pe.wait_ge(stacked.sem, stacked.at(b, stacked.per))
                for i in range(GH * T):
                    z, hp = place(i // T)
                    t = i % T
                    if i < 4:
                        pe.wait_ge(exp_done.sem, exp_done.before(b))
                    else:
                        pe.wait_ge(max_done.sem, max_done.at(b, i - 3))
                    pe.matmul(s_ps[:, i % 4, :], qs[z:z + KROWS, hp, t * P:(t + 1) * P], ks[z:z + KROWS, hp, :],
                              start=True, stop=True).then_inc(s_ready.sem, 1)
                pe.wait_ge(max_done.sem, max_done.at(b, 64))
                pe.wait_ge(prod_done.sem, prod_done.at(b, 4))
                pe.matmul(aux_ps[0:GH * T, 1, 0:P], mx[:], ident[:], start=True, stop=True).then_inc(mt_ready.sem, 1)

                def pv(q):
                    j, kt = q // T, q % T
                    pe.wait_ge(exp_done.sem, exp_done.at(b, 2 * q + 2))
                    if kt == 0 and j >= 2:
                        pe.wait_ge(os_ready.sem, os_ready.at(b, j - 1))
                    for c in range(4):
                        last = pe.matmul(pv_ps[32 * c:32 * c + 32, j % 2, :], va[:, kt, 4 * j + c, :],
                                         pt[:, (2 * q + c // 2) % 8, c % 2, :], start=(kt == 0), stop=(kt == T - 1),
                                         skip_group_check=True)
                    last.then_inc(pv_done.sem, 1)

                def out(j):
                    pe.wait_ge(os_ready.sem, os_ready.at(b, j + 1))
                    if j >= 2:
                        pe.wait_ge(out_steps.sem, out_steps.at(b, 2 * j - 2))
                    elif j == 1:
                        pe.wait_ge(m_steps.sem, m_steps.at(b, 1))
                    else:
                        pe.wait_ge(v_ready.sem, v_ready.at(b, 1))
                    for t in range(T):
                        last = pe.transpose(aux_ps[:, j % 2, t * P:(t + 1) * P], os[:, j % 2, t * P:(t + 1) * P], ident[:])
                    last.then_inc(ot_ready.sem, 1)

                pe.wait_ge(m_rows.sem, m_rows.at(b, m_rows.per))
                pe.wait_ge(v_ready.sem, v_ready.at(b, 1))
                for q in range(16):
                    j, kt = q // T, q % T
                    for c in range(4):
                        z, hp = place(4 * j + c)
                        pair = 2 * q + c // 2
                        if c % 2 == 0 and pair >= 2:
                            pe.wait_ge(exp_done.sem, exp_done.at(b, pair - 1))
                        mm = pe.matmul(s_ps[:, 2 * (pair % 2) + c % 2, :], ks[z:z + AROWS, hp, kt * P:(kt + 1) * P],
                                       qs[z:z + AROWS, hp, :], start=True, stop=True)
                        if c % 2 == 1:
                            mm.then_inc(st_ready.sem, 1)
                    if q >= 1:
                        pv(q - 1)
                    if q >= 5 and q % 4 == 1:
                        out(q // 4 - 1)
                pv(15)
                out(3)

        @block.vector
        def _(dve):
            for s in (prod_done, max_done, m_steps, out_steps):
                dve.sem_inc(s.sem, s.per)
            dve.memset(va[:], 0.0).then_inc(init, 1)
            dve.memset(ks[:], 1.0).then_inc(init, 1)
            dve.wait_ge(init, 2)
            dve.memset(va[:, :, :, GD:GD + 1], 1.0).then_inc(init, 1)
            dve.wait_ge(consts, 48)
            with dve.Fori(0, B) as b:
                dve.wait_ge(full_ready.sem, full_ready.before(b))
                for i in range(4):
                    dve.wait_ge(proj_ready.sem, proj_ready.at(b, i + 1))
                    dve.tensor_tensor(prod[:, i, :], aux_ps[:, i % 2, :], rope[:, i % 2, :], ALU.mult).then_inc(prod_done.sem, 1)
                dve.wait_ge(mt_ready.sem, mt_ready.before(b))
                for i in range(GH * T):
                    dve.wait_ge(s_ready.sem, s_ready.at(b, i + 1))
                    dve.tensor_reduce(mx[:, i:i + 1], s_ps[:, i % 4, :], AX.X, ALU.max).then_inc(max_done.sem, 1)
                dve.wait_ge(mt_ready.sem, mt_ready.at(b, 1))
                dve.wait_ge(m_out.sem, m_out.before(b))
                dve.tensor_scalar(mfull[:, 0, :], aux_ps[0:GH * T, 1, 0:P], -1.0, None, ALU.mult).then_inc(m_steps.sem, 1)
                for c in range(3):
                    dve.wait_ge(m_steps.sem, m_steps.at(b, 2 * c + 1))
                    dve.tensor_copy(mparts[:, c, :], mfull[:, c, :]).then_inc(m_steps.sem, 1)
                    if c < 2:
                        dve.wait_ge(m_steps.sem, m_steps.at(b, 2 * c + 2))
                        dve.tensor_tensor(mfull[:, c + 1, :], mfull[:, c, :], mparts[:, c, :], ALU.subtract).then_inc(m_steps.sem, 1)
                dve.wait_ge(y_ready.sem, y_ready.before(b))
                dve.wait_ge(stored.sem, stored.before(b))
                for j in range(GROUPS):
                    dve.wait_ge(ot_ready.sem, ot_ready.at(b, j + 1))
                    o = aux_ps[:, j % 2, :].rearrange("p (t c e) -> p t c e", t=T, c=4)
                    if j:
                        dve.wait_ge(out_steps.sem, out_steps.at(b, 2 * j))
                    dve.reciprocal(rec[:], o[:, :, :, GD]).then_inc(out_steps.sem, 1)
                    dve.wait_ge(out_steps.sem, out_steps.at(b, 2 * j + 1))
                    dve.tensor_tensor(y[:, :, 32 * j:32 * j + 32].rearrange("p t (c d) -> p t c d", d=GD), o[:, :, :, 0:GD],
                                      rec[:].unsqueeze(3).to_broadcast([P, T, 4, GD]), ALU.mult).then_inc(out_steps.sem, 1)

        @block.scalar
        def _(act):
            for s in (parts_ready, v_ready, exp_done, os_ready):
                act.sem_inc(s.sem, s.per)
            act.wait_ge(init, 3)
            with act.Fori(0, B) as b:
                act.wait_ge(pv_done.sem, pv_done.before(b))
                for a in range(2):
                    act.wait_ge(parts_out[a].sem, parts_out[a].before(b))
                    for c in range(3):
                        act.wait_ge(full_ready.sem, full_ready.at(b, 3 * a + c + 1))
                        act.copy(parts[:, a, c, :], full[:, a, c, :]).then_inc(parts_ready.sem, 1)
                act.wait_ge(proj_ready.sem, proj_ready.at(b, 5))
                act.copy(va[:, :, :, 0:GD], aux_ps[:, 0, :].rearrange("p (t h d) -> p t h d", t=T, h=GH)).then_inc(v_ready.sem, 1)

                def take(j):
                    act.wait_ge(pv_done.sem, pv_done.at(b, 4 * j + 4))
                    if j >= 2:
                        act.wait_ge(ot_ready.sem, ot_ready.at(b, j - 1))
                    else:
                        act.wait_ge(ot_ready.sem, ot_ready.before(b))
                    act.copy(os[:, j % 2, :], pv_ps[:, j % 2, :]).then_inc(os_ready.sem, 1)

                for pair in range(32):
                    act.wait_ge(st_ready.sem, st_ready.at(b, pair + 1))
                    if pair >= 8 and pair % 2 == 0:
                        act.wait_ge(pv_done.sem, pv_done.at(b, pair // 2 - 3))
                    act.activation(pt[:, pair % 8], s_ps[:, 2 * (pair % 2):2 * (pair % 2) + 2, :], ACT.Exp,
                                   scale=float(GD) ** -0.5).then_inc(exp_done.sem, 1)
                    if pair >= 10 and pair % 8 == 2:
                        take(pair // 8 - 1)
                take(3)

        @block.gpsimd
        def _(pool):
            for s in (xa_ready, full_ready, y_ready):
                pool.sem_inc(s.sem, s.per)
            with pool.Fori(0, B) as b:
                pool.wait_ge(proj_ready.sem, proj_ready.before(b))
                pool.tensor_copy(xa[:], X[:, bass.ds(b, 1), 1:1 + N].rearrange("p o n -> p (o n)")).then_inc(xa_ready.sem, 1)
                pool.wait_ge(parts_ready.sem, parts_ready.before(b))
                for a in range(2):
                    pool.wait_ge(prod_done.sem, prod_done.at(b, 2 * a + 2))
                    pool.tensor_tensor(full[:, a, 0, :], prod[:, 2 * a, :], prod[:, 2 * a + 1, :], ALU.add).then_inc(full_ready.sem, 1)
                    for c in range(2):
                        pool.wait_ge(full_ready.sem, full_ready.at(b, 3 * a + c + 1))
                        pool.wait_ge(parts_ready.sem, parts_ready.at(b, 3 * a + c + 1))
                        pool.tensor_tensor(full[:, a, c + 1, :], full[:, a, c, :], parts[:, a, c, :], ALU.subtract).then_inc(full_ready.sem, 1)
                pool.wait_ge(x_loaded.sem, x_loaded.at(b, 16))
                pool.wait_ge(out_steps.sem, out_steps.at(b, 8))
                pool.tensor_tensor(y[:], y[:], xraw[:], ALU.add).then_inc(y_ready.sem, 1)


LAYERS = 6
LH, LD = 16, 64
HALF = LD // 2
INNER = LH * LD
WIN = 32
NW = N // WIN
SPAN = 2 * WIN
HID = C * 4 * 2 // 3
CHUNKS = tuple((k, min(P, HID - k)) for k in range(0, HID, P))
NC_ = len(CHUNKS)
MASKED = -1e30
TINY = 1e-24
V_QS, V_KS, V_G, V_BLN, V_B1, V_B2, NVEC = 0, 2, 4, 5, 6, 6 + 2 * NC_, 7 + 2 * NC_
UNITS = 4


def layers_part(nc, X, d):
    with ExitStack() as ctx:
        sb = lambda n, s, dt=F32: ctx.enter_context(nc.sbuf_tensor(n, s, dt))
        ps = lambda n, s, dt=F32: ctx.enter_context(nc.psum_tensor(n, s, dt))
        sem = lambda n: ctx.enter_context(nc.semaphore("ly_" + n))
        signal = lambda n, per: Signal(sem(n), per)

        wqk = sb("ly_wqk", [P, UNITS, 4, P])
        mvo = sb("ly_mvo", [P, LH, P])
        w1 = sb("ly_w1", [P, 2 * HID])
        w2 = sb("ly_w2", [P, NC_, P])
        vec = sb("ly_vec", [P, NVEC])
        b1 = sb("ly_b1", [P, 2 * NC_])
        rot = sb("ly_rot", [P, 8, N])
        ident = sb("ly_ident", [P, P])
        ones = sb("ly_ones", [P, P])
        heads = sb("ly_heads", [P, 32])
        pick = sb("ly_pick", [P, 8])
        mask = sb("ly_mask", [P, 2, 512], BF16)
        identb = sb("ly_identb", [P, P], BF16)
        xs = sb("ly_xs", [P, WIN + N])
        prod = sb("ly_prod", [P, 8, N])
        sq = sb("ly_sq", [P, 4, N])
        nsum = sb("ly_nsum", [P, N])
        ss = sb("ly_ss", [P, T, 8])
        rn = sb("ly_rn", [P, 2, T, 8])
        rt = sb("ly_rt", [P, T, 8])
        rnx = sb("ly_rnx", [P, T, 4, HALF])
        qr = sb("ly_qr", [P, 2, 2, N])
        kr = sb("ly_kr", [P, 2, N])
        kn = sb("ly_kn", [P, 2, N])
        kbd = sb("ly_kbd", [P, 2, 4, WIN + N])
        sx = sb("ly_sx", [P, 2, T, 4, SPAN])
        smax = sb("ly_smax", [P, 2, T, 4])
        rsum = sb("ly_rsum", [P, 2, T, 4])
        pt = sb("ly_pt", [P, NW, LH // 2, WIN])
        xtok = sb("ly_xtok", [P, NW, P])
        u = sb("ly_u", [P, LH, NW, WIN])
        xf = sb("ly_xf", [P, N])
        xc = sb("ly_xc", [P, N])
        csq = sb("ly_csq", [P, N])
        rstd = sb("ly_rstd", [P, 3, T])
        gate = sb("ly_gate", [P, 2, N])
        hid = sb("ly_hid", [P, NC_, N])
        uf = u[:].rearrange("p h w q -> p (h w q)")
        wv_raw = uf[:, 0:1024].rearrange("p (h c) -> p h c", c=P)
        wo_raw = uf[:, 1024:2048].rearrange("p (h c) -> p h c", c=P)
        rot_raw = uf[:, 2048:4096].rearrange("p (i n) -> p i n", n=N)
        w1_raw = uf[:, 4096:4096 + 2 * HID]

        pj_ps = ps("ly_pj_ps", [P, 2, N])
        nr_ps = ps("ly_nr_ps", [P, N])
        st_ps = ps("ly_st_ps", [P, 2, 512])
        ta_ps = ps("ly_ta_ps", [P, 2, 512])
        to_ps = ps("ly_to_ps", [P, 512])

        consts, init = sem("consts"), sem("init")
        loaded = signal("loaded", 16 * 7)
        mvo_ready = signal("mvo_ready", 4 + 1)
        mvo_copied = signal("mvo_copied", 4 + 1)
        w1_scaled = signal("w1_scaled", 1)
        rot_ready = signal("rot_ready", 8)
        layer_done = signal("layer_done", 1)
        xs_ready = signal("xs_ready", 2)
        proj_ready = signal("proj_ready", 16)
        sq_done = signal("sq_done", 16)
        prod_done = signal("prod_done", 32)
        rot_done = signal("rot_done", 16)
        ns_ready = signal("ns_ready", 4)
        ns_copied = signal("ns_copied", 4)
        ss_ready = signal("ss_ready", 4)
        rn_steps = signal("rn_steps", 4 * NORM_LINKS)
        r_ready = signal("r_ready", 4)
        kn_done = signal("kn_done", 8)
        kbd_loaded = signal("kbd_loaded", 16 * 8 * 4)
        s_ready = signal("s_ready", 4)
        s_scaled = signal("s_scaled", 4)
        s_max = signal("s_max", 4)
        s_less = signal("s_less", 4)
        p_exp = signal("p_exp", 4)
        p_sum = signal("p_sum", 8)
        p_ready = signal("p_ready", 4)
        t_ready = signal("t_ready", 4)
        pt_done = signal("pt_done", 4)
        xtr_ready = signal("xtr_ready", 2)
        xtok_done = signal("xtok_done", 2)
        u_ready = signal("u_ready", 16)
        u_copied = signal("u_copied", 16)
        att_ready = signal("att_ready", 1)
        x1_done = signal("x1_done", 1)
        xf_done = signal("xf_done", 2)
        mean_ready = signal("mean_ready", 1)
        xc_done = signal("xc_done", 1)
        csq_done = signal("csq_done", 1)
        var_ready = signal("var_ready", 1)
        var_steps = signal("var_steps", 1 + RSQRT_LINKS)
        rb_ready = signal("rb_ready", 1)
        xn_done = signal("xn_done", 1)
        h_ready = signal("h_ready", 2 * NC_)
        gate_done = signal("gate_done", NC_)
        hid_done = signal("hid_done", NC_)
        ffn_ready = signal("ffn_ready", 1)
        x2_done = signal("x2_done", 1)
        block = ctx.enter_context(nc.Block())

        def layers(eng, layer_work, body):
            with eng.Fori(0, LAYERS) as layer:
                layer_work(layer)
                body(layer, 0, None)
                with eng.Fori(1, B) as b:
                    body(layer, b, b - 1)
                body(layer, None, B - 1)

        def unit_tables(i):
            k, upper = i // 2, i % 2
            return ((4 * k + 1, 4 * k + 1), (4 * k + 2, 4 * k + 2)) if upper else ((4 * k, 4 * k), (4 * k + 3, 4 * k + 3))

        @block.sync
        def _(sp):
            for s in (loaded, kbd_loaded):
                sp.sem_inc(s.sem, s.per)
            for dst, src in ((ident, d["ident"]), (ones, d["ones"]), (heads, d["heads"]), (pick, d["pick"]),
                             (mask, d["mask"]), (identb, d["identb"])):
                sp.dma_start(dst[:], src).then_inc(consts, 16)
            sp.wait_ge(init, 3)

            def layer_work(layer):
                sp.wait_ge(layer_done.sem, layer_done.before(layer))
                one = lambda a: a[bass.ds(layer, 1)]
                for dst, src in ((wqk[:], one(d["wqk"]).rearrange("o p u i c -> p (o u) i c")),
                                 (wv_raw, one(d["wv"]).rearrange("o p h c -> p (o h) c")),
                                 (wo_raw, one(d["wo"]).rearrange("o p h c -> p (o h) c")),
                                 (w1_raw, one(d["w1"]).rearrange("o p c -> p (o c)")),
                                 (w2[:], one(d["w2"]).rearrange("o p h c -> p (o h) c")),
                                 (vec[:], one(d["vec"]).rearrange("o p c -> p (o c)")),
                                 (rot_raw, d["rot"])):
                    sp.dma_start(dst, src).then_inc(loaded.sem, 16)

            def body(layer, core, tail):
                if core is None:
                    return
                n = layer * B + core
                for g in range(UNITS):
                    sp.wait_ge(kn_done.sem, kn_done.at(n, 2 * g + 2))
                    for half in range(2):
                        for h in range(4):
                            sp.dma_start(kbd[32 * h:32 * h + 32, half, h, WIN:], kn[32 * h:32 * h + 32, half, :]).then_inc(kbd_loaded.sem, 16)

            layers(sp, layer_work, body)

        @block.tensor
        def _(pe):
            for s in (mvo_ready, proj_ready, ns_ready, ss_ready, r_ready, s_ready, t_ready, xtr_ready, u_ready,
                      att_ready, mean_ready, var_ready, rb_ready, h_ready, ffn_ready):
                pe.sem_inc(s.sem, s.per)
            pe.wait_ge(consts, 16 * 6)

            def layer_work(layer):
                pe.wait_ge(loaded.sem, loaded.at(layer, loaded.per))
                for j in range(2):
                    if j:
                        pe.wait_ge(mvo_copied.sem, mvo_copied.at(layer, 2))
                    for i in range(4):
                        for z in range(2):
                            rows = slice(64 * z, 64 * z + 64)
                            mm = pe.matmul(st_ps[:, z, i * P:(i + 1) * P], wv_raw[rows, 4 * j + i, :], wo_raw[rows, 4 * j + i, :],
                                           start=True, stop=True)
                            if i == 3:
                                mm.then_inc(mvo_ready.sem, 1)
                for side in range(2):
                    for c, (k, m) in enumerate(CHUNKS):
                        last = pe.matmul(to_ps[0:m, side * NC_ + c:side * NC_ + c + 1], w1_raw[:, side * HID + k:side * HID + k + m],
                                         vec[:, V_BLN:V_BLN + 1], start=True, stop=True)
                last.then_inc(mvo_ready.sem, 1)
                pe.wait_ge(mvo_copied.sem, mvo_copied.at(layer, 5))
                pe.wait_ge(w1_scaled.sem, w1_scaled.at(layer, 1))

            def body(layer, core, tail):
                n = None if core is None else layer * B + core
                m = None if tail is None else layer * B + tail

                def project(g):
                    if g == 0:
                        pe.wait_ge(xs_ready.sem, xs_ready.at(n, 2))
                    for i in range(4):
                        k = 4 * g + i - 2
                        if k < 0:
                            pe.wait_ge(prod_done.sem, prod_done.before(n))
                            pe.wait_ge(sq_done.sem, sq_done.before(n))
                        else:
                            pe.wait_ge(prod_done.sem, prod_done.at(n, 2 * k + 2))
                            pe.wait_ge(sq_done.sem, sq_done.at(n, k + 1))
                        pe.matmul(pj_ps[:, i % 2, :], wqk[:, g, i, :], xs[:, WIN:], start=True, stop=True).then_inc(proj_ready.sem, 1)

                def square_sums(g):
                    if g == 0:
                        pe.wait_ge(kn_done.sem, kn_done.before(n))
                    else:
                        pe.wait_ge(kn_done.sem, kn_done.at(n, 2 * g))
                    pe.wait_ge(sq_done.sem, sq_done.at(n, 4 * g + 4))
                    for i in range(4):
                        last = pe.matmul(nr_ps[32 * i:32 * i + 32, :], heads[:], sq[:, i, :], start=True, stop=True)
                    last.then_inc(ns_ready.sem, 1)

                def sums_by_token(g):
                    pe.wait_ge(ns_copied.sem, ns_copied.at(n, g + 1))
                    for t in range(T):
                        last = pe.matmul(nr_ps[:, 8 * t:8 * t + 8], nsum[:, t * P:(t + 1) * P], pick[:], start=True, stop=True)
                    last.then_inc(ss_ready.sem, 1)

                def spread_norms(g):
                    pe.wait_ge(rn_steps.sem, rn_steps.at(n, (g + 1) * NORM_LINKS))
                    for t in range(T):
                        last = pe.transpose(nr_ps[:, t * P:(t + 1) * P],
                                            rnx[:, t].rearrange("p h d -> p (h d)"), ident[:])
                    last.then_inc(r_ready.sem, 1)

                def scores(g):
                    if g == 0:
                        pe.wait_ge(pt_done.sem, pt_done.before(n))
                    elif g == 1:
                        pe.wait_ge(s_scaled.sem, s_scaled.at(n, 1))
                    elif g == 2:
                        pe.wait_ge(pt_done.sem, pt_done.at(n, 1))
                    else:
                        pe.wait_ge(pt_done.sem, pt_done.at(n, 2))
                    pe.wait_ge(kbd_loaded.sem, kbd_loaded.at(n, 16 * 8 * (g + 1)))
                    pe.wait_ge(rot_done.sem, rot_done.at(n, 4 * g + 2))
                    for bank in range(2):
                        pe.matmul(st_ps[:, bank, :], identb[:], mask[:, bank, :], start=True, stop=False, skip_group_check=True)
                    for w in range(NW):
                        t, c = w // 4, w % 4
                        for half in range(2):
                            last = pe.matmul(st_ps[32 * c:32 * c + 32, t // 2, 256 * (t % 2):256 * (t % 2) + 256],
                                             qr[:, g % 2, half, WIN * w:WIN * w + WIN], kbd[:, half, :, WIN * w:WIN * w + SPAN],
                                             start=False, stop=(half == 1), skip_group_check=True)
                    last.then_inc(s_ready.sem, 1)

                def token_transposes(r):
                    if r == 0:
                        pe.wait_ge(s_scaled.sem, s_scaled.at(n, 2))
                    else:
                        pe.wait_ge(xtok_done.sem, xtok_done.at(n, 1))
                    for i in range(8):
                        w = 8 * r + i
                        for z in range(2):
                            last = pe.matmul(st_ps[64 * z:64 * z + SPAN, i // 4, (i % 4) * P:(i % 4 + 1) * P],
                                             xs[:, WIN * w:WIN * w + SPAN], ident[:], start=True, stop=True)
                    last.then_inc(xtr_ready.sem, 1)

                def prob_transposes(g):
                    if g == 0:
                        pe.wait_ge(xtok_done.sem, xtok_done.at(n, 2))
                    else:
                        pe.wait_ge(s_scaled.sem, s_scaled.at(n, g + 2 if g < 3 else 4))
                    if g == 3:
                        pe.wait_ge(pt_done.sem, pt_done.at(n, 3))
                    pe.wait_ge(p_ready.sem, p_ready.at(n, g + 1))
                    for hp in range(2):
                        for t in range(T):
                            last = pe.transpose(st_ps[:, hp, t * P:(t + 1) * P], sx[:, g % 2, t, 2 * hp:2 * hp + 2, :], ident[:])
                    last.then_inc(t_ready.sem, 1)

                def attend(r):
                    if r == 0:
                        pe.wait_ge(pt_done.sem, pt_done.at(m, 4))
                        pe.wait_ge(xtok_done.sem, xtok_done.at(m, 2))
                        pe.wait_ge(hid_done.sem, hid_done.before(m))
                        pe.wait_ge(gate_done.sem, gate_done.before(m))
                    for k in (2 * r, 2 * r + 1):
                        for w in (2 * k, 2 * k + 1):
                            for z in range(2):
                                if k and w % 2 == 0:
                                    pe.wait_ge(u_copied.sem, u_copied.at(m, 2 * k - 1 + z))
                                mm = pe.matmul(ta_ps[:, z, 256 * (w % 2):256 * (w % 2) + 256], xtok[64 * z:64 * z + 64, w, :],
                                               pt[64 * z:64 * z + 64, w, :, :], start=True, stop=True)
                                if w % 2:
                                    mm.then_inc(u_ready.sem, 1)

                def combine(r):
                    if r == 0:
                        pe.wait_ge(u_copied.sem, u_copied.at(m, 16))
                        pe.wait_ge(x2_done.sem, x2_done.before(m))
                    for h in range(4 * r, 4 * r + 4):
                        last = pe.matmul(to_ps[:], mvo[:, h, :], u[:, h, :, :], start=(h == 0), stop=(h == LH - 1),
                                         skip_group_check=True)
                    if r == 3:
                        last.then_inc(att_ready.sem, 1)

                def mean():
                    pe.wait_ge(xf_done.sem, xf_done.at(m, 2))
                    pe.matmul(ta_ps[:, 0, :], ones[:], xf[:], start=True, stop=True).then_inc(mean_ready.sem, 1)

                def variance():
                    pe.wait_ge(csq_done.sem, csq_done.at(m, 1))
                    for t in range(T):
                        last = pe.matmul(ta_ps[:, 1, t:t + 1], csq[:, t * P:(t + 1) * P], ones[:, 0:1], start=True, stop=True)
                    last.then_inc(var_ready.sem, 1)

                def spread_rstd():
                    pe.wait_ge(var_steps.sem, var_steps.at(m, 1 + RSQRT_LINKS))
                    for t in range(T):
                        last = pe.transpose(ta_ps[:, 0, t * P:(t + 1) * P], rstd[:, 1, t:t + 1].to_broadcast([P, P]), ident[:])
                    last.then_inc(rb_ready.sem, 1)

                def hidden(c):
                    k, w = CHUNKS[c]
                    if c == 0:
                        pe.wait_ge(xn_done.sem, xn_done.at(m, 1))
                    for side in (1, 0):
                        if c:
                            used = gate_done if side else hid_done
                            pe.wait_ge(used.sem, used.at(m, c))
                        pe.matmul(ta_ps[0:w, side, :], w1[:, side * HID + k:side * HID + k + w], csq[:],
                                  start=True, stop=True).then_inc(h_ready.sem, 1)

                def down(c):
                    k, w = CHUNKS[c]
                    pe.wait_ge(hid_done.sem, hid_done.at(m, c + 1))
                    if c == 0:
                        pe.wait_ge(x1_done.sem, x1_done.at(m, 1))
                    last = pe.matmul(to_ps[:], w2[0:w, c, :], hid[0:w, c, :], start=(c == 0), stop=(c == NC_ - 1), skip_group_check=True)
                    if c == NC_ - 1:
                        last.then_inc(ffn_ready.sem, 1)

                C_, T_ = core is not None, tail is not None
                if C_: project(0); square_sums(0)
                if T_: attend(0); attend(1)
                if C_: sums_by_token(0)
                if T_: attend(2)
                if C_: spread_norms(0)
                if T_: attend(3)
                if C_: project(1); square_sums(1)
                if C_: scores(0)
                if T_: combine(0)
                if C_: sums_by_token(1)
                if T_: combine(1)
                if C_: spread_norms(1); project(2); square_sums(2); scores(1)
                if T_: combine(2)
                if C_: sums_by_token(2)
                if T_: combine(3)
                if C_: token_transposes(0); spread_norms(2); token_transposes(1)
                if C_: project(3); prob_transposes(0)
                if T_: mean()
                if C_: square_sums(3); scores(2)
                if T_: variance()
                if C_: sums_by_token(3); prob_transposes(1)
                if T_: spread_rstd()
                if C_: spread_norms(3)
                if T_: hidden(0); hidden(1); down(0)
                if C_: scores(3)
                if T_: hidden(2); down(1); down(2)
                if C_: prob_transposes(2); prob_transposes(3)

            layers(pe, layer_work, body)

        @block.vector
        def _(dve):
            for s in (w1_scaled, layer_done, prod_done, rn_steps, kn_done, s_scaled, s_max, p_sum,
                      x1_done, xc_done, var_steps, xn_done, hid_done, x2_done, mvo_copied, rot_ready):
                dve.sem_inc(s.sem, s.per)
            dve.memset(kbd[:], 0.0).then_inc(init, 1)
            dve.memset(xs[:], 0.0).then_inc(init, 1)
            dve.memset(b1[:], 0.0).then_inc(init, 1)
            dve.wait_ge(init, 3)

            def layer_work(layer):
                dve.wait_ge(loaded.sem, loaded.at(layer, loaded.per))
                for i in range(8):
                    table, upper = 2 * (i // 4) + i % 2, (0, 1, 1, 0)[i % 4]
                    gain = vec[:, (V_KS if i >= 4 else V_QS) + upper:(V_KS if i >= 4 else V_QS) + upper + 1]
                    dve.tensor_scalar(rot[:, i, :], rot_raw[:, table, :], gain, None, ALU.mult).then_inc(rot_ready.sem, 1)
                dve.tensor_scalar(w1[:], w1_raw, vec[:, V_G:V_G + 1], None, ALU.mult).then_inc(w1_scaled.sem, 1)
                for j in range(4):
                    dve.wait_ge(mvo_ready.sem, mvo_ready.at(layer, j + 1))
                    dve.tensor_copy(mvo[:].rearrange("p (j h z) c -> p j z h c", j=2, z=2)[:, j // 2, j % 2],
                                    st_ps[:, j % 2, :].rearrange("p (h c) -> p h c", c=P)).then_inc(mvo_copied.sem, 1)
                dve.wait_ge(mvo_ready.sem, mvo_ready.at(layer, 5))
                for side in range(2):
                    for c, (k, w) in enumerate(CHUNKS):
                        i = side * NC_ + c
                        last = dve.tensor_tensor(b1[0:w, i:i + 1], to_ps[0:w, i:i + 1], vec[0:w, V_B1 + i:V_B1 + i + 1], ALU.add)
                last.then_inc(mvo_copied.sem, 1)
                dve.wait_ge(rot_ready.sem, rot_ready.at(layer, 8))

            def body(layer, core, tail):
                n = None if core is None else layer * B + core
                m = None if tail is None else layer * B + tail

                def products(g):
                    for i in range(4):
                        dve.wait_ge(sq_done.sem, sq_done.at(n, 4 * g + i + 1))
                        for table, k in unit_tables(i):
                            if g == 0:
                                dve.wait_ge(rot_done.sem, rot_done.before(n))
                            elif i % 2 == 0:
                                dve.wait_ge(rot_done.sem, rot_done.at(n, 4 * (g - 1) + i + 2))
                            dve.tensor_tensor(prod[:, k, :], pj_ps[:, i % 2, :], rot[:, table, :], ALU.mult).then_inc(prod_done.sem, 1)

                def norms(g):
                    dve.wait_ge(ss_ready.sem, ss_ready.at(n, g + 1))
                    if g >= 2:
                        dve.wait_ge(r_ready.sem, r_ready.at(n, g - 1))
                    done = g * NORM_LINKS
                    dve.tensor_scalar(ss[:], nr_ps[:, 0:8 * T].rearrange("p (t k) -> p t k", k=8), TINY, None, ALU.max).then_inc(rn_steps.sem, 1)
                    dve.wait_ge(rn_steps.sem, rn_steps.at(n, done + 1))
                    rsqrt(dve, rn[:, g % 2], ss[:], rt[:], rn_steps, n, done + 1)
                    dve.tensor_copy(rnx[:], rn[:, g % 2, :, 4:8].unsqueeze(3).to_broadcast([P, T, 4, HALF])).then_inc(rn_steps.sem, 1)

                def scale_keys(g):
                    dve.wait_ge(r_ready.sem, r_ready.at(n, g + 1))
                    if g == 0:
                        dve.wait_ge(kbd_loaded.sem, kbd_loaded.before(n))
                    else:
                        dve.wait_ge(kbd_loaded.sem, kbd_loaded.at(n, 16 * 8 * g))
                    dve.wait_ge(rot_done.sem, rot_done.at(n, 4 * g + 4))
                    for half in range(2):
                        dve.tensor_tensor(kn[:, half, :], kr[:, half, :], nr_ps[:], ALU.mult).then_inc(kn_done.sem, 1)

                def scale_scores(g):
                    dve.wait_ge(s_ready.sem, s_ready.at(n, g + 1))
                    if g >= 2:
                        dve.wait_ge(t_ready.sem, t_ready.at(n, g - 1))
                    else:
                        dve.wait_ge(t_ready.sem, t_ready.before(n))
                    dve.tensor_tensor(sx[:, g % 2], st_ps[:].rearrange("p b (t h k) -> p (b t) h k", h=4, k=SPAN),
                                      rn[:, g % 2, :, 0:4].unsqueeze(3).to_broadcast([P, T, 4, SPAN]), ALU.mult).then_inc(s_scaled.sem, 1)
                    dve.wait_ge(s_scaled.sem, s_scaled.at(n, g + 1))
                    if g >= 2:
                        dve.wait_ge(s_less.sem, s_less.at(n, g - 1))
                    else:
                        dve.wait_ge(s_less.sem, s_less.before(n))
                    dve.tensor_reduce(smax[:, g % 2], sx[:, g % 2], AX.X, ALU.max).then_inc(s_max.sem, 1)

                def prob_sums(g):
                    dve.wait_ge(p_exp.sem, p_exp.at(n, g + 1))
                    if g >= 2:
                        dve.wait_ge(p_ready.sem, p_ready.at(n, g - 1))
                    else:
                        dve.wait_ge(p_ready.sem, p_ready.before(n))
                    dve.tensor_reduce(rsum[:, g % 2], sx[:, g % 2], AX.X, ALU.add).then_inc(p_sum.sem, 1)
                    dve.wait_ge(p_sum.sem, p_sum.at(n, 2 * g + 1))
                    dve.reciprocal(rsum[:, g % 2], rsum[:, g % 2]).then_inc(p_sum.sem, 1)

                xb = None if tail is None else X[:, bass.ds(tail, 1), 1:1 + N].rearrange("p o n -> p (o n)")

                def attention_sum():
                    dve.wait_ge(att_ready.sem, att_ready.at(m, 1))
                    dve.tensor_tensor(xb, to_ps[:], xb, ALU.add).then_inc(x1_done.sem, 1)

                def centre():
                    dve.wait_ge(mean_ready.sem, mean_ready.at(m, 1))
                    dve.tensor_tensor(xc[:], xf[:], ta_ps[:, 0, :], ALU.subtract).then_inc(xc_done.sem, 1)

                def deviation():
                    dve.wait_ge(var_ready.sem, var_ready.at(m, 1))
                    dve.tensor_scalar(rstd[:, 0, :], ta_ps[:, 1, 0:T], EPS, None, ALU.add).then_inc(var_steps.sem, 1)
                    dve.wait_ge(var_steps.sem, var_steps.at(m, 1))
                    rsqrt(dve, rstd[:, 1, :], rstd[:, 0, :], rstd[:, 2, :], var_steps, m, 1)

                def normalise():
                    dve.wait_ge(rb_ready.sem, rb_ready.at(m, 1))
                    dve.tensor_tensor(csq[:], xc[:], ta_ps[:, 0, :], ALU.mult).then_inc(xn_done.sem, 1)

                def gated(c):
                    k, w = CHUNKS[c]
                    dve.wait_ge(h_ready.sem, h_ready.at(m, 2 * c + 2))
                    dve.wait_ge(gate_done.sem, gate_done.at(m, c + 1))
                    if c == 0:
                        dve.wait_ge(ffn_ready.sem, ffn_ready.before(m))
                    dve.scalar_tensor_tensor(hid[0:w, c, :], ta_ps[0:w, 0, :], b1[0:w, c:c + 1], gate[0:w, c % 2, :],
                                             ALU.add, ALU.mult).then_inc(hid_done.sem, 1)

                def ffn_sum():
                    dve.wait_ge(ffn_ready.sem, ffn_ready.at(m, 1))
                    dve.wait_ge(xf_done.sem, xf_done.at(m, 2))
                    dve.scalar_tensor_tensor(xb, to_ps[:], vec[:, V_B2:V_B2 + 1], xb, ALU.add, ALU.add).then_inc(x2_done.sem, 1)

                C_, T_ = core is not None, tail is not None
                if C_: products(0); norms(0); scale_keys(0); products(1); norms(1); scale_keys(1); scale_scores(0); products(2); prob_sums(0)
                if C_: norms(2); scale_scores(1); scale_keys(2)
                if T_: attention_sum()
                if C_: products(3); prob_sums(1)
                if T_: centre()
                if C_: scale_scores(2)
                if T_: deviation()
                if C_: norms(3)
                if T_: normalise()
                if C_: scale_keys(3); prob_sums(2)
                if T_: gated(0); gated(1)
                if C_: scale_scores(3)
                if T_: gated(2); ffn_sum()
                if C_: prob_sums(3)
                if core is None:
                    dve.wait_ge(x2_done.sem, x2_done.at(m, 1))
                    dve.sem_inc(layer_done.sem, 1)

            layers(dve, layer_work, body)

        @block.scalar
        def _(act):
            for s in (xs_ready, xf_done, sq_done, ns_copied, p_exp, pt_done, xtok_done, u_copied, csq_done, gate_done):
                act.sem_inc(s.sem, s.per)
            act.wait_ge(init, 3)
            shifts = lambda dst, b: ((dst[0:64], X[0:64, bass.ds(b, 1), 1:1 + N]), (dst[64:128], X[64:128, bass.ds(b, 1), 0:N]))

            def layer_work(layer):
                act.wait_ge(mvo_copied.sem, mvo_copied.at(layer, 5))

            def body(layer, core, tail):
                n = None if core is None else layer * B + core
                m = None if tail is None else layer * B + tail

                def tokens():
                    act.wait_ge(proj_ready.sem, proj_ready.before(n))
                    act.wait_ge(xtr_ready.sem, xtr_ready.before(n))
                    for dst, src in shifts(xs[:, WIN:], core):
                        act.copy(dst, src.rearrange("p o n -> p (o n)")).then_inc(xs_ready.sem, 1)

                def ffn_tokens():
                    act.wait_ge(x1_done.sem, x1_done.at(m, 1))
                    act.wait_ge(xc_done.sem, xc_done.before(m))
                    for dst, src in shifts(xf[:], tail):
                        act.copy(dst, src.rearrange("p o n -> p (o n)")).then_inc(xf_done.sem, 1)

                def squares(g):
                    for i in range(4):
                        act.wait_ge(proj_ready.sem, proj_ready.at(n, 4 * g + i + 1))
                        if i == 0:
                            if g == 0:
                                act.wait_ge(ns_ready.sem, ns_ready.before(n))
                            else:
                                act.wait_ge(ns_ready.sem, ns_ready.at(n, g))
                        act.activation(sq[:, i, :], pj_ps[:, i % 2, :], ACT.Square).then_inc(sq_done.sem, 1)

                def copy_sums(g):
                    act.wait_ge(ns_ready.sem, ns_ready.at(n, g + 1))
                    if g == 0:
                        act.wait_ge(ss_ready.sem, ss_ready.before(n))
                    else:
                        act.wait_ge(ss_ready.sem, ss_ready.at(n, g))
                    act.copy(nsum[:], nr_ps[:]).then_inc(ns_copied.sem, 1)

                def exponentials(g):
                    act.wait_ge(s_less.sem, s_less.at(n, g + 1))
                    act.activation(sx[:, g % 2], sx[:, g % 2], ACT.Exp).then_inc(p_exp.sem, 1)

                def copy_probs(g):
                    act.wait_ge(t_ready.sem, t_ready.at(n, g + 1))
                    if g == 0:
                        act.wait_ge(u_ready.sem, u_ready.before(n))
                    act.copy(pt[:, :, 2 * g:2 * g + 2, :].rearrange("p w h q -> p h w q"),
                             st_ps[:].rearrange("p h (w q) -> p h w q", q=WIN)).then_inc(pt_done.sem, 1)

                def copy_tokens(r):
                    act.wait_ge(xtr_ready.sem, xtr_ready.at(n, r + 1))
                    if r == 0:
                        act.wait_ge(u_ready.sem, u_ready.before(n))
                    act.copy(xtok[:, 8 * r:8 * r + 8, :].rearrange("p w c -> p (w c)"), st_ps[:].rearrange("p b x -> p (b x)")).then_inc(xtok_done.sem, 1)

                def take_u(r):
                    if r == 0:
                        act.wait_ge(att_ready.sem, att_ready.before(m))
                    for k in (2 * r, 2 * r + 1):
                        for z in range(2):
                            act.wait_ge(u_ready.sem, u_ready.at(m, 2 * k + z + 1))
                            act.copy(u[:].rearrange("p (h z) w q -> p z w h q", z=2)[:, z, 2 * k:2 * k + 2],
                                     ta_ps[:, z, :].rearrange("p (w h q) -> p w h q", w=2, q=WIN)).then_inc(u_copied.sem, 1)

                def centred_squares():
                    act.wait_ge(xc_done.sem, xc_done.at(m, 1))
                    act.activation(csq[:], xc[:], ACT.Square).then_inc(csq_done.sem, 1)

                def gates(c):
                    k, w = CHUNKS[c]
                    act.wait_ge(h_ready.sem, h_ready.at(m, 2 * c + 1))
                    if c == 0:
                        act.wait_ge(hid_done.sem, hid_done.before(m))
                    if c >= 2:
                        act.wait_ge(hid_done.sem, hid_done.at(m, c - 1))
                    act.activation(gate[0:w, c % 2, :], ta_ps[0:w, 1, :], ACT.Gelu, bias=b1[0:w, NC_ + c:NC_ + c + 1]).then_inc(gate_done.sem, 1)

                C_, T_ = core is not None, tail is not None
                if C_: tokens(); squares(0); copy_sums(0)
                if T_: take_u(0); take_u(1); take_u(2); take_u(3)
                if C_: squares(1); copy_sums(1); squares(2); exponentials(0); copy_sums(2)
                if C_: copy_tokens(0); copy_tokens(1)
                if T_: ffn_tokens()
                if C_: squares(3); exponentials(1); copy_probs(0)
                if T_: centred_squares()
                if C_: copy_sums(3); copy_probs(1); exponentials(2)
                if T_: gates(0); gates(1); gates(2)
                if C_: exponentials(3); copy_probs(2); copy_probs(3)

            layers(act, layer_work, body)

        @block.gpsimd
        def _(pool):
            for s in (rot_done, s_less, p_ready):
                pool.sem_inc(s.sem, s.per)

            def body(layer, core, tail):
                n = None if core is None else layer * B + core
                m = None if tail is None else layer * B + tail

                def rotate(g):
                    for i in range(4):
                        pool.wait_ge(prod_done.sem, prod_done.at(n, 8 * g + 4 * (i // 2) + 4))
                        if i < 2:
                            if g < 2:
                                pool.wait_ge(s_ready.sem, s_ready.before(n))
                            else:
                                pool.wait_ge(s_ready.sem, s_ready.at(n, g - 1))
                            dst = qr[:, g % 2, i, :]
                        else:
                            if g == 0:
                                pool.wait_ge(kn_done.sem, kn_done.before(n))
                            else:
                                pool.wait_ge(kn_done.sem, kn_done.at(n, 2 * g))
                            dst = kr[:, i % 2, :]
                        k = 2 * i
                        pool.tensor_tensor(dst, prod[:, k, :], prod[:, k + 1, :], ALU.add if i % 2 else ALU.subtract).then_inc(rot_done.sem, 1)

                def less_max(g):
                    pool.wait_ge(s_max.sem, s_max.at(n, g + 1))
                    pool.tensor_tensor(sx[:, g % 2], sx[:, g % 2], smax[:, g % 2].unsqueeze(3).to_broadcast([P, T, 4, SPAN]),
                                       ALU.subtract).then_inc(s_less.sem, 1)

                def normal_probs(g):
                    pool.wait_ge(p_sum.sem, p_sum.at(n, 2 * g + 2))
                    pool.tensor_tensor(sx[:, g % 2], sx[:, g % 2], rsum[:, g % 2].unsqueeze(3).to_broadcast([P, T, 4, SPAN]),
                                       ALU.mult).then_inc(p_ready.sem, 1)

                C_, T_ = core is not None, tail is not None
                if C_: rotate(0); rotate(1); less_max(0); rotate(2); normal_probs(0); less_max(1); rotate(3); normal_probs(1); less_max(2); normal_probs(2); less_max(3); normal_probs(3)

            def layer_work(layer):
                pool.wait_ge(layer_done.sem, layer_done.before(layer))

            layers(pool, layer_work, body)


def final_part(nc, sum_dram, ident_dram, X, out_dram):
    with ExitStack() as ctx:
        sb = lambda n, s: ctx.enter_context(nc.sbuf_tensor(n, s, F32))
        sem = lambda n: ctx.enter_context(nc.semaphore(n))
        part = sb("fi_part", [P, B * T, C])
        res = sb("fi_res", [P, B * T, C])
        ident = sb("fi_ident", [P, P])
        xt = sb("fi_xt", [P, 2, N])
        tr = ctx.enter_context(nc.psum_tensor("fi_tr", [P, 2, 512], F32))
        loaded, copied, transposed, added, stored = (sem("fi_" + n) for n in ("loaded", "copied", "transposed", "added", "stored"))
        block = ctx.enter_context(nc.Block())
        rows = lambda a: a.rearrange("b (t p) c -> p (b t) c", p=P)

        @block.sync
        def _(sp):
            sp.dma_start(part[:], rows(sum_dram)).then_inc(loaded, 16)
            sp.dma_start(ident[:], ident_dram).then_inc(loaded, 16)
            for b in range(B):
                sp.wait_ge(added, b + 1)
                sp.dma_start(rows(out_dram)[:, b * T:(b + 1) * T], res[:, b * T:(b + 1) * T]).then_inc(stored, 16)
            sp.wait_ge(stored, 16 * B)

        @block.scalar
        def _(act):
            for b in range(B):
                if b >= 2:
                    act.wait_ge(transposed, b - 1)
                act.copy(xt[:, b % 2, :], X[:, b, 1:1 + N]).then_inc(copied, 1)

        @block.tensor
        def _(pe):
            pe.wait_ge(loaded, 32)
            for b in range(B):
                pe.wait_ge(copied, b + 1)
                if b >= 2:
                    pe.wait_ge(added, b - 1)
                for t in range(T):
                    last = pe.transpose(tr[:, b % 2, t * P:(t + 1) * P], xt[:, b % 2, t * P:(t + 1) * P], ident[:])
                last.then_inc(transposed, 1)

        @block.vector
        def _(dve):
            dve.wait_ge(loaded, 32)
            for b in range(B):
                dve.wait_ge(transposed, b + 1)
                dve.tensor_tensor(res[:, b * T:(b + 1) * T].rearrange("p t c -> p (t c)"), tr[:, b % 2, :],
                                  part[:, b * T:(b + 1) * T].rearrange("p t c -> p (t c)"), ALU.add).then_inc(added, 1)


def program(nc, a):
    with nc.sbuf_tensor("x_all", [P, B, 1 + N], F32) as X:
        layernorm_part(nc, a["x"], a["ident"], X)
        global_attention_part(nc, a["x"], a["ga_w"], a["ga_rope"], a["ident"], X, a["sum"], a["ga_parts"], a["ga_maxes"])
        layers_part(nc, X, a)
        final_part(nc, a["sum"], a["ident"], X, a["out"])


def rope_tables():
    f = np.float32
    inv = np.power(f(10000.0), (f(-2.0) * np.arange(GD // 2, dtype=f) / f(GD)).astype(f)).astype(f)
    ang = np.arange(N, dtype=f)[:, None] * inv[None]
    cos, sin = (np.tile(np.repeat(g(ang), 2, axis=-1).T, (GH, 1)) for g in (np.cos, np.sin))
    sign = np.where(np.arange(P) % 2 == 0, -1, 1).astype(f)
    return np.ascontiguousarray(np.stack([cos, sin * sign[:, None]], axis=1).astype(f))


def rotation_tables():
    f = np.float32
    half = np.arange(0, LD, 2, dtype=f)
    t = np.arange(N, dtype=f)
    ang = t[:, None] * (f(1.0) / np.power(f(10000.0), half / f(LD))).astype(f)[None]
    scale = np.power(((half + f(0.4 * LD)) / f(1.4 * LD))[None], ((t - N // 2) / f(WIN // 2))[:, None]).astype(f)
    four = [f(8.0) * np.cos(ang) * scale, f(8.0) * np.sin(ang) * scale, np.cos(ang) / scale, np.sin(ang) / scale]
    return np.ascontiguousarray(np.stack([np.tile(a.T, (4, 1)) for a in four], axis=1).astype(f))


def score_mask():
    q = np.arange(P) % WIN
    k = np.arange(SPAN)
    seen = (q[:, None] <= k) & (k <= q[:, None] + WIN)
    first = (np.arange(P)[:, None] >= WIN) | (k[None] >= WIN)
    m = np.zeros((P, T, 4, SPAN), np.float32)
    m[:] = np.where(seen, 0, MASKED)[:, None, None]
    m[:, 0] = np.where(seen & first, 0, MASKED)[:, None]
    return m.reshape(P, 2, 512)


def constants():
    p = np.arange(P)
    pick = np.zeros((P, 8), np.float32)
    for r in p[p % 32 < 4]:
        pick[r, 4 * (r // 64) + r % 32] = 1
    return {
        "ident": np.eye(P, dtype=np.float32),
        "ones": np.full((P, P), 1.0 / C, np.float32),
        "heads": (p[:, None] // 32 == np.arange(32)[None] % 4).astype(np.float32),
        "pick": pick,
        "mask": score_mask(),
        "identb": np.eye(P, dtype=np.float32),
        "ga_rope": rope_tables(),
        "rot": rotation_tables(),
    }


def laid_out(i):
    a = {k: np.asarray(v) for k, v in i.items()}
    swap = np.arange(P) ^ 1
    wq, wk, wv = a["L0_attn_Wq"].T, a["L0_attn_Wk"].T, a["L0_attn_Wv"].T
    qkv = a["L0_ffn_Wqkv"].reshape(LAYERS, C, 3, LH, LD)
    qk = qkv[:, :, :2].reshape(LAYERS, C, 2, UNITS, 4, 2, HALF).transpose(0, 1, 3, 2, 5, 4, 6)
    pair = lambda m: m.reshape(LAYERS, LH // 2, P, C).transpose(0, 2, 1, 3)
    w2 = np.zeros((LAYERS, NC_, P, C), np.float32)
    vec = np.zeros((LAYERS, P, NVEC), np.float32)
    for c, (k, w) in enumerate(CHUNKS):
        w2[:, c, :w] = a["L0_ffn_W2"][:, k:k + w]
        for side in range(2):
            vec[:, :w, V_B1 + side * NC_ + c] = a["L0_ffn_b1"][:, side * HID + k:side * HID + k + w]
    for half in range(2):
        for col, name in ((V_QS, "q_scale"), (V_KS, "k_scale")):
            vec[:, :, col + half] = np.tile(a["L0_ffn_" + name][:, half * HALF:(half + 1) * HALF], (1, 4))
    vec[:, :, V_G], vec[:, :, V_BLN], vec[:, :, V_B2] = a["L0_ffn_ln_g"], a["L0_ffn_ln_b"], a["L0_ffn_b2"]
    return {
        "x": a["L0_attn_x"],
        "ga_w": np.stack([wq, wq[:, swap], wk, wk[:, swap], wv], axis=1),
        "wqk": qk.reshape(LAYERS, C, UNITS, 4, P),
        "wv": pair(qkv[:, :, 2].reshape(LAYERS, C, INNER).transpose(0, 2, 1)),
        "wo": pair(a["L0_ffn_Wo"]),
        "w1": a["L0_ffn_W1"],
        "w2": w2.transpose(0, 2, 1, 3),
        "vec": vec,
    }


def kernel(**inputs):
    import ml_dtypes
    import concourse.bacc as bacc
    from concourse.bass_utils import run_bass_kernel_spmd

    nc = bacc.Bacc("TRN2", target_bir_lowering=False, num_devices=1)
    arrays = {**laid_out(inputs), **constants()}
    for n in ("mask", "identb"):
        arrays[n] = arrays[n].astype(ml_dtypes.bfloat16)
    arrays = {n: np.ascontiguousarray(v) for n, v in arrays.items()}
    aps = {n: nc.dram_tensor("in_" + n, v.shape, mybir.dt.from_np(v.dtype), kind="ExternalInput").ap() for n, v in arrays.items()}
    for n, shape, dt, kind in (("sum", (B, N, C), F32, "Internal"), ("ga_parts", (B, P, 2, 3, N), BF16, "Internal"),
                               ("ga_maxes", (B, GH * T, 3, P), BF16, "Internal"), ("out", (B, N, C), F32, "ExternalOutput")):
        aps[n] = nc.dram_tensor(n + "_dram", shape, dt, kind=kind).ap()
    program(nc, aps)
    r = run_bass_kernel_spmd(nc, [{"in_" + n: v for n, v in arrays.items()}], core_ids=[0])
    return r.results[0]["out_dram"]
```

```python
from contextlib import ExitStack

import numpy as np
import concourse.bass as bass
from concourse import mybir

F32 = mybir.dt.float32
BF16 = mybir.dt.bfloat16
I32 = mybir.dt.int32
ALU = mybir.AluOpType
ACT = mybir.ActivationFunctionType
AX = mybir.AxisListType

P = 128
B, N, C = 8, 512, 128
T = N // P
EPS = 1e-5

GH, GD = 16, 8
GROUPS = 4
TERMS = ((0, 0), (0, 1), (1, 0), (1, 1), (0, 2), (2, 0))
KROWS = len(TERMS) * GD
AROWS = KROWS + 3

RSQRT_MAGIC = float(0x5F3759DF)


class Signal:

    def __init__(self, sem, per):
        self.sem, self.per = sem, per

    def at(self, batch, n):
        assert 1 <= n <= self.per
        return batch * self.per + self.per + n

    def before(self, batch):
        return batch * self.per + self.per


def rsqrt(eng, y, x, t, steps, batch, n):
    eng.tensor_scalar(y.bitcast(I32), x.bitcast(I32), -0.5, RSQRT_MAGIC, ALU.mult, ALU.add).then_inc(steps.sem, 1)
    for i in range(3):
        eng.wait_ge(steps.sem, steps.at(batch, n + 3 * i + 1))
        eng.tensor_tensor(t, y, y, ALU.mult).then_inc(steps.sem, 1)
        eng.wait_ge(steps.sem, steps.at(batch, n + 3 * i + 2))
        eng.scalar_tensor_tensor(t, t, -0.5, x, ALU.mult, ALU.mult).then_inc(steps.sem, 1)
        eng.wait_ge(steps.sem, steps.at(batch, n + 3 * i + 3))
        eng.scalar_tensor_tensor(y, t, 1.5, y, ALU.add, ALU.mult).then_inc(steps.sem, 1)
    eng.wait_ge(steps.sem, steps.at(batch, n + RSQRT_LINKS))


RSQRT_LINKS = 10
NORM_LINKS = RSQRT_LINKS + 2


def layernorm_part(nc, x_dram, ident_dram, X):
    with ExitStack() as ctx:
        sb = lambda n, s, d=F32: ctx.enter_context(nc.sbuf_tensor(n, s, d))
        sem = lambda n: ctx.enter_context(nc.semaphore(n))
        xt = sb("ln_xt", [P, B * T, C])
        xn = sb("ln_xn", [P, B * T, C])
        ident = sb("ln_ident", [P, P])
        stats = sb("ln_stats", [P, B * T, 6])
        mv = sb("ln_mv", [P, B * T, 2])
        var = sb("ln_var", [P, B * T])
        rstd = sb("ln_rstd", [P, B * T])
        tmp = sb("ln_tmp", [P, B * T])
        tr = ctx.enter_context(nc.psum_tensor("ln_tr", [P, 2, 512], F32))
        loaded, ident_loaded, normed, transposed, copied = (
            sem(n) for n in ("ln_loaded", "ln_ident_loaded", "ln_normed", "ln_transposed", "ln_copied"))
        chain = Signal(sem("ln_chain"), 3 + RSQRT_LINKS)
        block = ctx.enter_context(nc.Block())

        @block.sync
        def _(sp):
            sp.dma_start(xt[:], x_dram.rearrange("b (t p) c -> p (b t) c", p=P)).then_inc(loaded, 16)
            sp.dma_start(ident[:], ident_dram).then_inc(ident_loaded, 16)

        @block.vector
        def _(dve):
            dve.sem_inc(chain.sem, chain.per)
            dve.wait_ge(loaded, 16)
            for i in range(B * T):
                last = dve.bn_stats(stats[:, i, :], xt[:, i, :])
            last.then_inc(chain.sem, 1)
            dve.wait_ge(chain.sem, chain.at(0, 1))
            for i in range(B * T):
                last = dve.bn_aggr(mv[:, i, :], stats[:, i, :])
            last.then_inc(chain.sem, 1)
            dve.wait_ge(chain.sem, chain.at(0, 2))
            dve.tensor_scalar(var[:], mv[:, :, 1], EPS, None, ALU.add).then_inc(chain.sem, 1)
            dve.wait_ge(chain.sem, chain.at(0, 3))
            rsqrt(dve, rstd[:], var[:], tmp[:], chain, 0, 3)
            for i in range(B * T):
                dve.tensor_scalar(xn[:, i, :], xt[:, i, :], mv[:, i, 0:1], rstd[:, i:i + 1],
                                  ALU.subtract, ALU.mult).then_inc(normed, 1)

        @block.tensor
        def _(pe):
            pe.wait_ge(ident_loaded, 16)
            for b in range(B):
                pe.wait_ge(normed, T * (b + 1))
                if b >= 2:
                    pe.wait_ge(copied, b - 1)
                for t in range(T):
                    last = pe.transpose(tr[:, b % 2, t * P:(t + 1) * P], xn[:, b * T + t, :], ident[:])
                last.then_inc(transposed, 1)

        @block.scalar
        def _(act):
            for b in range(B):
                act.wait_ge(transposed, b + 1)
                act.copy(X[:, b, 1:1 + N], tr[:, b % 2, :]).then_inc(copied, 1)

        @block.gpsimd
        def _(pool):
            pool.memset(X[:, :, 0:1], 0.0)


def global_attention_part(nc, x_dram, w_dram, rope_dram, ident_dram, X, sum_dram, parts_dram, maxes_dram):
    with ExitStack() as ctx:
        sb = lambda n, s, d=F32: ctx.enter_context(nc.sbuf_tensor(n, s, d))
        ps = lambda n, s, d=F32: ctx.enter_context(nc.psum_tensor(n, s, d))
        sem = lambda n: ctx.enter_context(nc.semaphore(n))
        signal = lambda n, per: Signal(sem(n), per)
        w = sb("ga_w", [P, 5, P])
        rope = sb("ga_rope", [P, 2, N])
        ident = sb("ga_ident", [P, P])
        xa = sb("ga_xa", [P, N])
        prod = sb("ga_prod", [P, 4, N])
        full = sb("ga_full", [P, 2, 3, N])
        parts = sb("ga_parts", [P, 2, 3, N], BF16)
        qs = sb("ga_qs", [P, GH // 2, N], BF16)
        ks = sb("ga_ks", [P, GH // 2, N], BF16)
        va = sb("ga_va", [P, T, GH, 32])
        mx = sb("ga_mx", [P, GH * T])
        mfull = sb("ga_mfull", [GH * T, 3, P])
        mparts = sb("ga_mparts", [GH * T, 3, P], BF16)
        pt = sb("ga_pt", [P, 8, 2, N])
        os = sb("ga_os", [P, 2, N])
        rec = sb("ga_rec", [P, T, 4])
        xraw = sb("ga_xraw", [P, T, C])
        y = sb("ga_y", [P, T, C])
        s_ps = ps("ga_s_ps", [P, 4, N])
        pv_ps = ps("ga_pv_ps", [P, 2, N])
        aux_ps = ps("ga_aux_ps", [P, 2, N])
        consts, init = sem("ga_consts"), sem("ga_init")
        xa_ready = signal("ga_xa_ready", 1)
        proj_ready = signal("ga_proj_ready", 5)
        prod_done = signal("ga_prod_done", 4)
        v_ready = signal("ga_v_ready", 1)
        full_ready = signal("ga_full_ready", 6)
        parts_ready = signal("ga_parts_ready", 6)
        parts_out = [signal(f"ga_{n}_parts_out", 16) for n in "qk"]
        stacked = signal("ga_stacked", 16 * 4 * len(TERMS))
        s_ready = signal("ga_s_ready", 64)
        max_done = signal("ga_max_done", 64)
        mt_ready = signal("ga_mt_ready", 1)
        m_steps = signal("ga_m_steps", 6)
        m_out = signal("ga_m_out", 16)
        m_rows = signal("ga_m_rows", 16 * GH)
        st_ready = signal("ga_st_ready", 32)
        exp_done = signal("ga_exp_done", 32)
        pv_done = signal("ga_pv_done", 16)
        os_ready = signal("ga_os_ready", 4)
        ot_ready = signal("ga_ot_ready", 4)
        out_steps = signal("ga_out_steps", 8)
        x_loaded = signal("ga_x_loaded", 16)
        y_ready = signal("ga_y_ready", 1)
        stored = signal("ga_stored", 16)
        block = ctx.enter_context(nc.Block())

        def place(h):
            return 64 * (h % 2), h // 2

        @block.sync
        def _(sp):
            for s in (*parts_out, stacked, m_out, m_rows, x_loaded, stored):
                sp.sem_inc(s.sem, s.per)
            sp.dma_start(w[:], w_dram).then_inc(consts, 16)
            sp.dma_start(rope[:], rope_dram).then_inc(consts, 16)
            sp.dma_start(ident[:], ident_dram).then_inc(consts, 16)
            sp.wait_ge(init, 3)
            with sp.Fori(0, B) as b:
                sp.wait_ge(y_ready.sem, y_ready.before(b))
                sp.dma_start(xraw[:], x_dram[bass.ds(b, 1)].rearrange("o (t p) c -> p (o t) c", p=P)).then_inc(x_loaded.sem, 16)
                for a in range(2):
                    sp.wait_ge(parts_ready.sem, parts_ready.at(b, 3 * a + 3))
                    sp.dma_start(parts_dram[bass.ds(b, 1), :, a].rearrange("o p c n -> (o p) c n"), parts[:, a]).then_inc(parts_out[a].sem, 16)
                sp.wait_ge(st_ready.sem, st_ready.before(b))
                for a, dst in ((0, qs), (1, ks)):
                    sp.wait_ge(parts_out[a].sem, parts_out[a].at(b, 16))
                    for z in range(2):
                        for j, term in enumerate(TERMS):
                            at = 64 * z + GD * j
                            src = parts_dram[bass.ds(b, 1), :, a, term[a]].rearrange("o (hp z d) n -> z d (o hp) n", z=2, d=GD)
                            sp.dma_start(dst[at:at + GD], src[z]).then_inc(stacked.sem, 16)
                sp.wait_ge(m_steps.sem, m_steps.at(b, 6))
                sp.dma_start(maxes_dram[bass.ds(b, 1)].rearrange("o r c n -> (o r) c n"), mparts[:]).then_inc(m_out.sem, 16)
                sp.wait_ge(m_out.sem, m_out.at(b, 16))
                for z in range(2):
                    src = maxes_dram[bass.ds(b, 1)].rearrange("o (hp z t) c n -> z c (o hp) t n", z=2, t=T)[z]
                    for hp in range(GH // 2):
                        sp.dma_start(qs[64 * z + KROWS:64 * z + AROWS, hp].rearrange("c (t n) -> c t n", t=T), src[:, hp]).then_inc(m_rows.sem, 16)
                sp.wait_ge(y_ready.sem, y_ready.at(b, 1))
                sp.dma_start(sum_dram[bass.ds(b, 1)].rearrange("o (t p) c -> p (o t) c", p=P), y[:]).then_inc(stored.sem, 16)
            sp.wait_ge(stored.sem, stored.before(B))

        @block.tensor
        def _(pe):
            for s in (proj_ready, s_ready, mt_ready, st_ready, pv_done, ot_ready):
                pe.sem_inc(s.sem, s.per)
            pe.wait_ge(consts, 48)
            with pe.Fori(0, B) as b:
                pe.wait_ge(xa_ready.sem, xa_ready.at(b, 1))
                pe.wait_ge(out_steps.sem, out_steps.before(b))
                for i in range(4):
                    if i >= 2:
                        pe.wait_ge(prod_done.sem, prod_done.at(b, i - 1))
                    pe.matmul(aux_ps[:, i % 2, :], w[:, i, :], xa[:], start=True, stop=True).then_inc(proj_ready.sem, 1)
                pe.wait_ge(prod_done.sem, prod_done.at(b, 3))
                for t in range(T):
                    last = pe.matmul(aux_ps[:, 0, t * P:(t + 1) * P], xa[:, t * P:(t + 1) * P], w[:, 4, :], start=True, stop=True)
                last.then_inc(proj_ready.sem, 1)
                pe.wait_ge(stacked.sem, stacked.at(b, stacked.per))
                for i in range(GH * T):
                    z, hp = place(i // T)
                    t = i % T
                    if i < 4:
                        pe.wait_ge(exp_done.sem, exp_done.before(b))
                    else:
                        pe.wait_ge(max_done.sem, max_done.at(b, i - 3))
                    pe.matmul(s_ps[:, i % 4, :], qs[z:z + KROWS, hp, t * P:(t + 1) * P], ks[z:z + KROWS, hp, :],
                              start=True, stop=True).then_inc(s_ready.sem, 1)
                pe.wait_ge(max_done.sem, max_done.at(b, 64))
                pe.wait_ge(prod_done.sem, prod_done.at(b, 4))
                pe.matmul(aux_ps[0:GH * T, 1, 0:P], mx[:], ident[:], start=True, stop=True).then_inc(mt_ready.sem, 1)

                def pv(q):
                    j, kt = q // T, q % T
                    pe.wait_ge(exp_done.sem, exp_done.at(b, 2 * q + 2))
                    if kt == 0 and j >= 2:
                        pe.wait_ge(os_ready.sem, os_ready.at(b, j - 1))
                    for c in range(4):
                        last = pe.matmul(pv_ps[32 * c:32 * c + 32, j % 2, :], va[:, kt, 4 * j + c, :],
                                         pt[:, (2 * q + c // 2) % 8, c % 2, :], start=(kt == 0), stop=(kt == T - 1),
                                         skip_group_check=True)
                    last.then_inc(pv_done.sem, 1)

                def out(j):
                    pe.wait_ge(os_ready.sem, os_ready.at(b, j + 1))
                    if j >= 2:
                        pe.wait_ge(out_steps.sem, out_steps.at(b, 2 * j - 2))
                    elif j == 1:
                        pe.wait_ge(m_steps.sem, m_steps.at(b, 1))
                    else:
                        pe.wait_ge(v_ready.sem, v_ready.at(b, 1))
                    for t in range(T):
                        last = pe.transpose(aux_ps[:, j % 2, t * P:(t + 1) * P], os[:, j % 2, t * P:(t + 1) * P], ident[:])
                    last.then_inc(ot_ready.sem, 1)

                pe.wait_ge(m_rows.sem, m_rows.at(b, m_rows.per))
                pe.wait_ge(v_ready.sem, v_ready.at(b, 1))
                for q in range(16):
                    j, kt = q // T, q % T
                    for c in range(4):
                        z, hp = place(4 * j + c)
                        pair = 2 * q + c // 2
                        if c % 2 == 0 and pair >= 2:
                            pe.wait_ge(exp_done.sem, exp_done.at(b, pair - 1))
                        mm = pe.matmul(s_ps[:, 2 * (pair % 2) + c % 2, :], ks[z:z + AROWS, hp, kt * P:(kt + 1) * P],
                                       qs[z:z + AROWS, hp, :], start=True, stop=True)
                        if c % 2 == 1:
                            mm.then_inc(st_ready.sem, 1)
                    if q >= 1:
                        pv(q - 1)
                    if q >= 5 and q % 4 == 1:
                        out(q // 4 - 1)
                pv(15)
                out(3)

        @block.vector
        def _(dve):
            for s in (prod_done, max_done, m_steps, out_steps):
                dve.sem_inc(s.sem, s.per)
            dve.memset(va[:], 0.0).then_inc(init, 1)
            dve.memset(ks[:], 1.0).then_inc(init, 1)
            dve.wait_ge(init, 2)
            dve.memset(va[:, :, :, GD:GD + 1], 1.0).then_inc(init, 1)
            dve.wait_ge(consts, 48)
            with dve.Fori(0, B) as b:
                dve.wait_ge(full_ready.sem, full_ready.before(b))
                for i in range(4):
                    dve.wait_ge(proj_ready.sem, proj_ready.at(b, i + 1))
                    dve.tensor_tensor(prod[:, i, :], aux_ps[:, i % 2, :], rope[:, i % 2, :], ALU.mult).then_inc(prod_done.sem, 1)
                dve.wait_ge(mt_ready.sem, mt_ready.before(b))
                for i in range(GH * T):
                    dve.wait_ge(s_ready.sem, s_ready.at(b, i + 1))
                    dve.tensor_reduce(mx[:, i:i + 1], s_ps[:, i % 4, :], AX.X, ALU.max).then_inc(max_done.sem, 1)
                dve.wait_ge(mt_ready.sem, mt_ready.at(b, 1))
                dve.wait_ge(m_out.sem, m_out.before(b))
                dve.tensor_scalar(mfull[:, 0, :], aux_ps[0:GH * T, 1, 0:P], -1.0, None, ALU.mult).then_inc(m_steps.sem, 1)
                for c in range(3):
                    dve.wait_ge(m_steps.sem, m_steps.at(b, 2 * c + 1))
                    dve.tensor_copy(mparts[:, c, :], mfull[:, c, :]).then_inc(m_steps.sem, 1)
                    if c < 2:
                        dve.wait_ge(m_steps.sem, m_steps.at(b, 2 * c + 2))
                        dve.tensor_tensor(mfull[:, c + 1, :], mfull[:, c, :], mparts[:, c, :], ALU.subtract).then_inc(m_steps.sem, 1)
                dve.wait_ge(y_ready.sem, y_ready.before(b))
                dve.wait_ge(stored.sem, stored.before(b))
                for j in range(GROUPS):
                    dve.wait_ge(ot_ready.sem, ot_ready.at(b, j + 1))
                    o = aux_ps[:, j % 2, :].rearrange("p (t c e) -> p t c e", t=T, c=4)
                    if j:
                        dve.wait_ge(out_steps.sem, out_steps.at(b, 2 * j))
                    dve.reciprocal(rec[:], o[:, :, :, GD]).then_inc(out_steps.sem, 1)
                    dve.wait_ge(out_steps.sem, out_steps.at(b, 2 * j + 1))
                    dve.tensor_tensor(y[:, :, 32 * j:32 * j + 32].rearrange("p t (c d) -> p t c d", d=GD), o[:, :, :, 0:GD],
                                      rec[:].unsqueeze(3).to_broadcast([P, T, 4, GD]), ALU.mult).then_inc(out_steps.sem, 1)

        @block.scalar
        def _(act):
            for s in (parts_ready, v_ready, exp_done, os_ready):
                act.sem_inc(s.sem, s.per)
            act.wait_ge(init, 3)
            with act.Fori(0, B) as b:
                act.wait_ge(pv_done.sem, pv_done.before(b))
                for a in range(2):
                    act.wait_ge(parts_out[a].sem, parts_out[a].before(b))
                    for c in range(3):
                        act.wait_ge(full_ready.sem, full_ready.at(b, 3 * a + c + 1))
                        act.copy(parts[:, a, c, :], full[:, a, c, :]).then_inc(parts_ready.sem, 1)
                act.wait_ge(proj_ready.sem, proj_ready.at(b, 5))
                act.copy(va[:, :, :, 0:GD], aux_ps[:, 0, :].rearrange("p (t h d) -> p t h d", t=T, h=GH)).then_inc(v_ready.sem, 1)

                def take(j):
                    act.wait_ge(pv_done.sem, pv_done.at(b, 4 * j + 4))
                    if j >= 2:
                        act.wait_ge(ot_ready.sem, ot_ready.at(b, j - 1))
                    else:
                        act.wait_ge(ot_ready.sem, ot_ready.before(b))
                    act.copy(os[:, j % 2, :], pv_ps[:, j % 2, :]).then_inc(os_ready.sem, 1)

                for pair in range(32):
                    act.wait_ge(st_ready.sem, st_ready.at(b, pair + 1))
                    if pair >= 8 and pair % 2 == 0:
                        act.wait_ge(pv_done.sem, pv_done.at(b, pair // 2 - 3))
                    act.activation(pt[:, pair % 8], s_ps[:, 2 * (pair % 2):2 * (pair % 2) + 2, :], ACT.Exp,
                                   scale=float(GD) ** -0.5).then_inc(exp_done.sem, 1)
                    if pair >= 10 and pair % 8 == 2:
                        take(pair // 8 - 1)
                take(3)

        @block.gpsimd
        def _(pool):
            for s in (xa_ready, full_ready, y_ready):
                pool.sem_inc(s.sem, s.per)
            with pool.Fori(0, B) as b:
                pool.wait_ge(proj_ready.sem, proj_ready.before(b))
                pool.tensor_copy(xa[:], X[:, bass.ds(b, 1), 1:1 + N].rearrange("p o n -> p (o n)")).then_inc(xa_ready.sem, 1)
                pool.wait_ge(parts_ready.sem, parts_ready.before(b))
                for a in range(2):
                    pool.wait_ge(prod_done.sem, prod_done.at(b, 2 * a + 2))
                    pool.tensor_tensor(full[:, a, 0, :], prod[:, 2 * a, :], prod[:, 2 * a + 1, :], ALU.add).then_inc(full_ready.sem, 1)
                    for c in range(2):
                        pool.wait_ge(full_ready.sem, full_ready.at(b, 3 * a + c + 1))
                        pool.wait_ge(parts_ready.sem, parts_ready.at(b, 3 * a + c + 1))
                        pool.tensor_tensor(full[:, a, c + 1, :], full[:, a, c, :], parts[:, a, c, :], ALU.subtract).then_inc(full_ready.sem, 1)
                pool.wait_ge(x_loaded.sem, x_loaded.at(b, 16))
                pool.wait_ge(out_steps.sem, out_steps.at(b, 8))
                pool.tensor_tensor(y[:], y[:], xraw[:], ALU.add).then_inc(y_ready.sem, 1)


LAYERS = 6
LH, LD = 16, 64
HALF = LD // 2
INNER = LH * LD
WIN = 32
NW = N // WIN
SPAN = 2 * WIN
HID = C * 4 * 2 // 3
CHUNKS = tuple((k, min(P, HID - k)) for k in range(0, HID, P))
NC_ = len(CHUNKS)
MASKED = -1e30
TINY = 1e-24
V_G, V_BLN, V_B1, V_B2, NVEC = 0, 1, 2, 2 + 2 * NC_, 3 + 2 * NC_
UNITS = 4


def layers_part(nc, X, d):
    with ExitStack() as ctx:
        sb = lambda n, s, dt=F32: ctx.enter_context(nc.sbuf_tensor(n, s, dt))
        ps = lambda n, s, dt=F32: ctx.enter_context(nc.psum_tensor(n, s, dt))
        sem = lambda n: ctx.enter_context(nc.semaphore("ly_" + n))
        signal = lambda n, per: Signal(sem(n), per)

        wqk = sb("ly_wqk", [P, UNITS, 4, P])
        mvo = sb("ly_mvo", [P, LH, P])
        wv_raw = sb("ly_wv", [P, LH // 2, P])
        wo_raw = sb("ly_wo", [P, LH // 2, P])
        gains = sb("ly_gains", [P, 4])
        w1 = sb("ly_w1", [P, 2 * HID])
        w2 = sb("ly_w2", [P, NC_, P])
        vec = sb("ly_vec", [P, NVEC])
        rot = sb("ly_rot", [P, 8, N])
        ident = sb("ly_ident", [P, P])
        ones = sb("ly_ones", [P, P])
        heads = sb("ly_heads", [P, 32])
        pick = sb("ly_pick", [P, 8])
        mask = sb("ly_mask", [P, 2, 512], BF16)
        identb = sb("ly_identb", [P, P], BF16)
        tables = sb("ly_tables", [P, 4, N])
        xs = sb("ly_xs", [P, WIN + N])
        prod = sb("ly_prod", [P, 8, N])
        sq = sb("ly_sq", [P, 4, N])
        nsum = sb("ly_nsum", [P, N])
        ss = sb("ly_ss", [P, T, 8])
        rn = sb("ly_rn", [P, 2, T, 8])
        rt = sb("ly_rt", [P, T, 8])
        rnx = sb("ly_rnx", [P, T, 4, HALF])
        qr = sb("ly_qr", [P, 2, N])
        qp = sb("ly_qp", [P, 2, 2, N])
        kr = sb("ly_kr", [P, 2, N])
        kn = sb("ly_kn", [P, 2, N])
        kbd = sb("ly_kbd", [P, 2, 2, WIN + N])
        sx = sb("ly_sx", [P, 2, T, 4, SPAN])
        smax = sb("ly_smax", [P, 2, T, 4])
        rsum = sb("ly_rsum", [P, 2, T, 4])
        pt = sb("ly_pt", [P, NW, LH // 2, WIN])
        xtok = sb("ly_xtok", [P, NW, P])
        u = sb("ly_u", [P, LH, 2, 4, WIN])
        xf = sb("ly_xf", [P, N])
        xc = sb("ly_xc", [P, N])
        csq = sb("ly_csq", [P, N])
        rstd = sb("ly_rstd", [P, 3, T])
        gate = sb("ly_gate", [P, 2, N])
        hid = sb("ly_hid", [P, NC_, N])

        pj_ps = ps("ly_pj_ps", [P, 2, N])
        nr_ps = ps("ly_nr_ps", [P, N])
        st_ps = ps("ly_st_ps", [P, 2, 512])
        ta_ps = ps("ly_ta_ps", [P, 2, 512])
        to_ps = ps("ly_to_ps", [P, 512])

        consts, init = sem("consts"), sem("init")
        core_loaded = signal("core_loaded", 16 * 2)
        raw_loaded = signal("raw_loaded", 16 * 2)
        tail_loaded = signal("tail_loaded", 16 * 3)
        rot_ready = signal("rot_ready", 8)
        mvo_ready = signal("mvo_ready", 4)
        mvo_copied = signal("mvo_copied", 4)
        xs_ready = signal("xs_ready", 2)
        proj_ready = signal("proj_ready", 16)
        sq_done = signal("sq_done", 16)
        prod_done = signal("prod_done", 32)
        rot_done = signal("rot_done", 16)
        ns_ready = signal("ns_ready", 4)
        ns_copied = signal("ns_copied", 4)
        ss_ready = signal("ss_ready", 4)
        rn_steps = signal("rn_steps", 4 * NORM_LINKS)
        r_ready = signal("r_ready", 4)
        kn_done = signal("kn_done", 8)
        kbd_loaded = signal("kbd_loaded", 16 * 8 * 4)
        qp_loaded = signal("qp_loaded", 16 * 4 * 4)
        s_ready = signal("s_ready", 4)
        s_scaled = signal("s_scaled", 4)
        s_max = signal("s_max", 4)
        s_less = signal("s_less", 4)
        p_exp = signal("p_exp", 4)
        p_sum = signal("p_sum", 8)
        p_ready = signal("p_ready", 4)
        t_ready = signal("t_ready", 4)
        pt_done = signal("pt_done", 4)
        xtr_ready = signal("xtr_ready", 2)
        xtok_done = signal("xtok_done", 2)
        u_ready = signal("u_ready", 16)
        u_copied = signal("u_copied", 16)
        att_ready = signal("att_ready", 4)
        x1_done = signal("x1_done", 1)
        xf_done = signal("xf_done", 2)
        mean_ready = signal("mean_ready", 1)
        xc_done = signal("xc_done", 1)
        csq_done = signal("csq_done", 1)
        var_ready = signal("var_ready", 1)
        var_steps = signal("var_steps", 1 + RSQRT_LINKS)
        rb_ready = signal("rb_ready", 1)
        xg_done = signal("xg_done", 1)
        xn_done = signal("xn_done", 1)
        h_ready = signal("h_ready", 2 * NC_)
        gate_done = signal("gate_done", NC_)
        hid_done = signal("hid_done", NC_)
        ffn_ready = signal("ffn_ready", 1)
        x2_done = signal("x2_done", 1)
        block = ctx.enter_context(nc.Block())

        def layers(eng, body, new_layer=lambda layer: None, old_layer=lambda layer: None):
            last = LAYERS - 1

            def middle(layer):
                with eng.Fori(2, B) as b:
                    n = layer * B + b
                    body((n, b), (n - 1, b - 1), (n - 2, b - 2, layer), None)

            new_layer(0)
            body((0, 0), None, None, 0)
            body((1, 1), (0, 0), None, None)
            with eng.Fori(0, last) as layer:
                middle(layer)
                n = layer * B + B
                new_layer(layer + 1)
                body((n, 0), (n - 1, B - 1), (n - 2, B - 2, layer), layer + 1)
                body((n + 1, 1), (n, 0), (n - 1, B - 1, layer), None)
                old_layer(layer)
            middle(last)
            n = LAYERS * B
            body(None, (n - 1, B - 1), (n - 2, B - 2, last), None)
            body(None, None, (n - 1, B - 1, last), None)

        def unit_tables(i):
            k, upper = i // 2, i % 2
            return ((4 * k + 1, 4 * k + 1), (4 * k + 2, 4 * k + 2)) if upper else ((4 * k, 4 * k), (4 * k + 3, 4 * k + 3))

        @block.sync
        def _(sp):
            for s in (core_loaded, raw_loaded, tail_loaded, kbd_loaded, qp_loaded):
                sp.sem_inc(s.sem, s.per)
            one = lambda a, layer: a[bass.ds(layer, 1)] if not isinstance(layer, int) else a[layer:layer + 1]

            def load_core(layer):
                sp.dma_start(wqk[:], one(d["wqk"], layer).rearrange("o p u i c -> p (o u) i c")).then_inc(core_loaded.sem, 16)
                sp.dma_start(gains[:], one(d["gains"], layer).rearrange("o p c -> p (o c)")).then_inc(core_loaded.sem, 16)

            def load_raw(layer):
                sp.dma_start(wv_raw[:], one(d["wv"], layer).rearrange("o p h c -> p (o h) c")).then_inc(raw_loaded.sem, 16)
                sp.dma_start(wo_raw[:], one(d["wo"], layer).rearrange("o p h c -> p (o h) c")).then_inc(raw_loaded.sem, 16)

            def load_tail(layer):
                sp.dma_start(w1[:], one(d["w1"], layer).rearrange("o p c -> p (o c)")).then_inc(tail_loaded.sem, 16)
                sp.dma_start(w2[:], one(d["w2"], layer).rearrange("o p h c -> p (o h) c")).then_inc(tail_loaded.sem, 16)
                sp.dma_start(vec[:], one(d["vec"], layer).rearrange("o p c -> p (o c)")).then_inc(tail_loaded.sem, 16)

            load_core(0)
            for dst, src in ((tables, d["rot"]), (ident, d["ident"]), (heads, d["heads"]), (pick, d["pick"]), (ones, d["ones"]),
                             (mask, d["mask"]), (identb, d["identb"])):
                sp.dma_start(dst[:], src).then_inc(consts, 16)
            load_raw(0)
            load_tail(0)
            sp.wait_ge(init, 2)

            def new_layer(layer):
                if isinstance(layer, int) and layer == 0:
                    return
                sp.wait_ge(proj_ready.sem, proj_ready.at(layer * B - 1, proj_ready.per))
                load_core(layer)
                load_raw(layer)

            def old_layer(layer):
                sp.wait_ge(x2_done.sem, x2_done.before(layer * B + B))
                load_tail(layer + 1)

            def body(core, tail, ffn, fresh):
                if core is None:
                    return
                n, _ = core
                for g in range(UNITS):
                    sp.wait_ge(rot_done.sem, rot_done.at(n, 4 * g + 2))
                    for p in range(2):
                        for half in range(2):
                            sp.dma_start(qp[64 * half:64 * half + 64, g % 2, p], qr[64 * p:64 * p + 64, half]).then_inc(qp_loaded.sem, 16)
                    sp.wait_ge(kn_done.sem, kn_done.at(n, 2 * g + 2))
                    for p in range(2):
                        for z in range(2):
                            for half in range(2):
                                src, dst = 64 * p + 32 * z, 64 * half + 32 * z
                                sp.dma_start(kbd[dst:dst + 32, p, z, WIN:], kn[src:src + 32, half]).then_inc(kbd_loaded.sem, 16)

            layers(sp, body, new_layer, old_layer)

        @block.tensor
        def _(pe):
            for s in (mvo_ready, proj_ready, ns_ready, ss_ready, r_ready, s_ready, t_ready, xtr_ready, u_ready,
                      att_ready, mean_ready, var_ready, rb_ready, h_ready, ffn_ready):
                pe.sem_inc(s.sem, s.per)
            pe.wait_ge(consts, 16 * 7)

            def new_layer(layer):
                pe.wait_ge(core_loaded.sem, core_loaded.at(layer, core_loaded.per))

            def body(core, tail, ffn, fresh):
                n, place = core or (None, None)
                m, tail_place = tail or (None, None)
                q, ffn_place, layer = ffn or (None, None, None)

                def project(g, *tiles):
                    if g == 0:
                        pe.wait_ge(xs_ready.sem, xs_ready.at(n, 2))
                    for i in tiles:
                        k = 4 * g + i - 2
                        if k < 0:
                            pe.wait_ge(prod_done.sem, prod_done.before(n))
                            pe.wait_ge(sq_done.sem, sq_done.before(n))
                        else:
                            pe.wait_ge(prod_done.sem, prod_done.at(n, 2 * k + 2))
                            pe.wait_ge(sq_done.sem, sq_done.at(n, k + 1))
                        pe.matmul(pj_ps[:, i % 2, :], wqk[:, g, i, :], xs[:, WIN:], start=True, stop=True).then_inc(proj_ready.sem, 1)

                def square_sums(g):
                    if g == 0:
                        pe.wait_ge(kn_done.sem, kn_done.before(n))
                    else:
                        pe.wait_ge(kn_done.sem, kn_done.at(n, 2 * g))
                    pe.wait_ge(sq_done.sem, sq_done.at(n, 4 * g + 4))
                    for i in range(4):
                        last = pe.matmul(nr_ps[32 * i:32 * i + 32, :], heads[:], sq[:, i, :], start=True, stop=True)
                    last.then_inc(ns_ready.sem, 1)

                def sums_by_token(g):
                    pe.wait_ge(ns_copied.sem, ns_copied.at(n, g + 1))
                    for t in range(T):
                        last = pe.matmul(nr_ps[:, 8 * t:8 * t + 8], nsum[:, t * P:(t + 1) * P], pick[:], start=True, stop=True)
                    last.then_inc(ss_ready.sem, 1)

                def spread_norms(g):
                    pe.wait_ge(rn_steps.sem, rn_steps.at(n, (g + 1) * NORM_LINKS))
                    for t in range(T):
                        last = pe.transpose(nr_ps[:, t * P:(t + 1) * P],
                                            rnx[:, t].rearrange("p h d -> p (h d)"), ident[:])
                    last.then_inc(r_ready.sem, 1)

                def scores(g, n=n):
                    if g == 0:
                        pe.wait_ge(pt_done.sem, pt_done.before(n))
                    elif g == 1:
                        pe.wait_ge(s_scaled.sem, s_scaled.at(n, 1))
                    else:
                        pe.wait_ge(pt_done.sem, pt_done.at(n, g - 1))
                    pe.wait_ge(qp_loaded.sem, qp_loaded.at(n, 16 * 4 * (g + 1)))
                    pe.wait_ge(kbd_loaded.sem, kbd_loaded.at(n, 16 * 8 * (g + 1)))
                    for bank in range(2):
                        pe.matmul(st_ps[:, bank, :], identb[:], mask[:, bank, :], start=True, stop=False, skip_group_check=True)
                    for t in range(T):
                        for p in range(2):
                            for c in range(4):
                                w, at = 4 * t + c, 256 * (t % 2) + 128 * p
                                last = pe.matmul(st_ps[32 * c:32 * c + 32, t // 2, at:at + 128], qp[:, g % 2, p, WIN * w:WIN * w + WIN],
                                                 kbd[:, p, :, WIN * w:WIN * w + SPAN], start=False, stop=True, skip_group_check=True)
                    last.then_inc(s_ready.sem, 1)

                def token_transposes(r):
                    if r == 0:
                        pe.wait_ge(s_scaled.sem, s_scaled.at(n, 2))
                    else:
                        pe.wait_ge(xtok_done.sem, xtok_done.at(n, 1))
                    for i in range(8):
                        w = 8 * r + i
                        for z in range(2):
                            last = pe.matmul(st_ps[64 * z:64 * z + SPAN, i // 4, (i % 4) * P:(i % 4 + 1) * P],
                                             xs[:, WIN * w:WIN * w + SPAN], ident[:], start=True, stop=True)
                    last.then_inc(xtr_ready.sem, 1)

                def prob_transposes(g, n=n):
                    if g == 0:
                        pe.wait_ge(xtok_done.sem, xtok_done.at(n, 2))
                    elif g < 3:
                        pe.wait_ge(s_scaled.sem, s_scaled.at(n, g + 2))
                    else:
                        pe.wait_ge(pt_done.sem, pt_done.at(n, 3))
                    pe.wait_ge(p_ready.sem, p_ready.at(n, g + 1))
                    for hp in range(2):
                        for t in range(T):
                            last = pe.transpose(st_ps[:, hp, t * P:(t + 1) * P], sx[:, g % 2, t, 2 * hp:2 * hp + 2, :], ident[:])
                    last.then_inc(t_ready.sem, 1)

                def attend(*ks):
                    for k in ks:
                        if k == 0:
                            pe.wait_ge(pt_done.sem, pt_done.at(m, 4))
                            pe.wait_ge(xtok_done.sem, xtok_done.at(m, 2))
                            pe.wait_ge(hid_done.sem, hid_done.before(m))
                            pe.wait_ge(gate_done.sem, gate_done.before(m))
                        for w in (2 * k, 2 * k + 1):
                            for z in range(2):
                                if k and w % 2 == 0:
                                    pe.wait_ge(u_copied.sem, u_copied.at(m, 2 * k - 1 + z))
                                mm = pe.matmul(ta_ps[:, z, 256 * (w % 2):256 * (w % 2) + 256], xtok[64 * z:64 * z + 64, w, :],
                                               pt[64 * z:64 * z + 64, w, :, :], start=True, stop=True)
                                if w % 2:
                                    mm.then_inc(u_ready.sem, 1)

                def combine(r, half):
                    if half == 0:
                        pe.wait_ge(u_copied.sem, u_copied.at(m, 4 * r + 4))
                        if r == 0:
                            pe.wait_ge(x2_done.sem, x2_done.before(m))
                    for h in range(8 * half, 8 * half + 8):
                        last = pe.matmul(to_ps[:, P * r:P * r + P], mvo[:, h, :], u[:, h, r % 2], start=(h == 0), stop=(h == LH - 1),
                                         skip_group_check=True)
                    if half:
                        last.then_inc(att_ready.sem, 1)

                def value_output():
                    pe.wait_ge(raw_loaded.sem, raw_loaded.at(fresh, raw_loaded.per))
                    pe.wait_ge(u_copied.sem, u_copied.before(n))
                    for j in range(2):
                        if j:
                            pe.wait_ge(mvo_copied.sem, mvo_copied.at(fresh, 2))
                        for i in range(4):
                            for z in range(2):
                                rows = slice(64 * z, 64 * z + 64)
                                mm = pe.matmul(ta_ps[:, z, i * P:(i + 1) * P], wv_raw[rows, 4 * j + i, :], wo_raw[rows, 4 * j + i, :],
                                               start=True, stop=True)
                                if i == 3:
                                    mm.then_inc(mvo_ready.sem, 1)
                    pe.wait_ge(mvo_copied.sem, mvo_copied.at(fresh, 4))

                def mean():
                    pe.wait_ge(xf_done.sem, xf_done.at(q, 2))
                    pe.matmul(ta_ps[:, 0, :], ones[:], xf[:], start=True, stop=True).then_inc(mean_ready.sem, 1)

                def variance():
                    pe.wait_ge(csq_done.sem, csq_done.at(q, 1))
                    for t in range(T):
                        last = pe.matmul(ta_ps[:, 1, t:t + 1], csq[:, t * P:(t + 1) * P], ones[:, 0:1], start=True, stop=True)
                    last.then_inc(var_ready.sem, 1)

                def spread_rstd():
                    pe.wait_ge(var_steps.sem, var_steps.at(q, 1 + RSQRT_LINKS))
                    for t in range(T):
                        last = pe.transpose(ta_ps[:, 0, t * P:(t + 1) * P], rstd[:, 1, t:t + 1].to_broadcast([P, P]), ident[:])
                    last.then_inc(rb_ready.sem, 1)

                def hidden(c):
                    k, w = CHUNKS[c]
                    if c == 0:
                        pe.wait_ge(tail_loaded.sem, tail_loaded.at(layer, tail_loaded.per))
                        pe.wait_ge(xn_done.sem, xn_done.at(q, 1))
                    for side in (1, 0):
                        if c:
                            used = gate_done if side else hid_done
                            pe.wait_ge(used.sem, used.at(q, c))
                        pe.matmul(ta_ps[0:w, side, :], w1[:, side * HID + k:side * HID + k + w], csq[:],
                                  start=True, stop=True).then_inc(h_ready.sem, 1)

                def down(c):
                    k, w = CHUNKS[c]
                    pe.wait_ge(hid_done.sem, hid_done.at(q, c + 1))
                    if c == 0:
                        pe.wait_ge(x1_done.sem, x1_done.at(q, 1))
                    last = pe.matmul(to_ps[:], w2[0:w, c, :], hid[0:w, c, :], start=(c == 0), stop=(c == NC_ - 1), skip_group_check=True)
                    if c == NC_ - 1:
                        last.then_inc(ffn_ready.sem, 1)

                C_, T_, F_ = core is not None, tail is not None, ffn is not None
                if C_: project(0, 0, 1)
                if F_: mean()
                if C_: project(0, 2, 3)
                if F_: variance()
                if T_: scores(3, m)
                if C_: square_sums(0); sums_by_token(0)
                if F_: spread_rstd()
                if T_: prob_transposes(2, m)
                if C_: project(1, 0)
                if F_: hidden(0)
                if C_: spread_norms(0); project(1, 1)
                if F_: hidden(1)
                if C_: project(1, 2)
                if F_: down(0); hidden(2)
                if C_: project(1, 3)
                if F_: down(1); down(2)
                if C_: square_sums(1)
                if T_: prob_transposes(3, m)
                if C_: sums_by_token(1); project(2, 0)
                if T_: attend(0)
                if C_: project(2, 1)
                if T_: attend(1)
                if C_: scores(0); spread_norms(1)
                if T_: attend(2, 3)
                if C_: project(2, 2)
                if T_: combine(0, 0)
                if C_: project(2, 3)
                if T_: combine(0, 1)
                if C_: square_sums(2)
                if T_: attend(4)
                if C_: sums_by_token(2)
                if T_: attend(5); combine(1, 0)
                if C_: scores(1); spread_norms(2); project(3, 0)
                if T_: combine(1, 1)
                if C_: project(3, 1)
                if T_: attend(6)
                if C_: project(3, 2)
                if T_: attend(7)
                if C_: project(3, 3); token_transposes(0); square_sums(3); token_transposes(1); sums_by_token(3)
                if T_: combine(2, 0)
                if C_: prob_transposes(0)
                if T_: combine(2, 1)
                if C_: scores(2); spread_norms(3)
                if T_: combine(3, 0); combine(3, 1)
                if fresh is not None: value_output()
                if C_: prob_transposes(1)

            layers(pe, body, new_layer)

        @block.vector
        def _(dve):
            for s in (prod_done, rn_steps, kn_done, s_scaled, s_max, p_sum,
                      x1_done, xc_done, var_steps, xg_done, hid_done, x2_done, rot_ready):
                dve.sem_inc(s.sem, s.per)
            dve.memset(kbd[:], 0.0).then_inc(init, 1)
            dve.memset(xs[:], 0.0).then_inc(init, 1)
            dve.wait_ge(init, 2)
            dve.wait_ge(consts, 16 * 7)

            def new_layer(layer):
                dve.wait_ge(core_loaded.sem, core_loaded.at(layer, core_loaded.per))
                for i in range(8):
                    table, gain = 2 * (i // 4) + i % 2, 2 * (i // 4) + (0, 1, 1, 0)[i % 4]
                    dve.tensor_scalar(rot[:, i, :], tables[:, table, :], gains[:, gain:gain + 1], None, ALU.mult).then_inc(rot_ready.sem, 1)
                dve.wait_ge(rot_ready.sem, rot_ready.at(layer, 8))

            def body(core, tail, ffn, fresh):
                n, place = core or (None, None)
                m, tail_place = tail or (None, None)
                q, ffn_place, layer = ffn or (None, None, None)

                def products(g, *tiles):
                    for i in tiles:
                        dve.wait_ge(sq_done.sem, sq_done.at(n, 4 * g + i + 1))
                        for table, k in unit_tables(i):
                            if g == 0:
                                dve.wait_ge(rot_done.sem, rot_done.before(n))
                            elif i % 2 == 0:
                                dve.wait_ge(rot_done.sem, rot_done.at(n, 4 * (g - 1) + i + 2))
                            dve.tensor_tensor(prod[:, k, :], pj_ps[:, i % 2, :], rot[:, table, :], ALU.mult).then_inc(prod_done.sem, 1)

                def norms(g):
                    dve.wait_ge(ss_ready.sem, ss_ready.at(n, g + 1))
                    if g >= 2:
                        dve.wait_ge(r_ready.sem, r_ready.at(n, g - 1))
                    done = g * NORM_LINKS
                    dve.tensor_scalar(ss[:], nr_ps[:, 0:8 * T].rearrange("p (t k) -> p t k", k=8), TINY, None, ALU.max).then_inc(rn_steps.sem, 1)
                    dve.wait_ge(rn_steps.sem, rn_steps.at(n, done + 1))
                    rsqrt(dve, rn[:, g % 2], ss[:], rt[:], rn_steps, n, done + 1)
                    dve.tensor_copy(rnx[:], rn[:, g % 2, :, 4:8].unsqueeze(3).to_broadcast([P, T, 4, HALF])).then_inc(rn_steps.sem, 1)

                def scale_keys(g):
                    dve.wait_ge(r_ready.sem, r_ready.at(n, g + 1))
                    if g == 0:
                        dve.wait_ge(kbd_loaded.sem, kbd_loaded.before(n))
                    else:
                        dve.wait_ge(kbd_loaded.sem, kbd_loaded.at(n, 16 * 8 * g))
                    dve.wait_ge(rot_done.sem, rot_done.at(n, 4 * g + 4))
                    for half in range(2):
                        dve.tensor_tensor(kn[:, half, :], kr[:, half, :], nr_ps[:], ALU.mult).then_inc(kn_done.sem, 1)

                def scale_scores(g, n=n):
                    dve.wait_ge(s_ready.sem, s_ready.at(n, g + 1))
                    if g >= 2:
                        dve.wait_ge(t_ready.sem, t_ready.at(n, g - 1))
                    else:
                        dve.wait_ge(t_ready.sem, t_ready.before(n))
                    dve.tensor_tensor(sx[:, g % 2], st_ps[:].rearrange("p b (t h k) -> p (b t) h k", h=4, k=SPAN),
                                      rn[:, g % 2, :, 0:4].unsqueeze(3).to_broadcast([P, T, 4, SPAN]), ALU.mult).then_inc(s_scaled.sem, 1)
                    dve.wait_ge(s_scaled.sem, s_scaled.at(n, g + 1))
                    if g >= 2:
                        dve.wait_ge(s_less.sem, s_less.at(n, g - 1))
                    else:
                        dve.wait_ge(s_less.sem, s_less.before(n))
                    dve.tensor_reduce(smax[:, g % 2], sx[:, g % 2], AX.X, ALU.max).then_inc(s_max.sem, 1)

                def prob_sums(g, n=n):
                    dve.wait_ge(p_exp.sem, p_exp.at(n, g + 1))
                    if g >= 2:
                        dve.wait_ge(p_ready.sem, p_ready.at(n, g - 1))
                    else:
                        dve.wait_ge(p_ready.sem, p_ready.before(n))
                    dve.tensor_reduce(rsum[:, g % 2], sx[:, g % 2], AX.X, ALU.add).then_inc(p_sum.sem, 1)
                    dve.wait_ge(p_sum.sem, p_sum.at(n, 2 * g + 1))
                    dve.reciprocal(rsum[:, g % 2], rsum[:, g % 2]).then_inc(p_sum.sem, 1)

                batch = lambda place: X[:, bass.ds(place, 1), 1:1 + N].rearrange("p o n -> p (o n)")

                def attention_sum():
                    dve.wait_ge(att_ready.sem, att_ready.at(m, 4))
                    xb = batch(tail_place)
                    dve.tensor_tensor(xb, to_ps[:], xb, ALU.add).then_inc(x1_done.sem, 1)

                def centre():
                    dve.wait_ge(mean_ready.sem, mean_ready.at(q, 1))
                    dve.tensor_tensor(xc[:], xf[:], ta_ps[:, 0, :], ALU.subtract).then_inc(xc_done.sem, 1)

                def deviation():
                    dve.wait_ge(var_ready.sem, var_ready.at(q, 1))
                    dve.tensor_scalar(rstd[:, 0, :], ta_ps[:, 1, 0:T], EPS, None, ALU.add).then_inc(var_steps.sem, 1)
                    dve.wait_ge(var_steps.sem, var_steps.at(q, 1))
                    rsqrt(dve, rstd[:, 1, :], rstd[:, 0, :], rstd[:, 2, :], var_steps, q, 1)

                def normalise():
                    dve.wait_ge(rb_ready.sem, rb_ready.at(q, 1))
                    dve.wait_ge(tail_loaded.sem, tail_loaded.at(layer, tail_loaded.per))
                    dve.scalar_tensor_tensor(csq[:], xc[:], vec[:, V_G:V_G + 1], ta_ps[:, 0, :], ALU.mult, ALU.mult).then_inc(xg_done.sem, 1)

                def gated(c):
                    k, w = CHUNKS[c]
                    dve.wait_ge(h_ready.sem, h_ready.at(q, 2 * c + 2))
                    dve.wait_ge(gate_done.sem, gate_done.at(q, c + 1))
                    if c == 0:
                        dve.wait_ge(ffn_ready.sem, ffn_ready.before(q))
                    dve.scalar_tensor_tensor(hid[0:w, c, :], ta_ps[0:w, 0, :], vec[0:w, V_B1 + c:V_B1 + c + 1], gate[0:w, c % 2, :],
                                             ALU.add, ALU.mult).then_inc(hid_done.sem, 1)

                def ffn_sum():
                    dve.wait_ge(ffn_ready.sem, ffn_ready.at(q, 1))
                    dve.wait_ge(xf_done.sem, xf_done.at(q, 2))
                    xb = batch(ffn_place)
                    dve.scalar_tensor_tensor(xb, to_ps[:], vec[:, V_B2:V_B2 + 1], xb, ALU.add, ALU.add).then_inc(x2_done.sem, 1)

                C_, T_, F_ = core is not None, tail is not None, ffn is not None
                if C_: products(0, 0, 1)
                if F_: centre()
                if T_: prob_sums(2, m)
                if C_: products(0, 2, 3)
                if F_: deviation()
                if T_: scale_scores(3, m)
                if F_: normalise()
                if C_: norms(0); scale_keys(0)
                if F_: gated(0)
                if C_: products(1, 0, 1)
                if T_: prob_sums(3, m)
                if F_: gated(1)
                if C_: products(1, 2)
                if F_: gated(2)
                if C_: products(1, 3)
                if F_: ffn_sum()
                if C_: norms(1); products(2, 0, 1); scale_keys(1); scale_scores(0); products(2, 2); prob_sums(0); products(2, 3)
                if C_: norms(2); scale_keys(2); scale_scores(1); products(3, 0, 1, 2); prob_sums(1); products(3, 3)
                if C_: norms(3); scale_keys(3); scale_scores(2)
                if T_: attention_sum()

            layers(dve, body, new_layer)

        @block.scalar
        def _(act):
            for s in (xs_ready, xf_done, sq_done, ns_copied, p_exp, pt_done, xtok_done, u_copied, csq_done, xn_done, mvo_copied, gate_done):
                act.sem_inc(s.sem, s.per)
            act.wait_ge(init, 2)
            shifts = lambda dst, b: ((dst[0:64], X[0:64, bass.ds(b, 1), 1:1 + N]), (dst[64:128], X[64:128, bass.ds(b, 1), 0:N]))

            def body(core, tail, ffn, fresh):
                n, place = core or (None, None)
                m, tail_place = tail or (None, None)
                q, ffn_place, layer = ffn or (None, None, None)

                def tokens():
                    act.wait_ge(proj_ready.sem, proj_ready.before(n))
                    act.wait_ge(xtr_ready.sem, xtr_ready.before(n))
                    if ffn is not None:
                        act.wait_ge(x2_done.sem, x2_done.before(q))
                    for dst, src in shifts(xs[:, WIN:], place):
                        act.copy(dst, src.rearrange("p o n -> p (o n)")).then_inc(xs_ready.sem, 1)

                def ffn_tokens():
                    act.wait_ge(x1_done.sem, x1_done.at(q, 1))
                    act.wait_ge(xc_done.sem, xc_done.before(q))
                    for dst, src in shifts(xf[:], ffn_place):
                        act.copy(dst, src.rearrange("p o n -> p (o n)")).then_inc(xf_done.sem, 1)

                def squares(g, *tiles):
                    for i in tiles:
                        act.wait_ge(proj_ready.sem, proj_ready.at(n, 4 * g + i + 1))
                        if i == 0:
                            if g == 0:
                                act.wait_ge(ns_ready.sem, ns_ready.before(n))
                            else:
                                act.wait_ge(ns_ready.sem, ns_ready.at(n, g))
                        act.activation(sq[:, i, :], pj_ps[:, i % 2, :], ACT.Square).then_inc(sq_done.sem, 1)

                def copy_sums(g):
                    act.wait_ge(ns_ready.sem, ns_ready.at(n, g + 1))
                    if g == 0:
                        act.wait_ge(ss_ready.sem, ss_ready.before(n))
                    else:
                        act.wait_ge(ss_ready.sem, ss_ready.at(n, g))
                    act.copy(nsum[:], nr_ps[:]).then_inc(ns_copied.sem, 1)

                def exponentials(g, n=n):
                    act.wait_ge(s_less.sem, s_less.at(n, g + 1))
                    act.activation(sx[:, g % 2], sx[:, g % 2], ACT.Exp).then_inc(p_exp.sem, 1)

                def copy_probs(g, n=n):
                    act.wait_ge(t_ready.sem, t_ready.at(n, g + 1))
                    if g == 0:
                        act.wait_ge(u_ready.sem, u_ready.before(n))
                    act.copy(pt[:, :, 2 * g:2 * g + 2, :].rearrange("p w h q -> p h w q"),
                             st_ps[:].rearrange("p h (w q) -> p h w q", q=WIN)).then_inc(pt_done.sem, 1)

                def copy_tokens(r):
                    act.wait_ge(xtr_ready.sem, xtr_ready.at(n, r + 1))
                    if r == 0:
                        act.wait_ge(u_ready.sem, u_ready.before(n))
                    act.copy(xtok[:, 8 * r:8 * r + 8, :].rearrange("p w c -> p (w c)"), st_ps[:].rearrange("p b x -> p (b x)")).then_inc(xtok_done.sem, 1)

                def take_u(*ks):
                    for k in ks:
                        if k % 2 == 0:
                            if k < 4:
                                act.wait_ge(att_ready.sem, att_ready.before(m))
                            else:
                                act.wait_ge(att_ready.sem, att_ready.at(m, k // 2 - 1))
                        for z in range(2):
                            act.wait_ge(u_ready.sem, u_ready.at(m, 2 * k + z + 1))
                            act.copy(u[:].rearrange("p (h z) r w q -> p z r w h q", z=2)[:, z, k // 2 % 2, 2 * (k % 2):2 * (k % 2) + 2],
                                     ta_ps[:, z, :].rearrange("p (w h q) -> p w h q", w=2, q=WIN)).then_inc(u_copied.sem, 1)

                def copy_mvo():
                    for j in range(2):
                        for z in range(2):
                            act.wait_ge(mvo_ready.sem, mvo_ready.at(fresh, 2 * j + z + 1))
                            act.copy(mvo[:].rearrange("p (j h z) c -> p j z h c", j=2, z=2)[:, j, z],
                                     ta_ps[:, z, :].rearrange("p (h c) -> p h c", c=P)).then_inc(mvo_copied.sem, 1)

                def centred_squares():
                    act.wait_ge(xc_done.sem, xc_done.at(q, 1))
                    act.wait_ge(h_ready.sem, h_ready.before(q))
                    act.activation(csq[:], xc[:], ACT.Square).then_inc(csq_done.sem, 1)

                def add_bias():
                    act.wait_ge(xg_done.sem, xg_done.at(q, 1))
                    act.activation(csq[:], csq[:], ACT.Identity, bias=vec[:, V_BLN:V_BLN + 1]).then_inc(xn_done.sem, 1)

                def gates(c):
                    k, w = CHUNKS[c]
                    act.wait_ge(h_ready.sem, h_ready.at(q, 2 * c + 1))
                    if c == 0:
                        act.wait_ge(hid_done.sem, hid_done.before(q))
                    if c >= 2:
                        act.wait_ge(hid_done.sem, hid_done.at(q, c - 1))
                    act.activation(gate[0:w, c % 2, :], ta_ps[0:w, 1, :], ACT.Gelu, bias=vec[0:w, V_B1 + NC_ + c:V_B1 + NC_ + c + 1]).then_inc(gate_done.sem, 1)

                C_, T_, F_ = core is not None, tail is not None, ffn is not None
                if C_: tokens(); squares(0, 0)
                if F_: ffn_tokens()
                if C_: squares(0, 1)
                if T_: copy_probs(1, m); exponentials(2, m)
                if F_: centred_squares()
                if C_: squares(0, 2, 3); copy_sums(0)
                if F_: add_bias()
                if T_: copy_probs(2, m)
                if C_: squares(1, 0)
                if T_: exponentials(3, m)
                if F_: gates(0)
                if C_: squares(1, 1)
                if F_: gates(1)
                if C_: squares(1, 2)
                if F_: gates(2)
                if C_: squares(1, 3); copy_sums(1)
                if T_: copy_probs(3, m)
                if C_: squares(2, 0)
                if T_: take_u(0)
                if C_: squares(2, 1)
                if T_: take_u(1, 2, 3)
                if C_: squares(2, 2); exponentials(0); squares(2, 3); copy_sums(2)
                if T_: take_u(4, 5)
                if C_: squares(3, 0, 1)
                if T_: take_u(6)
                if C_: squares(3, 2); exponentials(1)
                if T_: take_u(7)
                if C_: squares(3, 3); copy_tokens(0); copy_sums(3); copy_tokens(1); copy_probs(0)
                if fresh is not None: copy_mvo()

            layers(act, body)

        @block.gpsimd
        def _(pool):
            for s in (rot_done, s_less, p_ready):
                pool.sem_inc(s.sem, s.per)

            def body(core, tail, ffn, fresh):
                n, place = core or (None, None)
                m, tail_place = tail or (None, None)
                q, ffn_place, layer = ffn or (None, None, None)

                def rotate(g, *tiles):
                    for i in tiles:
                        pool.wait_ge(prod_done.sem, prod_done.at(n, 8 * g + 4 * (i // 2) + 4))
                        if i < 2:
                            if g >= 2:
                                pool.wait_ge(s_ready.sem, s_ready.at(n, g - 1))
                            elif tail is not None:
                                pool.wait_ge(s_ready.sem, s_ready.at(m, g + 3))
                            dst = qr[:, i, :]
                            if g == 0:
                                pool.wait_ge(qp_loaded.sem, qp_loaded.before(n))
                            else:
                                pool.wait_ge(qp_loaded.sem, qp_loaded.at(n, 16 * 4 * g))
                        else:
                            if g == 0:
                                pool.wait_ge(kn_done.sem, kn_done.before(n))
                            else:
                                pool.wait_ge(kn_done.sem, kn_done.at(n, 2 * g))
                            dst = kr[:, i % 2, :]
                        k = 2 * i
                        pool.tensor_tensor(dst, prod[:, k, :], prod[:, k + 1, :], ALU.add if i % 2 else ALU.subtract).then_inc(rot_done.sem, 1)

                def less_max(g, n=n):
                    pool.wait_ge(s_max.sem, s_max.at(n, g + 1))
                    pool.tensor_tensor(sx[:, g % 2], sx[:, g % 2], smax[:, g % 2].unsqueeze(3).to_broadcast([P, T, 4, SPAN]),
                                       ALU.subtract).then_inc(s_less.sem, 1)

                def normal_probs(g, n=n):
                    pool.wait_ge(p_sum.sem, p_sum.at(n, 2 * g + 2))
                    pool.tensor_tensor(sx[:, g % 2], sx[:, g % 2], rsum[:, g % 2].unsqueeze(3).to_broadcast([P, T, 4, SPAN]),
                                       ALU.mult).then_inc(p_ready.sem, 1)

                C_, T_, F_ = core is not None, tail is not None, ffn is not None
                if C_: rotate(0, 0, 1)
                if T_: normal_probs(2, m)
                if C_: rotate(0, 2, 3)
                if T_: less_max(3, m)
                if C_: rotate(1, 0, 1)
                if T_: normal_probs(3, m)
                if C_: rotate(1, 2, 3); less_max(0); rotate(2, 0, 1); normal_probs(0); rotate(2, 2, 3)
                if C_: less_max(1); rotate(3, 0, 1); normal_probs(1); rotate(3, 2, 3); less_max(2)

            layers(pool, body)


def final_part(nc, sum_dram, ident_dram, X, out_dram):
    with ExitStack() as ctx:
        sb = lambda n, s: ctx.enter_context(nc.sbuf_tensor(n, s, F32))
        sem = lambda n: ctx.enter_context(nc.semaphore(n))
        part = sb("fi_part", [P, B * T, C])
        res = sb("fi_res", [P, B * T, C])
        ident = sb("fi_ident", [P, P])
        xt = sb("fi_xt", [P, 2, N])
        tr = ctx.enter_context(nc.psum_tensor("fi_tr", [P, 2, 512], F32))
        loaded, copied, transposed, added, stored = (sem("fi_" + n) for n in ("loaded", "copied", "transposed", "added", "stored"))
        block = ctx.enter_context(nc.Block())
        rows = lambda a: a.rearrange("b (t p) c -> p (b t) c", p=P)

        @block.sync
        def _(sp):
            sp.dma_start(part[:], rows(sum_dram)).then_inc(loaded, 16)
            sp.dma_start(ident[:], ident_dram).then_inc(loaded, 16)
            for b in range(B):
                sp.wait_ge(added, b + 1)
                sp.dma_start(rows(out_dram)[:, b * T:(b + 1) * T], res[:, b * T:(b + 1) * T]).then_inc(stored, 16)
            sp.wait_ge(stored, 16 * B)

        @block.scalar
        def _(act):
            for b in range(B):
                if b >= 2:
                    act.wait_ge(transposed, b - 1)
                act.copy(xt[:, b % 2, :], X[:, b, 1:1 + N]).then_inc(copied, 1)

        @block.tensor
        def _(pe):
            pe.wait_ge(loaded, 32)
            for b in range(B):
                pe.wait_ge(copied, b + 1)
                if b >= 2:
                    pe.wait_ge(added, b - 1)
                for t in range(T):
                    last = pe.transpose(tr[:, b % 2, t * P:(t + 1) * P], xt[:, b % 2, t * P:(t + 1) * P], ident[:])
                last.then_inc(transposed, 1)

        @block.vector
        def _(dve):
            dve.wait_ge(loaded, 32)
            for b in range(B):
                dve.wait_ge(transposed, b + 1)
                dve.tensor_tensor(res[:, b * T:(b + 1) * T].rearrange("p t c -> p (t c)"), tr[:, b % 2, :],
                                  part[:, b * T:(b + 1) * T].rearrange("p t c -> p (t c)"), ALU.add).then_inc(added, 1)


def program(nc, a):
    with nc.sbuf_tensor("x_all", [P, B, 1 + N], F32) as X:
        layernorm_part(nc, a["x"], a["ident"], X)
        global_attention_part(nc, a["x"], a["ga_w"], a["ga_rope"], a["ident"], X, a["sum"], a["ga_parts"], a["ga_maxes"])
        layers_part(nc, X, a)
        final_part(nc, a["sum"], a["ident"], X, a["out"])


def rope_tables():
    f = np.float32
    inv = np.power(f(10000.0), (f(-2.0) * np.arange(GD // 2, dtype=f) / f(GD)).astype(f)).astype(f)
    ang = np.arange(N, dtype=f)[:, None] * inv[None]
    cos, sin = (np.tile(np.repeat(g(ang), 2, axis=-1).T, (GH, 1)) for g in (np.cos, np.sin))
    sign = np.where(np.arange(P) % 2 == 0, -1, 1).astype(f)
    return np.ascontiguousarray(np.stack([cos, sin * sign[:, None]], axis=1).astype(f))


def rotation_tables():
    f = np.float32
    half = np.arange(0, LD, 2, dtype=f)
    t = np.arange(N, dtype=f)
    ang = t[:, None] * (f(1.0) / np.power(f(10000.0), half / f(LD))).astype(f)[None]
    scale = np.power(((half + f(0.4 * LD)) / f(1.4 * LD))[None], ((t - N // 2) / f(WIN // 2))[:, None]).astype(f)
    four = [f(8.0) * np.cos(ang) * scale, f(8.0) * np.sin(ang) * scale, np.cos(ang) / scale, np.sin(ang) / scale]
    return np.ascontiguousarray(np.stack([np.tile(a.T, (4, 1)) for a in four], axis=1).astype(f))


def score_mask():
    q = np.arange(P) % WIN
    k = np.arange(SPAN)
    seen = (q[:, None] <= k) & (k <= q[:, None] + WIN)
    first = (np.arange(P)[:, None] >= WIN) | (k[None] >= WIN)
    m = np.zeros((P, T, 4, SPAN), np.float32)
    m[:] = np.where(seen, 0, MASKED)[:, None, None]
    m[:, 0] = np.where(seen & first, 0, MASKED)[:, None]
    return m.reshape(P, 2, 512)


def constants():
    p = np.arange(P)
    pick = np.zeros((P, 8), np.float32)
    for r in p[p % 32 < 4]:
        pick[r, 4 * (r // 64) + r % 32] = 1
    return {
        "ident": np.eye(P, dtype=np.float32),
        "ones": np.full((P, P), 1.0 / C, np.float32),
        "heads": (p[:, None] // 32 == np.arange(32)[None] % 4).astype(np.float32),
        "pick": pick,
        "mask": score_mask(),
        "identb": np.eye(P, dtype=np.float32),
        "ga_rope": rope_tables(),
        "rot": rotation_tables(),
    }


def laid_out(i):
    a = {k: np.asarray(v) for k, v in i.items()}
    swap = np.arange(P) ^ 1
    wq, wk, wv = a["L0_attn_Wq"].T, a["L0_attn_Wk"].T, a["L0_attn_Wv"].T
    qkv = a["L0_ffn_Wqkv"].reshape(LAYERS, C, 3, LH, LD)
    qk = qkv[:, :, :2].reshape(LAYERS, C, 2, UNITS, 4, 2, HALF).transpose(0, 1, 3, 2, 5, 4, 6)
    pair = lambda m: m.reshape(LAYERS, LH // 2, P, C).transpose(0, 2, 1, 3)
    w2 = np.zeros((LAYERS, NC_, P, C), np.float32)
    vec = np.zeros((LAYERS, P, NVEC), np.float32)
    for c, (k, w) in enumerate(CHUNKS):
        w2[:, c, :w] = a["L0_ffn_W2"][:, k:k + w]
        for side in range(2):
            vec[:, :w, V_B1 + side * NC_ + c] = a["L0_ffn_b1"][:, side * HID + k:side * HID + k + w]
    gains = np.stack([np.tile(a["L0_ffn_" + name].reshape(LAYERS, 2, HALF)[:, half], (1, 4))
                      for name in ("q_scale", "k_scale") for half in range(2)], axis=2)
    vec[:, :, V_G], vec[:, :, V_BLN], vec[:, :, V_B2] = a["L0_ffn_ln_g"], a["L0_ffn_ln_b"], a["L0_ffn_b2"]
    return {
        "x": a["L0_attn_x"],
        "ga_w": np.stack([wq, wq[:, swap], wk, wk[:, swap], wv], axis=1),
        "wqk": qk.reshape(LAYERS, C, UNITS, 4, P),
        "wv": pair(qkv[:, :, 2].reshape(LAYERS, C, INNER).transpose(0, 2, 1)),
        "wo": pair(a["L0_ffn_Wo"]),
        "w1": a["L0_ffn_W1"],
        "w2": w2.transpose(0, 2, 1, 3),
        "vec": vec,
        "gains": gains,
    }


def kernel(**inputs):
    import ml_dtypes
    import concourse.bacc as bacc
    from concourse.bass_utils import run_bass_kernel_spmd

    nc = bacc.Bacc("TRN2", target_bir_lowering=False, num_devices=1)
    arrays = {**laid_out(inputs), **constants()}
    for n in ("mask", "identb"):
        arrays[n] = arrays[n].astype(ml_dtypes.bfloat16)
    arrays = {n: np.ascontiguousarray(v) for n, v in arrays.items()}
    aps = {n: nc.dram_tensor("in_" + n, v.shape, mybir.dt.from_np(v.dtype), kind="ExternalInput").ap() for n, v in arrays.items()}
    for n, shape, dt, kind in (("sum", (B, N, C), F32, "Internal"), ("ga_parts", (B, P, 2, 3, N), BF16, "Internal"),
                               ("ga_maxes", (B, GH * T, 3, P), BF16, "Internal"), ("out", (B, N, C), F32, "ExternalOutput")):
        aps[n] = nc.dram_tensor(n + "_dram", shape, dt, kind=kind).ap()
    program(nc, aps)
    r = run_bass_kernel_spmd(nc, [{"in_" + n: v for n, v in arrays.items()}], core_ids=[0])
    return r.results[0]["out_dram"]
```

```python
from contextlib import ExitStack

import numpy as np
import concourse.bass as bass
from concourse import mybir

F32 = mybir.dt.float32
BF16 = mybir.dt.bfloat16
I32 = mybir.dt.int32
ALU = mybir.AluOpType
ACT = mybir.ActivationFunctionType
AX = mybir.AxisListType

P = 128
B, N, C = 8, 512, 128
T = N // P
EPS = 1e-5

GH, GD = 16, 8
GROUPS = 4
TERMS = ((0, 0), (0, 1), (1, 0), (1, 1), (0, 2), (2, 0))
KROWS = len(TERMS) * GD
FIRST = 6
AROWS = KROWS + 3

RSQRT_MAGIC = float(0x5F3759DF)


class Signal:

    def __init__(self, sem, per):
        self.sem, self.per = sem, per

    def at(self, batch, n):
        assert 1 <= n <= self.per
        return batch * self.per + self.per + n

    def before(self, batch):
        return batch * self.per + self.per


def rsqrt(eng, y, x, t, steps, batch, n):
    eng.tensor_scalar(y.bitcast(I32), x.bitcast(I32), -0.5, RSQRT_MAGIC, ALU.mult, ALU.add).then_inc(steps.sem, 1)
    for i in range(3):
        eng.wait_ge(steps.sem, steps.at(batch, n + 3 * i + 1))
        eng.tensor_tensor(t, y, y, ALU.mult).then_inc(steps.sem, 1)
        eng.wait_ge(steps.sem, steps.at(batch, n + 3 * i + 2))
        eng.scalar_tensor_tensor(t, t, -0.5, x, ALU.mult, ALU.mult).then_inc(steps.sem, 1)
        eng.wait_ge(steps.sem, steps.at(batch, n + 3 * i + 3))
        eng.scalar_tensor_tensor(y, t, 1.5, y, ALU.add, ALU.mult).then_inc(steps.sem, 1)
    eng.wait_ge(steps.sem, steps.at(batch, n + RSQRT_LINKS))


RSQRT_LINKS = 10
NORM_LINKS = RSQRT_LINKS + 2


def layernorm_part(nc, x_dram, ident_dram, X):
    with ExitStack() as ctx:
        sb = lambda n, s, d=F32: ctx.enter_context(nc.sbuf_tensor(n, s, d))
        sem = lambda n: ctx.enter_context(nc.semaphore(n))
        xt = sb("ln_xt", [P, B * T, C])
        xn = sb("ln_xn", [P, B * T, C])
        ident = sb("ln_ident", [P, P])
        stats = sb("ln_stats", [P, B * T, 6])
        mv = sb("ln_mv", [P, B * T, 2])
        var = sb("ln_var", [P, B * T])
        rstd = sb("ln_rstd", [P, B * T])
        tmp = sb("ln_tmp", [P, B * T])
        tr = ctx.enter_context(nc.psum_tensor("ln_tr", [P, 2, 512], F32))
        loaded, ident_loaded, normed, transposed, copied = (
            sem(n) for n in ("ln_loaded", "ln_ident_loaded", "ln_normed", "ln_transposed", "ln_copied"))
        chain = Signal(sem("ln_chain"), 3 + RSQRT_LINKS)
        block = ctx.enter_context(nc.Block())

        @block.sync
        def _(sp):
            sp.dma_start(xt[:], x_dram.rearrange("b (t p) c -> p (b t) c", p=P)).then_inc(loaded, 16)
            sp.dma_start(ident[:], ident_dram).then_inc(ident_loaded, 16)

        @block.vector
        def _(dve):
            dve.sem_inc(chain.sem, chain.per)
            dve.wait_ge(loaded, 16)
            for i in range(B * T):
                last = dve.bn_stats(stats[:, i, :], xt[:, i, :])
            last.then_inc(chain.sem, 1)
            dve.wait_ge(chain.sem, chain.at(0, 1))
            for i in range(B * T):
                last = dve.bn_aggr(mv[:, i, :], stats[:, i, :])
            last.then_inc(chain.sem, 1)
            dve.wait_ge(chain.sem, chain.at(0, 2))
            dve.tensor_scalar(var[:], mv[:, :, 1], EPS, None, ALU.add).then_inc(chain.sem, 1)
            dve.wait_ge(chain.sem, chain.at(0, 3))
            rsqrt(dve, rstd[:], var[:], tmp[:], chain, 0, 3)
            for i in range(B * T):
                dve.tensor_scalar(xn[:, i, :], xt[:, i, :], mv[:, i, 0:1], rstd[:, i:i + 1],
                                  ALU.subtract, ALU.mult).then_inc(normed, 1)

        @block.tensor
        def _(pe):
            pe.wait_ge(ident_loaded, 16)
            for b in range(B):
                pe.wait_ge(normed, T * (b + 1))
                if b >= 2:
                    pe.wait_ge(copied, b - 1)
                for t in range(T):
                    last = pe.transpose(tr[:, b % 2, t * P:(t + 1) * P], xn[:, b * T + t, :], ident[:])
                last.then_inc(transposed, 1)

        @block.scalar
        def _(act):
            for b in range(B):
                act.wait_ge(transposed, b + 1)
                act.copy(X[:, b, 1:1 + N], tr[:, b % 2, :]).then_inc(copied, 1)

        @block.gpsimd
        def _(pool):
            pool.memset(X[:, :, 0:1], 0.0)


def global_attention_part(nc, x_dram, w_dram, rope_dram, ident_dram, X, sum_dram, parts_dram, maxes_dram):
    with ExitStack() as ctx:
        sb = lambda n, s, d=F32: ctx.enter_context(nc.sbuf_tensor(n, s, d))
        ps = lambda n, s, d=F32: ctx.enter_context(nc.psum_tensor(n, s, d))
        sem = lambda n: ctx.enter_context(nc.semaphore(n))
        signal = lambda n, per: Signal(sem(n), per)
        w = sb("ga_w", [P, 5, P])
        rope = sb("ga_rope", [P, 2, N])
        ident = sb("ga_ident", [P, P])
        xa = sb("ga_xa", [P, N])
        prod = sb("ga_prod", [P, 4, N])
        full = sb("ga_full", [P, 2, 3, N])
        parts = sb("ga_parts", [P, 2, 3, N], BF16)
        qs = sb("ga_qs", [P, 2, GH // 2, N], BF16)
        ks = sb("ga_ks", [P, 2, GH // 2, N], BF16)
        va = sb("ga_va", [P, 2, T, GH, 32])
        mx = sb("ga_mx", [P, GH * T])
        mfull = sb("ga_mfull", [GH * T, 3, P])
        mparts = sb("ga_mparts", [GH * T, 3, P], BF16)
        pt = sb("ga_pt", [P, 8, 2, N])
        os = sb("ga_os", [P, 2, N])
        rec = sb("ga_rec", [P, T, 4])
        xraw = sb("ga_xraw", [P, T, C])
        y = sb("ga_y", [P, T, C])
        f_ps = ps("ga_f_ps", [P, 2, N])
        s_ps = ps("ga_s_ps", [P, 4, N])
        pv_ps = ps("ga_pv_ps", [P, N])
        aux_ps = ps("ga_aux_ps", [P, N])
        consts, init = sem("ga_consts"), sem("ga_init")
        xa_ready = signal("ga_xa_ready", 1)
        proj_ready = signal("ga_proj_ready", 5)
        prod_done = signal("ga_prod_done", 4)
        v_ready = signal("ga_v_ready", 1)
        full_ready = signal("ga_full_ready", 6)
        parts_ready = signal("ga_parts_ready", 6)
        parts_out = [signal(f"ga_{n}_parts_out", 16) for n in "qk"]
        stacked = signal("ga_stacked", 16 * 4 * len(TERMS))
        s_ready = signal("ga_s_ready", 64)
        max_done = signal("ga_max_done", 64)
        mt_ready = signal("ga_mt_ready", 1)
        m_steps = signal("ga_m_steps", 6)
        m_out = signal("ga_m_out", 16)
        m_rows = [signal(f"ga_m_rows_{n}", 32) for n in ("first", "rest")]
        st_ready = signal("ga_st_ready", 32)
        exp_done = signal("ga_exp_done", 32)
        pv_done = signal("ga_pv_done", 16)
        os_ready = signal("ga_os_ready", 4)
        ot_ready = signal("ga_ot_ready", 4)
        out_steps = signal("ga_out_steps", 8)
        x_loaded = signal("ga_x_loaded", 16)
        y_ready = signal("ga_y_ready", 1)
        stored = signal("ga_stored", 16)
        block = ctx.enter_context(nc.Block())

        def place(h):
            return 64 * (h % 2), h // 2

        def batches(eng, body):
            body(0, 0, None, None)
            with eng.Fori(0, B // 2 - 1) as i:
                body(2 * i + 1, 1, 2 * i, 0)
                body(2 * i + 2, 0, 2 * i + 1, 1)
            body(B - 1, 1, B - 2, 0)
            body(None, None, B - 1, 1)

        @block.sync
        def _(sp):
            for s in (*parts_out, stacked, m_out, *m_rows, x_loaded, stored):
                sp.sem_inc(s.sem, s.per)
            sp.dma_start(w[:], w_dram).then_inc(consts, 16)
            sp.dma_start(rope[:], rope_dram).then_inc(consts, 16)
            sp.dma_start(ident[:], ident_dram).then_inc(consts, 16)
            sp.wait_ge(init, 3)

            def body(n, slot, b, old):
                if b is not None:
                    sp.wait_ge(y_ready.sem, y_ready.before(b))
                    sp.dma_start(xraw[:], x_dram[bass.ds(b, 1)].rearrange("o (t p) c -> p (o t) c", p=P)).then_inc(x_loaded.sem, 16)
                if n is not None:
                    for a in range(2):
                        sp.wait_ge(parts_ready.sem, parts_ready.at(n, 3 * a + 3))
                        sp.dma_start(parts_dram[bass.ds(n, 1), :, a].rearrange("o p c n -> (o p) c n"), parts[:, a]).then_inc(parts_out[a].sem, 16)
                    if b is not None:
                        sp.wait_ge(st_ready.sem, st_ready.before(b))
                    for a, dst in ((0, qs), (1, ks)):
                        sp.wait_ge(parts_out[a].sem, parts_out[a].at(n, 16))
                        for z in range(2):
                            for j, term in enumerate(TERMS):
                                at = 64 * z + GD * j
                                src = parts_dram[bass.ds(n, 1), :, a, term[a]].rearrange("o (hp z d) n -> z d (o hp) n", z=2, d=GD)
                                sp.dma_start(dst[at:at + GD, slot], src[z]).then_inc(stacked.sem, 16)
                    sp.wait_ge(m_steps.sem, m_steps.at(n, 6))
                    sp.dma_start(maxes_dram[bass.ds(n, 1)].rearrange("o c r n -> (o r) c n"), mparts[:]).then_inc(m_out.sem, 16)
                    sp.wait_ge(m_out.sem, m_out.at(n, 16))
                    src = maxes_dram[bass.ds(n, 1)].rearrange("o c (hp z t) n -> z c (o hp) (t n)", z=2, t=T)
                    for part, heads in enumerate((slice(0, 2), slice(2, GH // 2))):
                        for z in range(2):
                            sp.dma_start(qs[64 * z + KROWS:64 * z + AROWS, slot, heads], src[z][:, heads]).then_inc(m_rows[part].sem, 16)
                if b is not None:
                    sp.wait_ge(y_ready.sem, y_ready.at(b, 1))
                    sp.dma_start(sum_dram[bass.ds(b, 1)].rearrange("o (t p) c -> p (o t) c", p=P), y[:]).then_inc(stored.sem, 16)

            batches(sp, body)
            sp.wait_ge(stored.sem, stored.before(B))

        @block.tensor
        def _(pe):
            for s in (proj_ready, s_ready, mt_ready, st_ready, pv_done, ot_ready):
                pe.sem_inc(s.sem, s.per)
            pe.wait_ge(consts, 48)

            def body(n, slot, b, old):
                def projections():
                    pe.wait_ge(xa_ready.sem, xa_ready.at(n, 1))
                    pe.wait_ge(max_done.sem, max_done.before(n))
                    for i in range(4):
                        if i >= 2:
                            pe.wait_ge(prod_done.sem, prod_done.at(n, i - 1))
                        pe.matmul(f_ps[:, i % 2, :], w[:, i, :], xa[:], start=True, stop=True).then_inc(proj_ready.sem, 1)
                    if b is not None:
                        pe.wait_ge(m_steps.sem, m_steps.at(b, 1))
                    for t in range(T):
                        last = pe.matmul(aux_ps[:, t * P:(t + 1) * P], xa[:, t * P:(t + 1) * P], w[:, 4, :], start=True, stop=True)
                    last.then_inc(proj_ready.sem, 1)

                def first(i):
                    z, hp = place(i // T)
                    t = i % T
                    if i == 0:
                        pe.wait_ge(stacked.sem, stacked.at(n, stacked.per))
                        pe.wait_ge(prod_done.sem, prod_done.at(n, 4))
                    if i >= 2:
                        pe.wait_ge(max_done.sem, max_done.at(n, i - 1))
                    pe.matmul(f_ps[:, i % 2, :], qs[z:z + KROWS, slot, hp, t * P:(t + 1) * P], ks[z:z + KROWS, slot, hp, :],
                              start=True, stop=True).then_inc(s_ready.sem, 1)

                def transposed_maxima():
                    pe.wait_ge(max_done.sem, max_done.at(n, 64))
                    if b is None:
                        pe.wait_ge(v_ready.sem, v_ready.at(n, 1))
                    else:
                        pe.wait_ge(out_steps.sem, out_steps.at(b, 8))
                    pe.matmul(aux_ps[0:GH * T, 0:P], mx[:], ident[:], start=True, stop=True).then_inc(mt_ready.sem, 1)

                def second(q, c):
                    z, hp = place(4 * (q // T) + c)
                    kt, pair = q % T, 2 * q + c // 2
                    if q == 0 and c == 0:
                        pe.wait_ge(m_rows[0].sem, m_rows[0].at(b, 32))
                    if q == T and c == 0:
                        pe.wait_ge(m_rows[1].sem, m_rows[1].at(b, 32))
                    if c % 2 == 0:
                        if pair < 2:
                            pe.wait_ge(exp_done.sem, exp_done.before(b))
                        else:
                            pe.wait_ge(exp_done.sem, exp_done.at(b, pair - 1))
                    mm = pe.matmul(s_ps[:, 2 * (pair % 2) + c % 2, :], ks[z:z + AROWS, old, hp, kt * P:(kt + 1) * P],
                                   qs[z:z + AROWS, old, hp, :], start=True, stop=True)
                    if c % 2 == 1:
                        mm.then_inc(st_ready.sem, 1)

                def pv(q, c):
                    j, kt = q // T, q % T
                    if c == 0:
                        pe.wait_ge(exp_done.sem, exp_done.at(b, 2 * q + 2))
                        if q == 0:
                            pe.wait_ge(v_ready.sem, v_ready.at(b, 1))
                            pe.wait_ge(os_ready.sem, os_ready.before(b))
                        elif kt == 0:
                            pe.wait_ge(os_ready.sem, os_ready.at(b, j))
                    mm = pe.matmul(pv_ps[32 * c:32 * c + 32, :], va[:, old, kt, 4 * j + c, :], pt[:, (2 * q + c // 2) % 8, c % 2, :],
                                   start=(kt == 0), stop=(kt == T - 1), skip_group_check=True)
                    if c == 3:
                        mm.then_inc(pv_done.sem, 1)

                def out(j):
                    pe.wait_ge(os_ready.sem, os_ready.at(b, j + 1))
                    if j:
                        pe.wait_ge(out_steps.sem, out_steps.at(b, 2 * j))
                    elif n is not None:
                        pe.wait_ge(v_ready.sem, v_ready.at(n, 1))
                    else:
                        pe.wait_ge(m_steps.sem, m_steps.at(b, 1))
                    for t in range(T):
                        last = pe.transpose(aux_ps[:, t * P:(t + 1) * P], os[:, j % 2, t * P:(t + 1) * P], ident[:])
                    last.then_inc(ot_ready.sem, 1)

                if n is not None:
                    projections()
                if b is None:
                    for i in range(GH * T):
                        first(i)
                else:
                    for q in range(16):
                        for c in range(4):
                            i = 2 * 4 * (q - FIRST) + 2 * c
                            front = n is not None and 0 <= i < GH * T
                            if front: first(i)
                            second(q, c)
                            if front: first(i + 1)
                            if q >= 1:
                                pv(q - 1, c)
                        if q >= 5 and q % 4 == 1:
                            out(q // 4 - 1)
                    for c in range(4):
                        pv(15, c)
                    out(3)
                if n is not None:
                    transposed_maxima()

            batches(pe, body)

        @block.vector
        def _(dve):
            for s in (prod_done, max_done, m_steps, out_steps):
                dve.sem_inc(s.sem, s.per)
            dve.memset(va[:], 0.0).then_inc(init, 1)
            dve.memset(ks[:], 1.0).then_inc(init, 1)
            dve.wait_ge(init, 2)
            dve.memset(va[:, :, :, :, GD:GD + 1], 1.0).then_inc(init, 1)
            dve.wait_ge(consts, 48)

            def body(n, slot, b, old):
                def products():
                    dve.wait_ge(full_ready.sem, full_ready.before(n))
                    for i in range(4):
                        dve.wait_ge(proj_ready.sem, proj_ready.at(n, i + 1))
                        dve.tensor_tensor(prod[:, i, :], f_ps[:, i % 2, :], rope[:, i % 2, :], ALU.mult).then_inc(prod_done.sem, 1)
                    dve.wait_ge(mt_ready.sem, mt_ready.before(n))

                def maxima(step):
                    for i in range(8 * step, 8 * step + 8):
                        dve.wait_ge(s_ready.sem, s_ready.at(n, i + 1))
                        dve.tensor_reduce(mx[:, i:i + 1], f_ps[:, i % 2, :], AX.X, ALU.max).then_inc(max_done.sem, 1)

                def cut_maxima():
                    dve.wait_ge(mt_ready.sem, mt_ready.at(n, 1))
                    dve.wait_ge(m_out.sem, m_out.before(n))
                    dve.tensor_scalar(mfull[:, 0, :], aux_ps[0:GH * T, 0:P], -1.0, None, ALU.mult).then_inc(m_steps.sem, 1)
                    for c in range(3):
                        dve.wait_ge(m_steps.sem, m_steps.at(n, 2 * c + 1))
                        dve.tensor_copy(mparts[:, c, :], mfull[:, c, :]).then_inc(m_steps.sem, 1)
                        if c < 2:
                            dve.wait_ge(m_steps.sem, m_steps.at(n, 2 * c + 2))
                            dve.tensor_tensor(mfull[:, c + 1, :], mfull[:, c, :], mparts[:, c, :], ALU.subtract).then_inc(m_steps.sem, 1)

                def output(j):
                    if j == 0:
                        dve.wait_ge(y_ready.sem, y_ready.before(b))
                        dve.wait_ge(stored.sem, stored.before(b))
                    dve.wait_ge(ot_ready.sem, ot_ready.at(b, j + 1))
                    o = aux_ps[:].rearrange("p (t c e) -> p t c e", t=T, c=4)
                    if j:
                        dve.wait_ge(out_steps.sem, out_steps.at(b, 2 * j))
                    dve.reciprocal(rec[:], o[:, :, :, GD]).then_inc(out_steps.sem, 1)
                    dve.wait_ge(out_steps.sem, out_steps.at(b, 2 * j + 1))
                    dve.tensor_tensor(y[:, :, 32 * j:32 * j + 32].rearrange("p t (c d) -> p t c d", d=GD), o[:, :, :, 0:GD],
                                      rec[:].unsqueeze(3).to_broadcast([P, T, 4, GD]), ALU.mult).then_inc(out_steps.sem, 1)

                if n is not None:
                    products()
                if b is not None:
                    output(0)
                for step in range(8):
                    if n is not None:
                        maxima(step)
                    if b is not None and FIRST + step == 10:
                        output(1)
                if b is not None:
                    output(2)
                    output(3)
                if n is not None:
                    cut_maxima()

            batches(dve, body)

        @block.scalar
        def _(act):
            for s in (parts_ready, v_ready, exp_done, os_ready):
                act.sem_inc(s.sem, s.per)
            act.wait_ge(init, 3)

            def body(n, slot, b, old):
                def cut(a, c):
                    if n is None:
                        return
                    if c == 0:
                        act.wait_ge(parts_out[a].sem, parts_out[a].before(n))
                    act.wait_ge(full_ready.sem, full_ready.at(n, 3 * a + c + 1))
                    act.copy(parts[:, a, c, :], full[:, a, c, :]).then_inc(parts_ready.sem, 1)

                def copy_v():
                    if n is None:
                        return
                    if b is not None:
                        act.wait_ge(pv_done.sem, pv_done.before(b))
                    act.wait_ge(proj_ready.sem, proj_ready.at(n, 5))
                    act.copy(va[:, slot, :, :, 0:GD], aux_ps[:].rearrange("p (t h d) -> p t h d", t=T, h=GH)).then_inc(v_ready.sem, 1)

                def take(j):
                    act.wait_ge(pv_done.sem, pv_done.at(b, 4 * j + 4))
                    if j >= 2:
                        act.wait_ge(ot_ready.sem, ot_ready.at(b, j - 1))
                    else:
                        act.wait_ge(ot_ready.sem, ot_ready.before(b))
                    act.copy(os[:, j % 2, :], pv_ps[:]).then_inc(os_ready.sem, 1)

                def exponentials(*pairs):
                    if b is None:
                        return
                    for pair in pairs:
                        act.wait_ge(st_ready.sem, st_ready.at(b, pair + 1))
                        if pair >= 8 and pair % 2 == 0:
                            act.wait_ge(pv_done.sem, pv_done.at(b, pair // 2 - 3))
                        if pair < 8 and pair % 2 == 0:
                            act.wait_ge(pv_done.sem, pv_done.before(b))
                        act.activation(pt[:, pair % 8], s_ps[:, 2 * (pair % 2):2 * (pair % 2) + 2, :], ACT.Exp,
                                       scale=float(GD) ** -0.5).then_inc(exp_done.sem, 1)
                        if pair >= 9 and pair % 8 == 1:
                            take(pair // 8 - 1)

                cut(0, 0); cut(0, 1); copy_v(); cut(0, 2)
                exponentials(0, 1)
                cut(1, 0)
                exponentials(2)
                cut(1, 1)
                exponentials(3)
                cut(1, 2)
                exponentials(*range(4, 32))
                if b is not None:
                    take(3)

            batches(act, body)

        @block.gpsimd
        def _(pool):
            for s in (xa_ready, full_ready, y_ready):
                pool.sem_inc(s.sem, s.per)

            def body(n, slot, b, old):
                def take_x(n):
                    pool.wait_ge(proj_ready.sem, proj_ready.before(n))
                    pool.tensor_copy(xa[:], X[:, bass.ds(n, 1), 1:1 + N].rearrange("p o n -> p (o n)")).then_inc(xa_ready.sem, 1)

                if b is None:
                    take_x(0)
                if n is not None:
                    pool.wait_ge(parts_ready.sem, parts_ready.before(n))
                    for a in range(2):
                        pool.wait_ge(prod_done.sem, prod_done.at(n, 2 * a + 2))
                        pool.tensor_tensor(full[:, a, 0, :], prod[:, 2 * a, :], prod[:, 2 * a + 1, :], ALU.add).then_inc(full_ready.sem, 1)
                        for c in range(2):
                            pool.wait_ge(full_ready.sem, full_ready.at(n, 3 * a + c + 1))
                            pool.wait_ge(parts_ready.sem, parts_ready.at(n, 3 * a + c + 1))
                            pool.tensor_tensor(full[:, a, c + 1, :], full[:, a, c, :], parts[:, a, c, :], ALU.subtract).then_inc(full_ready.sem, 1)
                if n is not None and not (isinstance(n, int) and n == B - 1):
                    take_x(n + 1)
                if b is not None:
                    pool.wait_ge(x_loaded.sem, x_loaded.at(b, 16))
                    pool.wait_ge(out_steps.sem, out_steps.at(b, 8))
                    pool.tensor_tensor(y[:], y[:], xraw[:], ALU.add).then_inc(y_ready.sem, 1)

            batches(pool, body)


LAYERS = 6
LH, LD = 16, 64
HALF = LD // 2
INNER = LH * LD
WIN = 32
NW = N // WIN
SPAN = 2 * WIN
HID = C * 4 * 2 // 3
CHUNKS = tuple((k, min(P, HID - k)) for k in range(0, HID, P))
NC_ = len(CHUNKS)
MASKED = -1e30
TINY = 1e-24
V_G, V_BLN, V_B1, V_B2, NVEC = 0, 1, 2, 2 + 2 * NC_, 3 + 2 * NC_
UNITS = 4


def layers_part(nc, X, d):
    with ExitStack() as ctx:
        sb = lambda n, s, dt=F32: ctx.enter_context(nc.sbuf_tensor(n, s, dt))
        ps = lambda n, s, dt=F32: ctx.enter_context(nc.psum_tensor(n, s, dt))
        sem = lambda n: ctx.enter_context(nc.semaphore("ly_" + n))
        signal = lambda n, per: Signal(sem(n), per)

        wqk = sb("ly_wqk", [P, UNITS, 4, P])
        mvo = sb("ly_mvo", [P, LH, P])
        wv_raw = sb("ly_wv", [P, LH // 2, P])
        wo_raw = sb("ly_wo", [P, LH // 2, P])
        gains = sb("ly_gains", [P, 4])
        w1 = sb("ly_w1", [P, 2 * HID])
        w2 = sb("ly_w2", [P, NC_, P])
        vec = sb("ly_vec", [P, NVEC])
        rot = sb("ly_rot", [P, 8, N])
        ident = sb("ly_ident", [P, P])
        ones = sb("ly_ones", [P, P])
        heads = sb("ly_heads", [P, 32])
        pick = sb("ly_pick", [P, 8])
        mask = sb("ly_mask", [P, 2, 512], BF16)
        identb = sb("ly_identb", [P, P], BF16)
        tables = sb("ly_tables", [P, 4, N])
        xs = sb("ly_xs", [P, WIN + N])
        prod = sb("ly_prod", [P, 8, N])
        sq = sb("ly_sq", [P, 4, N])
        nsum = sb("ly_nsum", [P, N])
        ss = sb("ly_ss", [P, T, 8])
        rn = sb("ly_rn", [P, 2, T, 8])
        rt = sb("ly_rt", [P, T, 8])
        rnx = sb("ly_rnx", [P, T, 4, HALF])
        qr = sb("ly_qr", [P, 2, N])
        qp = sb("ly_qp", [P, 2, 2, N])
        kr = sb("ly_kr", [P, 2, N])
        kn = sb("ly_kn", [P, 2, N])
        kbd = sb("ly_kbd", [P, 2, 2, WIN + N])
        sx = sb("ly_sx", [P, 2, T, 4, SPAN])
        smax = sb("ly_smax", [P, 2, T, 4])
        rsum = sb("ly_rsum", [P, 2, T, 4])
        pt = sb("ly_pt", [P, NW, LH // 2, WIN])
        xtok = sb("ly_xtok", [P, NW, P])
        u = sb("ly_u", [P, LH, 2, 4, WIN])
        xf = sb("ly_xf", [P, N])
        xc = sb("ly_xc", [P, N])
        csq = sb("ly_csq", [P, N])
        rstd = sb("ly_rstd", [P, 3, T])
        gate = sb("ly_gate", [P, 2, N])
        hid = sb("ly_hid", [P, NC_, N])

        pj_ps = ps("ly_pj_ps", [P, 2, N])
        nr_ps = ps("ly_nr_ps", [P, N])
        st_ps = ps("ly_st_ps", [P, 2, 512])
        ta_ps = ps("ly_ta_ps", [P, 2, 512])
        to_ps = ps("ly_to_ps", [P, 512])

        consts, init = sem("consts"), sem("init")
        core_loaded = signal("core_loaded", 16 * 2)
        raw_loaded = signal("raw_loaded", 16 * 2)
        tail_loaded = signal("tail_loaded", 16 * 3)
        rot_ready = signal("rot_ready", 8)
        mvo_ready = signal("mvo_ready", 4)
        mvo_copied = signal("mvo_copied", 4)
        xs_ready = signal("xs_ready", 2)
        proj_ready = signal("proj_ready", 16)
        sq_done = signal("sq_done", 16)
        prod_done = signal("prod_done", 32)
        rot_done = signal("rot_done", 16)
        ns_ready = signal("ns_ready", 4)
        ns_copied = signal("ns_copied", 4)
        ss_ready = signal("ss_ready", 4)
        rn_steps = signal("rn_steps", 4 * NORM_LINKS)
        r_ready = signal("r_ready", 4)
        kn_done = signal("kn_done", 8)
        kbd_loaded = signal("kbd_loaded", 16 * 8 * 4)
        qp_loaded = signal("qp_loaded", 16 * 4 * 4)
        s_ready = signal("s_ready", 4)
        s_scaled = signal("s_scaled", 4)
        s_max = signal("s_max", 4)
        s_less = signal("s_less", 4)
        p_exp = signal("p_exp", 4)
        p_sum = signal("p_sum", 8)
        p_ready = signal("p_ready", 4)
        t_ready = signal("t_ready", 4)
        pt_done = signal("pt_done", 4)
        xtr_ready = signal("xtr_ready", 2)
        xtok_done = signal("xtok_done", 2)
        u_ready = signal("u_ready", 16)
        u_copied = signal("u_copied", 16)
        att_ready = signal("att_ready", 4)
        x1_done = signal("x1_done", 1)
        xf_done = signal("xf_done", 2)
        mean_ready = signal("mean_ready", 1)
        xc_done = signal("xc_done", 1)
        csq_done = signal("csq_done", 1)
        var_ready = signal("var_ready", 1)
        var_steps = signal("var_steps", 1 + RSQRT_LINKS)
        rb_ready = signal("rb_ready", 1)
        xg_done = signal("xg_done", 1)
        xn_done = signal("xn_done", 1)
        h_ready = signal("h_ready", 2 * NC_)
        gate_done = signal("gate_done", NC_)
        hid_done = signal("hid_done", NC_)
        ffn_ready = signal("ffn_ready", 1)
        x2_done = signal("x2_done", 1)
        block = ctx.enter_context(nc.Block())

        def layers(eng, body, new_layer=lambda layer: None, old_layer=lambda layer: None):
            last = LAYERS - 1

            def middle(layer):
                with eng.Fori(2, B) as b:
                    n = layer * B + b
                    body((n, b), (n - 1, b - 1), (n - 2, b - 2, layer), None)

            new_layer(0)
            body((0, 0), None, None, 0)
            body((1, 1), (0, 0), None, None)
            with eng.Fori(0, last) as layer:
                middle(layer)
                n = layer * B + B
                new_layer(layer + 1)
                body((n, 0), (n - 1, B - 1), (n - 2, B - 2, layer), layer + 1)
                body((n + 1, 1), (n, 0), (n - 1, B - 1, layer), None)
                old_layer(layer)
            middle(last)
            n = LAYERS * B
            body(None, (n - 1, B - 1), (n - 2, B - 2, last), None)
            body(None, None, (n - 1, B - 1, last), None)

        def unit_tables(i):
            k, upper = i // 2, i % 2
            return ((4 * k + 1, 4 * k + 1), (4 * k + 2, 4 * k + 2)) if upper else ((4 * k, 4 * k), (4 * k + 3, 4 * k + 3))

        @block.sync
        def _(sp):
            for s in (core_loaded, raw_loaded, tail_loaded, kbd_loaded, qp_loaded):
                sp.sem_inc(s.sem, s.per)
            one = lambda a, layer: a[bass.ds(layer, 1)] if not isinstance(layer, int) else a[layer:layer + 1]

            def load_core(layer):
                sp.dma_start(wqk[:], one(d["wqk"], layer).rearrange("o p u i c -> p (o u) i c")).then_inc(core_loaded.sem, 16)
                sp.dma_start(gains[:], one(d["gains"], layer).rearrange("o p c -> p (o c)")).then_inc(core_loaded.sem, 16)

            def load_raw(layer):
                sp.dma_start(wv_raw[:], one(d["wv"], layer).rearrange("o p h c -> p (o h) c")).then_inc(raw_loaded.sem, 16)
                sp.dma_start(wo_raw[:], one(d["wo"], layer).rearrange("o p h c -> p (o h) c")).then_inc(raw_loaded.sem, 16)

            def load_tail(layer):
                sp.dma_start(w1[:], one(d["w1"], layer).rearrange("o p c -> p (o c)")).then_inc(tail_loaded.sem, 16)
                sp.dma_start(w2[:], one(d["w2"], layer).rearrange("o p h c -> p (o h) c")).then_inc(tail_loaded.sem, 16)
                sp.dma_start(vec[:], one(d["vec"], layer).rearrange("o p c -> p (o c)")).then_inc(tail_loaded.sem, 16)

            load_core(0)
            for dst, src in ((tables, d["rot"]), (ident, d["ident"]), (heads, d["heads"]), (pick, d["pick"]), (ones, d["ones"]),
                             (mask, d["mask"]), (identb, d["identb"])):
                sp.dma_start(dst[:], src).then_inc(consts, 16)
            load_raw(0)
            load_tail(0)
            sp.wait_ge(init, 2)

            def new_layer(layer):
                if isinstance(layer, int) and layer == 0:
                    return
                sp.wait_ge(proj_ready.sem, proj_ready.at(layer * B - 1, proj_ready.per))
                load_core(layer)
                load_raw(layer)

            def old_layer(layer):
                sp.wait_ge(x2_done.sem, x2_done.before(layer * B + B))
                load_tail(layer + 1)

            def body(core, tail, ffn, fresh):
                if core is None:
                    return
                n, _ = core
                for g in range(UNITS):
                    sp.wait_ge(rot_done.sem, rot_done.at(n, 4 * g + 2))
                    for p in range(2):
                        for half in range(2):
                            sp.dma_start(qp[64 * half:64 * half + 64, g % 2, p], qr[64 * p:64 * p + 64, half]).then_inc(qp_loaded.sem, 16)
                    sp.wait_ge(kn_done.sem, kn_done.at(n, 2 * g + 2))
                    for p in range(2):
                        for z in range(2):
                            for half in range(2):
                                src, dst = 64 * p + 32 * z, 64 * half + 32 * z
                                sp.dma_start(kbd[dst:dst + 32, p, z, WIN:], kn[src:src + 32, half]).then_inc(kbd_loaded.sem, 16)

            layers(sp, body, new_layer, old_layer)

        @block.tensor
        def _(pe):
            for s in (mvo_ready, proj_ready, ns_ready, ss_ready, r_ready, s_ready, t_ready, xtr_ready, u_ready,
                      att_ready, mean_ready, var_ready, rb_ready, h_ready, ffn_ready):
                pe.sem_inc(s.sem, s.per)
            pe.wait_ge(consts, 16 * 7)

            def new_layer(layer):
                pe.wait_ge(core_loaded.sem, core_loaded.at(layer, core_loaded.per))

            def body(core, tail, ffn, fresh):
                n, place = core or (None, None)
                m, tail_place = tail or (None, None)
                q, ffn_place, layer = ffn or (None, None, None)

                def project(g, *tiles):
                    if g == 0:
                        pe.wait_ge(xs_ready.sem, xs_ready.at(n, 2))
                    for i in tiles:
                        k = 4 * g + i - 2
                        if k < 0:
                            pe.wait_ge(prod_done.sem, prod_done.before(n))
                            pe.wait_ge(sq_done.sem, sq_done.before(n))
                        else:
                            pe.wait_ge(prod_done.sem, prod_done.at(n, 2 * k + 2))
                            pe.wait_ge(sq_done.sem, sq_done.at(n, k + 1))
                        pe.matmul(pj_ps[:, i % 2, :], wqk[:, g, i, :], xs[:, WIN:], start=True, stop=True).then_inc(proj_ready.sem, 1)

                def square_sums(g):
                    if g == 0:
                        pe.wait_ge(kn_done.sem, kn_done.before(n))
                    else:
                        pe.wait_ge(kn_done.sem, kn_done.at(n, 2 * g))
                    pe.wait_ge(sq_done.sem, sq_done.at(n, 4 * g + 4))
                    for i in range(4):
                        last = pe.matmul(nr_ps[32 * i:32 * i + 32, :], heads[:], sq[:, i, :], start=True, stop=True)
                    last.then_inc(ns_ready.sem, 1)

                def sums_by_token(g):
                    pe.wait_ge(ns_copied.sem, ns_copied.at(n, g + 1))
                    for t in range(T):
                        last = pe.matmul(nr_ps[:, 8 * t:8 * t + 8], nsum[:, t * P:(t + 1) * P], pick[:], start=True, stop=True)
                    last.then_inc(ss_ready.sem, 1)

                def spread_norms(g):
                    pe.wait_ge(rn_steps.sem, rn_steps.at(n, (g + 1) * NORM_LINKS))
                    for t in range(T):
                        last = pe.transpose(nr_ps[:, t * P:(t + 1) * P],
                                            rnx[:, t].rearrange("p h d -> p (h d)"), ident[:])
                    last.then_inc(r_ready.sem, 1)

                def scores(g, n=n):
                    if g == 0:
                        pe.wait_ge(pt_done.sem, pt_done.before(n))
                    elif g == 1:
                        pe.wait_ge(s_scaled.sem, s_scaled.at(n, 1))
                    else:
                        pe.wait_ge(pt_done.sem, pt_done.at(n, g - 1))
                    pe.wait_ge(qp_loaded.sem, qp_loaded.at(n, 16 * 4 * (g + 1)))
                    pe.wait_ge(kbd_loaded.sem, kbd_loaded.at(n, 16 * 8 * (g + 1)))
                    for bank in range(2):
                        pe.matmul(st_ps[:, bank, :], identb[:], mask[:, bank, :], start=True, stop=False, skip_group_check=True)
                    for t in range(T):
                        for p in range(2):
                            for c in range(4):
                                w, at = 4 * t + c, 256 * (t % 2) + 128 * p
                                last = pe.matmul(st_ps[32 * c:32 * c + 32, t // 2, at:at + 128], qp[:, g % 2, p, WIN * w:WIN * w + WIN],
                                                 kbd[:, p, :, WIN * w:WIN * w + SPAN], start=False, stop=True, skip_group_check=True)
                    last.then_inc(s_ready.sem, 1)

                def token_transposes(r):
                    if r == 0:
                        pe.wait_ge(s_scaled.sem, s_scaled.at(n, 2))
                    else:
                        pe.wait_ge(xtok_done.sem, xtok_done.at(n, 1))
                    for i in range(8):
                        w = 8 * r + i
                        for z in range(2):
                            last = pe.matmul(st_ps[64 * z:64 * z + SPAN, i // 4, (i % 4) * P:(i % 4 + 1) * P],
                                             xs[:, WIN * w:WIN * w + SPAN], ident[:], start=True, stop=True)
                    last.then_inc(xtr_ready.sem, 1)

                def prob_transposes(g, n=n):
                    if g == 0:
                        pe.wait_ge(xtok_done.sem, xtok_done.at(n, 2))
                    elif g < 3:
                        pe.wait_ge(s_scaled.sem, s_scaled.at(n, g + 2))
                    else:
                        pe.wait_ge(pt_done.sem, pt_done.at(n, 3))
                    pe.wait_ge(p_ready.sem, p_ready.at(n, g + 1))
                    for hp in range(2):
                        for t in range(T):
                            last = pe.transpose(st_ps[:, hp, t * P:(t + 1) * P], sx[:, g % 2, t, 2 * hp:2 * hp + 2, :], ident[:])
                    last.then_inc(t_ready.sem, 1)

                def attend(*ks):
                    for k in ks:
                        if k == 0:
                            pe.wait_ge(pt_done.sem, pt_done.at(m, 4))
                            pe.wait_ge(xtok_done.sem, xtok_done.at(m, 2))
                            pe.wait_ge(hid_done.sem, hid_done.before(m))
                            pe.wait_ge(gate_done.sem, gate_done.before(m))
                        for w in (2 * k, 2 * k + 1):
                            for z in range(2):
                                if k and w % 2 == 0:
                                    pe.wait_ge(u_copied.sem, u_copied.at(m, 2 * k - 1 + z))
                                mm = pe.matmul(ta_ps[:, z, 256 * (w % 2):256 * (w % 2) + 256], xtok[64 * z:64 * z + 64, w, :],
                                               pt[64 * z:64 * z + 64, w, :, :], start=True, stop=True)
                                if w % 2:
                                    mm.then_inc(u_ready.sem, 1)

                def combine(r, half):
                    if half == 0:
                        pe.wait_ge(u_copied.sem, u_copied.at(m, 4 * r + 4))
                        if r == 0:
                            pe.wait_ge(x2_done.sem, x2_done.before(m))
                    for h in range(8 * half, 8 * half + 8):
                        last = pe.matmul(to_ps[:, P * r:P * r + P], mvo[:, h, :], u[:, h, r % 2], start=(h == 0), stop=(h == LH - 1),
                                         skip_group_check=True)
                    if half:
                        last.then_inc(att_ready.sem, 1)

                def value_output():
                    pe.wait_ge(raw_loaded.sem, raw_loaded.at(fresh, raw_loaded.per))
                    pe.wait_ge(u_copied.sem, u_copied.before(n))
                    for j in range(2):
                        if j:
                            pe.wait_ge(mvo_copied.sem, mvo_copied.at(fresh, 2))
                        for i in range(4):
                            for z in range(2):
                                rows = slice(64 * z, 64 * z + 64)
                                mm = pe.matmul(ta_ps[:, z, i * P:(i + 1) * P], wv_raw[rows, 4 * j + i, :], wo_raw[rows, 4 * j + i, :],
                                               start=True, stop=True)
                                if i == 3:
                                    mm.then_inc(mvo_ready.sem, 1)
                    pe.wait_ge(mvo_copied.sem, mvo_copied.at(fresh, 4))

                def mean():
                    pe.wait_ge(xf_done.sem, xf_done.at(q, 2))
                    pe.matmul(ta_ps[:, 0, :], ones[:], xf[:], start=True, stop=True).then_inc(mean_ready.sem, 1)

                def variance():
                    pe.wait_ge(csq_done.sem, csq_done.at(q, 1))
                    for t in range(T):
                        last = pe.matmul(ta_ps[:, 1, t:t + 1], csq[:, t * P:(t + 1) * P], ones[:, 0:1], start=True, stop=True)
                    last.then_inc(var_ready.sem, 1)

                def spread_rstd():
                    pe.wait_ge(var_steps.sem, var_steps.at(q, 1 + RSQRT_LINKS))
                    for t in range(T):
                        last = pe.transpose(ta_ps[:, 0, t * P:(t + 1) * P], rstd[:, 1, t:t + 1].to_broadcast([P, P]), ident[:])
                    last.then_inc(rb_ready.sem, 1)

                def hidden(c):
                    k, w = CHUNKS[c]
                    if c == 0:
                        pe.wait_ge(tail_loaded.sem, tail_loaded.at(layer, tail_loaded.per))
                        pe.wait_ge(xn_done.sem, xn_done.at(q, 1))
                    for side in (1, 0):
                        if c:
                            used = gate_done if side else hid_done
                            pe.wait_ge(used.sem, used.at(q, c))
                        pe.matmul(ta_ps[0:w, side, :], w1[:, side * HID + k:side * HID + k + w], csq[:],
                                  start=True, stop=True).then_inc(h_ready.sem, 1)

                def down(c):
                    k, w = CHUNKS[c]
                    pe.wait_ge(hid_done.sem, hid_done.at(q, c + 1))
                    if c == 0:
                        pe.wait_ge(x1_done.sem, x1_done.at(q, 1))
                    last = pe.matmul(to_ps[:], w2[0:w, c, :], hid[0:w, c, :], start=(c == 0), stop=(c == NC_ - 1), skip_group_check=True)
                    if c == NC_ - 1:
                        last.then_inc(ffn_ready.sem, 1)

                C_, T_, F_ = core is not None, tail is not None, ffn is not None
                if C_: project(0, 0, 1)
                if T_: prob_transposes(1, m)
                if F_: mean()
                if C_: project(0, 2, 3)
                if F_: variance()
                if T_: scores(3, m)
                if C_: square_sums(0); sums_by_token(0)
                if F_: spread_rstd()
                if T_: prob_transposes(2, m)
                if C_: project(1, 0)
                if F_: hidden(0)
                if C_: spread_norms(0); project(1, 1)
                if F_: hidden(1)
                if C_: project(1, 2)
                if F_: down(0); hidden(2)
                if C_: project(1, 3)
                if F_: down(1); down(2)
                if C_: square_sums(1)
                if T_: prob_transposes(3, m)
                if C_: project(2, 0); sums_by_token(1)
                if T_: attend(0)
                if C_: project(2, 1)
                if T_: attend(1)
                if C_: scores(0); spread_norms(1)
                if T_: attend(2)
                if C_: project(2, 2)
                if T_: attend(3); combine(0, 0)
                if C_: project(2, 3)
                if T_: combine(0, 1)
                if C_: square_sums(2)
                if T_: attend(4)
                if C_: sums_by_token(2)
                if T_: attend(5); combine(1, 0)
                if C_: scores(1); spread_norms(2); project(3, 0)
                if T_: combine(1, 1)
                if C_: project(3, 1)
                if T_: attend(6)
                if C_: project(3, 2)
                if T_: attend(7)
                if C_: project(3, 3); token_transposes(0); square_sums(3); token_transposes(1); sums_by_token(3)
                if T_: combine(2, 0)
                if C_: prob_transposes(0)
                if T_: combine(2, 1)
                if C_: scores(2); spread_norms(3)
                if T_: combine(3, 0); combine(3, 1)
                if fresh is not None: value_output()

            layers(pe, body, new_layer)

        @block.vector
        def _(dve):
            for s in (prod_done, rn_steps, kn_done, s_scaled, s_max, p_sum,
                      x1_done, xc_done, var_steps, xg_done, hid_done, x2_done, rot_ready):
                dve.sem_inc(s.sem, s.per)
            dve.memset(kbd[:], 0.0).then_inc(init, 1)
            dve.memset(xs[:], 0.0).then_inc(init, 1)
            dve.wait_ge(init, 2)
            dve.wait_ge(consts, 16 * 7)

            def new_layer(layer):
                dve.wait_ge(core_loaded.sem, core_loaded.at(layer, core_loaded.per))
                for i in range(8):
                    table, gain = 2 * (i // 4) + i % 2, 2 * (i // 4) + (0, 1, 1, 0)[i % 4]
                    dve.tensor_scalar(rot[:, i, :], tables[:, table, :], gains[:, gain:gain + 1], None, ALU.mult).then_inc(rot_ready.sem, 1)
                dve.wait_ge(rot_ready.sem, rot_ready.at(layer, 8))

            def body(core, tail, ffn, fresh):
                n, place = core or (None, None)
                m, tail_place = tail or (None, None)
                q, ffn_place, layer = ffn or (None, None, None)

                def products(g, *tiles):
                    for i in tiles:
                        dve.wait_ge(sq_done.sem, sq_done.at(n, 4 * g + i + 1))
                        for table, k in unit_tables(i):
                            if g == 0:
                                dve.wait_ge(rot_done.sem, rot_done.before(n))
                            elif i % 2 == 0:
                                dve.wait_ge(rot_done.sem, rot_done.at(n, 4 * (g - 1) + i + 2))
                            dve.tensor_tensor(prod[:, k, :], pj_ps[:, i % 2, :], rot[:, table, :], ALU.mult).then_inc(prod_done.sem, 1)

                def norms(g):
                    dve.wait_ge(ss_ready.sem, ss_ready.at(n, g + 1))
                    if g >= 2:
                        dve.wait_ge(r_ready.sem, r_ready.at(n, g - 1))
                    done = g * NORM_LINKS
                    dve.tensor_scalar(ss[:], nr_ps[:, 0:8 * T].rearrange("p (t k) -> p t k", k=8), TINY, None, ALU.max).then_inc(rn_steps.sem, 1)
                    dve.wait_ge(rn_steps.sem, rn_steps.at(n, done + 1))
                    rsqrt(dve, rn[:, g % 2], ss[:], rt[:], rn_steps, n, done + 1)
                    dve.tensor_copy(rnx[:], rn[:, g % 2, :, 4:8].unsqueeze(3).to_broadcast([P, T, 4, HALF])).then_inc(rn_steps.sem, 1)

                def scale_keys(g):
                    dve.wait_ge(r_ready.sem, r_ready.at(n, g + 1))
                    if g == 0:
                        dve.wait_ge(kbd_loaded.sem, kbd_loaded.before(n))
                    else:
                        dve.wait_ge(kbd_loaded.sem, kbd_loaded.at(n, 16 * 8 * g))
                    dve.wait_ge(rot_done.sem, rot_done.at(n, 4 * g + 4))
                    for half in range(2):
                        dve.tensor_tensor(kn[:, half, :], kr[:, half, :], nr_ps[:], ALU.mult).then_inc(kn_done.sem, 1)

                def scale_scores(g, n=n):
                    dve.wait_ge(s_ready.sem, s_ready.at(n, g + 1))
                    if g >= 2:
                        dve.wait_ge(t_ready.sem, t_ready.at(n, g - 1))
                    else:
                        dve.wait_ge(t_ready.sem, t_ready.before(n))
                    dve.tensor_tensor(sx[:, g % 2], st_ps[:].rearrange("p b (t h k) -> p (b t) h k", h=4, k=SPAN),
                                      rn[:, g % 2, :, 0:4].unsqueeze(3).to_broadcast([P, T, 4, SPAN]), ALU.mult).then_inc(s_scaled.sem, 1)
                    dve.wait_ge(s_scaled.sem, s_scaled.at(n, g + 1))
                    if g >= 2:
                        dve.wait_ge(s_less.sem, s_less.at(n, g - 1))
                    else:
                        dve.wait_ge(s_less.sem, s_less.before(n))
                    dve.tensor_reduce(smax[:, g % 2], sx[:, g % 2], AX.X, ALU.max).then_inc(s_max.sem, 1)

                def prob_sums(g, n=n):
                    dve.wait_ge(p_exp.sem, p_exp.at(n, g + 1))
                    if g >= 2:
                        dve.wait_ge(p_ready.sem, p_ready.at(n, g - 1))
                    else:
                        dve.wait_ge(p_ready.sem, p_ready.before(n))
                    dve.tensor_reduce(rsum[:, g % 2], sx[:, g % 2], AX.X, ALU.add).then_inc(p_sum.sem, 1)
                    dve.wait_ge(p_sum.sem, p_sum.at(n, 2 * g + 1))
                    dve.reciprocal(rsum[:, g % 2], rsum[:, g % 2]).then_inc(p_sum.sem, 1)

                batch = lambda place: X[:, bass.ds(place, 1), 1:1 + N].rearrange("p o n -> p (o n)")

                def attention_sum():
                    dve.wait_ge(att_ready.sem, att_ready.at(m, 4))
                    xb = batch(tail_place)
                    dve.tensor_tensor(xb, to_ps[:], xb, ALU.add).then_inc(x1_done.sem, 1)

                def centre():
                    dve.wait_ge(mean_ready.sem, mean_ready.at(q, 1))
                    dve.tensor_tensor(xc[:], xf[:], ta_ps[:, 0, :], ALU.subtract).then_inc(xc_done.sem, 1)

                def deviation():
                    dve.wait_ge(var_ready.sem, var_ready.at(q, 1))
                    dve.tensor_scalar(rstd[:, 0, :], ta_ps[:, 1, 0:T], EPS, None, ALU.add).then_inc(var_steps.sem, 1)
                    dve.wait_ge(var_steps.sem, var_steps.at(q, 1))
                    rsqrt(dve, rstd[:, 1, :], rstd[:, 0, :], rstd[:, 2, :], var_steps, q, 1)

                def normalise():
                    dve.wait_ge(rb_ready.sem, rb_ready.at(q, 1))
                    dve.wait_ge(tail_loaded.sem, tail_loaded.at(layer, tail_loaded.per))
                    dve.scalar_tensor_tensor(csq[:], xc[:], vec[:, V_G:V_G + 1], ta_ps[:, 0, :], ALU.mult, ALU.mult).then_inc(xg_done.sem, 1)

                def gated(c):
                    k, w = CHUNKS[c]
                    dve.wait_ge(h_ready.sem, h_ready.at(q, 2 * c + 2))
                    dve.wait_ge(gate_done.sem, gate_done.at(q, c + 1))
                    if c == 0:
                        dve.wait_ge(ffn_ready.sem, ffn_ready.before(q))
                    dve.scalar_tensor_tensor(hid[0:w, c, :], ta_ps[0:w, 0, :], vec[0:w, V_B1 + c:V_B1 + c + 1], gate[0:w, c % 2, :],
                                             ALU.add, ALU.mult).then_inc(hid_done.sem, 1)

                def ffn_sum():
                    dve.wait_ge(ffn_ready.sem, ffn_ready.at(q, 1))
                    dve.wait_ge(xf_done.sem, xf_done.at(q, 2))
                    xb = batch(ffn_place)
                    dve.scalar_tensor_tensor(xb, to_ps[:], vec[:, V_B2:V_B2 + 1], xb, ALU.add, ALU.add).then_inc(x2_done.sem, 1)

                C_, T_, F_ = core is not None, tail is not None, ffn is not None
                if C_: products(0, 0, 1)
                if F_: centre()
                if T_: prob_sums(2, m)
                if C_: products(0, 2, 3)
                if F_: deviation()
                if T_: scale_scores(3, m)
                if F_: normalise()
                if C_: norms(0); scale_keys(0)
                if F_: gated(0)
                if C_: products(1, 0, 1)
                if F_: gated(1)
                if T_: prob_sums(3, m)
                if C_: products(1, 2)
                if F_: gated(2)
                if C_: products(1, 3)
                if F_: ffn_sum()
                if C_: norms(1); products(2, 0, 1); scale_keys(1); scale_scores(0); products(2, 2); prob_sums(0); products(2, 3)
                if C_: norms(2); scale_keys(2); scale_scores(1); products(3, 0, 1, 2); prob_sums(1); products(3, 3)
                if C_: norms(3); scale_keys(3); scale_scores(2)
                if T_: attention_sum()

            layers(dve, body, new_layer)

        @block.scalar
        def _(act):
            for s in (xs_ready, xf_done, sq_done, ns_copied, p_exp, pt_done, xtok_done, u_copied, csq_done, xn_done, mvo_copied, gate_done):
                act.sem_inc(s.sem, s.per)
            act.wait_ge(init, 2)
            shifts = lambda dst, b: ((dst[0:64], X[0:64, bass.ds(b, 1), 1:1 + N]), (dst[64:128], X[64:128, bass.ds(b, 1), 0:N]))

            def body(core, tail, ffn, fresh):
                n, place = core or (None, None)
                m, tail_place = tail or (None, None)
                q, ffn_place, layer = ffn or (None, None, None)

                def tokens():
                    act.wait_ge(proj_ready.sem, proj_ready.before(n))
                    act.wait_ge(xtr_ready.sem, xtr_ready.before(n))
                    if ffn is not None:
                        act.wait_ge(x2_done.sem, x2_done.before(q))
                    for dst, src in shifts(xs[:, WIN:], place):
                        act.copy(dst, src.rearrange("p o n -> p (o n)")).then_inc(xs_ready.sem, 1)

                def ffn_tokens():
                    act.wait_ge(x1_done.sem, x1_done.at(q, 1))
                    act.wait_ge(xc_done.sem, xc_done.before(q))
                    for dst, src in shifts(xf[:], ffn_place):
                        act.copy(dst, src.rearrange("p o n -> p (o n)")).then_inc(xf_done.sem, 1)

                def squares(g, *tiles):
                    for i in tiles:
                        act.wait_ge(proj_ready.sem, proj_ready.at(n, 4 * g + i + 1))
                        if i == 0:
                            if g == 0:
                                act.wait_ge(ns_ready.sem, ns_ready.before(n))
                            else:
                                act.wait_ge(ns_ready.sem, ns_ready.at(n, g))
                        act.activation(sq[:, i, :], pj_ps[:, i % 2, :], ACT.Square).then_inc(sq_done.sem, 1)

                def copy_sums(g):
                    act.wait_ge(ns_ready.sem, ns_ready.at(n, g + 1))
                    if g == 0:
                        act.wait_ge(ss_ready.sem, ss_ready.before(n))
                    else:
                        act.wait_ge(ss_ready.sem, ss_ready.at(n, g))
                    act.copy(nsum[:], nr_ps[:]).then_inc(ns_copied.sem, 1)

                def exponentials(g, n=n):
                    act.wait_ge(s_less.sem, s_less.at(n, g + 1))
                    act.activation(sx[:, g % 2], sx[:, g % 2], ACT.Exp).then_inc(p_exp.sem, 1)

                def copy_probs(g, n=n):
                    act.wait_ge(t_ready.sem, t_ready.at(n, g + 1))
                    if g == 0:
                        act.wait_ge(u_ready.sem, u_ready.before(n))
                    act.copy(pt[:, :, 2 * g:2 * g + 2, :].rearrange("p w h q -> p h w q"),
                             st_ps[:].rearrange("p h (w q) -> p h w q", q=WIN)).then_inc(pt_done.sem, 1)

                def copy_tokens(r):
                    act.wait_ge(xtr_ready.sem, xtr_ready.at(n, r + 1))
                    if r == 0:
                        act.wait_ge(u_ready.sem, u_ready.before(n))
                    act.copy(xtok[:, 8 * r:8 * r + 8, :].rearrange("p w c -> p (w c)"), st_ps[:].rearrange("p b x -> p (b x)")).then_inc(xtok_done.sem, 1)

                def take_u(*ks):
                    for k in ks:
                        if k % 2 == 0:
                            if k < 4:
                                act.wait_ge(att_ready.sem, att_ready.before(m))
                            else:
                                act.wait_ge(att_ready.sem, att_ready.at(m, k // 2 - 1))
                        for z in range(2):
                            act.wait_ge(u_ready.sem, u_ready.at(m, 2 * k + z + 1))
                            act.copy(u[:].rearrange("p (h z) r w q -> p z r w h q", z=2)[:, z, k // 2 % 2, 2 * (k % 2):2 * (k % 2) + 2],
                                     ta_ps[:, z, :].rearrange("p (w h q) -> p w h q", w=2, q=WIN)).then_inc(u_copied.sem, 1)

                def copy_mvo():
                    for j in range(2):
                        for z in range(2):
                            act.wait_ge(mvo_ready.sem, mvo_ready.at(fresh, 2 * j + z + 1))
                            act.copy(mvo[:].rearrange("p (j h z) c -> p j z h c", j=2, z=2)[:, j, z],
                                     ta_ps[:, z, :].rearrange("p (h c) -> p h c", c=P)).then_inc(mvo_copied.sem, 1)

                def centred_squares():
                    act.wait_ge(xc_done.sem, xc_done.at(q, 1))
                    act.wait_ge(h_ready.sem, h_ready.before(q))
                    act.activation(csq[:], xc[:], ACT.Square).then_inc(csq_done.sem, 1)

                def add_bias():
                    act.wait_ge(xg_done.sem, xg_done.at(q, 1))
                    act.activation(csq[:], csq[:], ACT.Identity, bias=vec[:, V_BLN:V_BLN + 1]).then_inc(xn_done.sem, 1)

                def gates(c):
                    k, w = CHUNKS[c]
                    act.wait_ge(h_ready.sem, h_ready.at(q, 2 * c + 1))
                    if c == 0:
                        act.wait_ge(hid_done.sem, hid_done.before(q))
                    if c >= 2:
                        act.wait_ge(hid_done.sem, hid_done.at(q, c - 1))
                    act.activation(gate[0:w, c % 2, :], ta_ps[0:w, 1, :], ACT.Gelu, bias=vec[0:w, V_B1 + NC_ + c:V_B1 + NC_ + c + 1]).then_inc(gate_done.sem, 1)

                C_, T_, F_ = core is not None, tail is not None, ffn is not None
                if C_: tokens(); squares(0, 0)
                if F_: ffn_tokens()
                if C_: squares(0, 1)
                if T_: copy_probs(1, m); exponentials(2, m)
                if F_: centred_squares()
                if C_: squares(0, 2, 3); copy_sums(0)
                if F_: add_bias()
                if C_: squares(1, 0)
                if T_: exponentials(3, m)
                if F_: gates(0)
                if T_: copy_probs(2, m)
                if C_: squares(1, 1)
                if F_: gates(1)
                if C_: squares(1, 2)
                if F_: gates(2)
                if C_: squares(1, 3); copy_sums(1)
                if T_: copy_probs(3, m)
                if C_: squares(2, 0)
                if T_: take_u(0)
                if C_: squares(2, 1)
                if T_: take_u(1, 2)
                if C_: squares(2, 2)
                if T_: take_u(3)
                if C_: exponentials(0); squares(2, 3); copy_sums(2)
                if T_: take_u(4, 5)
                if C_: squares(3, 0, 1)
                if T_: take_u(6)
                if C_: squares(3, 2); exponentials(1)
                if T_: take_u(7)
                if C_: squares(3, 3); copy_tokens(0); copy_sums(3); copy_tokens(1); copy_probs(0)
                if fresh is not None: copy_mvo()

            layers(act, body)

        @block.gpsimd
        def _(pool):
            for s in (rot_done, s_less, p_ready):
                pool.sem_inc(s.sem, s.per)

            def body(core, tail, ffn, fresh):
                n, place = core or (None, None)
                m, tail_place = tail or (None, None)
                q, ffn_place, layer = ffn or (None, None, None)

                def rotate(g, *tiles):
                    for i in tiles:
                        pool.wait_ge(prod_done.sem, prod_done.at(n, 8 * g + 4 * (i // 2) + 4))
                        if i < 2:
                            if g >= 2:
                                pool.wait_ge(s_ready.sem, s_ready.at(n, g - 1))
                            elif tail is not None:
                                pool.wait_ge(s_ready.sem, s_ready.at(m, g + 3))
                            dst = qr[:, i, :]
                            if g == 0:
                                pool.wait_ge(qp_loaded.sem, qp_loaded.before(n))
                            else:
                                pool.wait_ge(qp_loaded.sem, qp_loaded.at(n, 16 * 4 * g))
                        else:
                            if g == 0:
                                pool.wait_ge(kn_done.sem, kn_done.before(n))
                            else:
                                pool.wait_ge(kn_done.sem, kn_done.at(n, 2 * g))
                            dst = kr[:, i % 2, :]
                        k = 2 * i
                        pool.tensor_tensor(dst, prod[:, k, :], prod[:, k + 1, :], ALU.add if i % 2 else ALU.subtract).then_inc(rot_done.sem, 1)

                def less_max(g, n=n):
                    pool.wait_ge(s_max.sem, s_max.at(n, g + 1))
                    pool.tensor_tensor(sx[:, g % 2], sx[:, g % 2], smax[:, g % 2].unsqueeze(3).to_broadcast([P, T, 4, SPAN]),
                                       ALU.subtract).then_inc(s_less.sem, 1)

                def normal_probs(g, n=n):
                    pool.wait_ge(p_sum.sem, p_sum.at(n, 2 * g + 2))
                    pool.tensor_tensor(sx[:, g % 2], sx[:, g % 2], rsum[:, g % 2].unsqueeze(3).to_broadcast([P, T, 4, SPAN]),
                                       ALU.mult).then_inc(p_ready.sem, 1)

                C_, T_, F_ = core is not None, tail is not None, ffn is not None
                if C_: rotate(0, 0, 1)
                if T_: normal_probs(2, m)
                if C_: rotate(0, 2, 3)
                if T_: less_max(3, m); normal_probs(3, m)
                if C_: rotate(1, 0, 1)
                if C_: rotate(1, 2, 3); less_max(0); rotate(2, 0, 1); normal_probs(0); rotate(2, 2, 3)
                if C_: less_max(1); rotate(3, 0, 1); normal_probs(1); rotate(3, 2, 3); less_max(2)

            layers(pool, body)


def final_part(nc, sum_dram, ident_dram, X, out_dram):
    with ExitStack() as ctx:
        sb = lambda n, s: ctx.enter_context(nc.sbuf_tensor(n, s, F32))
        sem = lambda n: ctx.enter_context(nc.semaphore(n))
        part = sb("fi_part", [P, B * T, C])
        res = sb("fi_res", [P, B * T, C])
        ident = sb("fi_ident", [P, P])
        xt = sb("fi_xt", [P, 2, N])
        tr = ctx.enter_context(nc.psum_tensor("fi_tr", [P, 2, 512], F32))
        loaded, copied, transposed, added, stored = (sem("fi_" + n) for n in ("loaded", "copied", "transposed", "added", "stored"))
        block = ctx.enter_context(nc.Block())
        rows = lambda a: a.rearrange("b (t p) c -> p (b t) c", p=P)

        @block.sync
        def _(sp):
            sp.dma_start(part[:], rows(sum_dram)).then_inc(loaded, 16)
            sp.dma_start(ident[:], ident_dram).then_inc(loaded, 16)
            for b in range(B):
                sp.wait_ge(added, b + 1)
                sp.dma_start(rows(out_dram)[:, b * T:(b + 1) * T], res[:, b * T:(b + 1) * T]).then_inc(stored, 16)
            sp.wait_ge(stored, 16 * B)

        @block.scalar
        def _(act):
            for b in range(B):
                if b >= 2:
                    act.wait_ge(transposed, b - 1)
                act.copy(xt[:, b % 2, :], X[:, b, 1:1 + N]).then_inc(copied, 1)

        @block.tensor
        def _(pe):
            pe.wait_ge(loaded, 32)
            for b in range(B):
                pe.wait_ge(copied, b + 1)
                if b >= 2:
                    pe.wait_ge(added, b - 1)
                for t in range(T):
                    last = pe.transpose(tr[:, b % 2, t * P:(t + 1) * P], xt[:, b % 2, t * P:(t + 1) * P], ident[:])
                last.then_inc(transposed, 1)

        @block.vector
        def _(dve):
            dve.wait_ge(loaded, 32)
            for b in range(B):
                dve.wait_ge(transposed, b + 1)
                dve.tensor_tensor(res[:, b * T:(b + 1) * T].rearrange("p t c -> p (t c)"), tr[:, b % 2, :],
                                  part[:, b * T:(b + 1) * T].rearrange("p t c -> p (t c)"), ALU.add).then_inc(added, 1)


def program(nc, a):
    with nc.sbuf_tensor("x_all", [P, B, 1 + N], F32) as X:
        layernorm_part(nc, a["x"], a["ident"], X)
        global_attention_part(nc, a["x"], a["ga_w"], a["ga_rope"], a["ident"], X, a["sum"], a["ga_parts"], a["ga_maxes"])
        layers_part(nc, X, a)
        final_part(nc, a["sum"], a["ident"], X, a["out"])


def rope_tables():
    f = np.float32
    inv = np.power(f(10000.0), (f(-2.0) * np.arange(GD // 2, dtype=f) / f(GD)).astype(f)).astype(f)
    ang = np.arange(N, dtype=f)[:, None] * inv[None]
    cos, sin = (np.tile(np.repeat(g(ang), 2, axis=-1).T, (GH, 1)) for g in (np.cos, np.sin))
    sign = np.where(np.arange(P) % 2 == 0, -1, 1).astype(f)
    return np.ascontiguousarray(np.stack([cos, sin * sign[:, None]], axis=1).astype(f))


def rotation_tables():
    f = np.float32
    half = np.arange(0, LD, 2, dtype=f)
    t = np.arange(N, dtype=f)
    ang = t[:, None] * (f(1.0) / np.power(f(10000.0), half / f(LD))).astype(f)[None]
    scale = np.power(((half + f(0.4 * LD)) / f(1.4 * LD))[None], ((t - N // 2) / f(WIN // 2))[:, None]).astype(f)
    four = [f(8.0) * np.cos(ang) * scale, f(8.0) * np.sin(ang) * scale, np.cos(ang) / scale, np.sin(ang) / scale]
    return np.ascontiguousarray(np.stack([np.tile(a.T, (4, 1)) for a in four], axis=1).astype(f))


def score_mask():
    q = np.arange(P) % WIN
    k = np.arange(SPAN)
    seen = (q[:, None] <= k) & (k <= q[:, None] + WIN)
    first = (np.arange(P)[:, None] >= WIN) | (k[None] >= WIN)
    m = np.zeros((P, T, 4, SPAN), np.float32)
    m[:] = np.where(seen, 0, MASKED)[:, None, None]
    m[:, 0] = np.where(seen & first, 0, MASKED)[:, None]
    return m.reshape(P, 2, 512)


def constants():
    p = np.arange(P)
    pick = np.zeros((P, 8), np.float32)
    for r in p[p % 32 < 4]:
        pick[r, 4 * (r // 64) + r % 32] = 1
    return {
        "ident": np.eye(P, dtype=np.float32),
        "ones": np.full((P, P), 1.0 / C, np.float32),
        "heads": (p[:, None] // 32 == np.arange(32)[None] % 4).astype(np.float32),
        "pick": pick,
        "mask": score_mask(),
        "identb": np.eye(P, dtype=np.float32),
        "ga_rope": rope_tables(),
        "rot": rotation_tables(),
    }


def laid_out(i):
    a = {k: np.asarray(v) for k, v in i.items()}
    swap = np.arange(P) ^ 1
    wq, wk, wv = a["L0_attn_Wq"].T, a["L0_attn_Wk"].T, a["L0_attn_Wv"].T
    qkv = a["L0_ffn_Wqkv"].reshape(LAYERS, C, 3, LH, LD)
    qk = qkv[:, :, :2].reshape(LAYERS, C, 2, UNITS, 4, 2, HALF).transpose(0, 1, 3, 2, 5, 4, 6)
    pair = lambda m: m.reshape(LAYERS, LH // 2, P, C).transpose(0, 2, 1, 3)
    w2 = np.zeros((LAYERS, NC_, P, C), np.float32)
    vec = np.zeros((LAYERS, P, NVEC), np.float32)
    for c, (k, w) in enumerate(CHUNKS):
        w2[:, c, :w] = a["L0_ffn_W2"][:, k:k + w]
        for side in range(2):
            vec[:, :w, V_B1 + side * NC_ + c] = a["L0_ffn_b1"][:, side * HID + k:side * HID + k + w]
    gains = np.stack([np.tile(a["L0_ffn_" + name].reshape(LAYERS, 2, HALF)[:, half], (1, 4))
                      for name in ("q_scale", "k_scale") for half in range(2)], axis=2)
    vec[:, :, V_G], vec[:, :, V_BLN], vec[:, :, V_B2] = a["L0_ffn_ln_g"], a["L0_ffn_ln_b"], a["L0_ffn_b2"]
    return {
        "x": a["L0_attn_x"],
        "ga_w": np.stack([wq, wq[:, swap], wk, wk[:, swap], wv], axis=1),
        "wqk": qk.reshape(LAYERS, C, UNITS, 4, P),
        "wv": pair(qkv[:, :, 2].reshape(LAYERS, C, INNER).transpose(0, 2, 1)),
        "wo": pair(a["L0_ffn_Wo"]),
        "w1": a["L0_ffn_W1"],
        "w2": w2.transpose(0, 2, 1, 3),
        "vec": vec,
        "gains": gains,
    }


def kernel(**inputs):
    import ml_dtypes
    import concourse.bacc as bacc
    from concourse.bass_utils import run_bass_kernel_spmd

    nc = bacc.Bacc("TRN2", target_bir_lowering=False, num_devices=1)
    arrays = {**laid_out(inputs), **constants()}
    for n in ("mask", "identb"):
        arrays[n] = arrays[n].astype(ml_dtypes.bfloat16)
    arrays = {n: np.ascontiguousarray(v) for n, v in arrays.items()}
    aps = {n: nc.dram_tensor("in_" + n, v.shape, mybir.dt.from_np(v.dtype), kind="ExternalInput").ap() for n, v in arrays.items()}
    for n, shape, dt, kind in (("sum", (B, N, C), F32, "Internal"), ("ga_parts", (B, P, 2, 3, N), BF16, "Internal"),
                               ("ga_maxes", (B, 3, GH * T, P), BF16, "Internal"), ("out", (B, N, C), F32, "ExternalOutput")):
        aps[n] = nc.dram_tensor(n + "_dram", shape, dt, kind=kind).ap()
    program(nc, aps)
    r = run_bass_kernel_spmd(nc, [{"in_" + n: v for n, v in arrays.items()}], core_ids=[0])
    return r.results[0]["out_dram"]
```
